# Optimizing a Trainium2 kernel written in Bass

```python
import numpy as np
import jax
import jax.numpy as jnp

def _softmax(x, axis=-1):
    return jax.nn.softmax(x, axis=axis)

def _gelu(x):
    return jax.nn.gelu(x, approximate=True)

def _silu(x):
    return jax.nn.silu(x)

def _sigmoid(x):
    return jax.nn.sigmoid(x)

def _layernorm(x, axis=-1, eps=1e-05):
    m = jnp.mean(x, axis=axis, keepdims=True)
    v = jnp.var(x, axis=axis, keepdims=True)
    return (x - m) / jnp.sqrt(v + eps)

def _scatter_add(tgt, idx, src, axis=0):
    return tgt.at[idx].add(src)

def _segment_sum(src, seg, n):
    return jax.ops.segment_sum(src, seg, n)
kernel_name = 'mk_prb_d2_jaxref_r8_aed37d'

def setup_inputs(seed: int=0):
    np.random.seed(seed)
    _w = jnp.asarray

    def _L0_attn_setup():
        import jax, jax.numpy as jnp
        import numpy as np
        D_MODEL = 128
        N_HEADS = 16
        HEAD_DIM = D_MODEL // N_HEADS
        KV_LATENT = 32
        LN_EPS = 1e-05

        def apply_rope(x):
            b, h, t, d = x.shape
            half = d // 2
            pos = jnp.arange(t, dtype=x.dtype)[:, None]
            inv_freq = 1.0 / 10000.0 ** (jnp.arange(half, dtype=x.dtype) / half)
            angles = pos * inv_freq[None, :]
            sin = jnp.sin(angles)[None, None]
            cos = jnp.cos(angles)[None, None]
            x1, x2 = (x[..., :half], x[..., half:])
            return jnp.concatenate([x1 * cos - x2 * sin, x1 * sin + x2 * cos], axis=-1)
        key = jax.random.key(seed)
        ks = jax.random.split(key, 6)
        d, L = (D_MODEL, KV_LATENT)
        s = 1.0 / np.sqrt(d)
        sl = 1.0 / np.sqrt(L)
        return {'x': jax.random.normal(ks[0], (2, 256, d), dtype=jnp.float32), 'W_q': jax.random.uniform(ks[1], (d, d), jnp.float32, -s, s), 'W_dkv': jax.random.uniform(ks[2], (d, L), jnp.float32, -s, s), 'W_uk': jax.random.uniform(ks[3], (L, d), jnp.float32, -sl, sl), 'W_uv': jax.random.uniform(ks[4], (L, d), jnp.float32, -sl, sl), 'W_o': jax.random.uniform(ks[5], (d, d), jnp.float32, -s, s), 'ln_gamma': jnp.ones((L,), jnp.float32), 'ln_beta': jnp.zeros((L,), jnp.float32)}
    _L0_attn_in = _L0_attn_setup()

    def _L0_ffn_setup():
        import jax, jax.numpy as jnp
        import numpy as np
        from jax import lax
        B, S, H = (2, 128, 128)
        I = 64
        E = 32
        TOP_K = 4
        N_GROUP = 4
        TOPK_GROUP = 2
        SCALE = 2.5
        N_SHARED = 2
        SH_I = I * N_SHARED

        def _route(tokens, router_weight, router_bias):
            logits = tokens.astype(jnp.float32) @ router_weight.astype(jnp.float32).T
            scores = jax.nn.sigmoid(logits)
            sfc = scores + router_bias[None, :]
            T = tokens.shape[0]
            grp = sfc.reshape(T, N_GROUP, E // N_GROUP)
            group_scores = lax.top_k(grp, 2)[0].sum(-1)
            _, gidx = lax.top_k(group_scores, TOPK_GROUP)
            gmask = jax.nn.one_hot(gidx, N_GROUP, dtype=sfc.dtype).sum(1)
            smask = jnp.broadcast_to(gmask[:, :, None], (T, N_GROUP, E // N_GROUP)).reshape(T, E)
            tmp = jnp.where(smask > 0, sfc, 0.0)
            _, topk_idx = lax.top_k(tmp, TOP_K)
            topk_w = jnp.take_along_axis(scores, topk_idx, axis=1)
            topk_w = topk_w / (topk_w.sum(-1, keepdims=True) + 1e-20)
            topk_w = topk_w * SCALE
            return (topk_idx, topk_w)
        key = jax.random.key(seed)
        ks = jax.random.split(key, 10)
        std = 0.02
        return {'hidden_states': jax.random.normal(ks[0], (B, S, H), jnp.float32), 'router_weight': jax.random.normal(ks[1], (E, H), jnp.float32) * std, 'router_bias': jnp.zeros((E,), jnp.float32), 'gate_w': jax.random.normal(ks[2], (E, I, H), jnp.float32) * std, 'up_w': jax.random.normal(ks[3], (E, I, H), jnp.float32) * std, 'down_w': jax.random.normal(ks[4], (E, H, I), jnp.float32) * std, 'shared_gate_w': jax.random.normal(ks[5], (SH_I, H), jnp.float32) * std, 'shared_up_w': jax.random.normal(ks[6], (SH_I, H), jnp.float32) * std, 'shared_down_w': jax.random.normal(ks[7], (H, SH_I), jnp.float32) * std}
    _L0_ffn_in = _L0_ffn_setup()

    def _L1_attn_setup():
        import jax, jax.numpy as jnp
        import numpy as np
        HID = 128
        HK, HV = (4, 8)
        DK, DV = (128, 128)
        KEY_DIM = HK * DK
        VAL_DIM = HV * DV
        CONV_DIM = 2 * KEY_DIM + VAL_DIM
        KCONV = 4
        NEXP, TOPK, INTER = (8, 2, 64)
        EPS = 1e-06

        def zrms(x, w):
            v = jnp.mean(x * x, axis=-1, keepdims=True)
            return x * jax.lax.rsqrt(v + EPS) * (1.0 + w)

        def causal_dwconv(x, w):
            xp = jnp.pad(x, ((0, 0), (KCONV - 1, 0), (0, 0)))
            kern = w.T[:, None, :]
            return jax.lax.conv_general_dilated(xp, kern, (1,), 'VALID', dimension_numbers=('NHC', 'HIO', 'NHC'), feature_group_count=CONV_DIM)

        def gated_delta_rule(q, k, v, g, beta):
            B = q.shape[0]
            S0 = jnp.zeros((B, HV, DK, DV), q.dtype)

            def step(S, inp):
                qt, kt, vt, gt, bt = inp
                S = S * jnp.exp(gt)[..., None, None]
                kv = jnp.einsum('bhk,bhkv->bhv', kt, S)
                delta = (vt - kv) * bt[..., None]
                S = S + jnp.einsum('bhk,bhv->bhkv', kt, delta)
                o = jnp.einsum('bhk,bhkv->bhv', qt, S)
                return (S, o)
            xs = tuple((jnp.moveaxis(a, 1, 0) for a in (q, k, v, g, beta)))
            _, o = jax.lax.scan(step, S0, xs)
            return jnp.moveaxis(o, 0, 1)

        def _reference_tuple_inner(hidden_states, w_ln1, w_ln2, W_qkvz, W_ba, conv_w, dt_bias, A_log, gate_norm_w, W_out, W_router, W_gate_e, W_up_e, W_down_e):
            B, S, _ = hidden_states.shape
            resid = hidden_states
            x = zrms(hidden_states, w_ln1)
            qkvz = x @ W_qkvz
            q, k, v, z = jnp.split(qkvz, [KEY_DIM, 2 * KEY_DIM, 2 * KEY_DIM + VAL_DIM], axis=-1)
            b, a = jnp.split(x @ W_ba, 2, axis=-1)
            beta = jax.nn.sigmoid(b)
            g = -jnp.exp(A_log) * jax.nn.softplus(a + dt_bias)
            mixed = jnp.concatenate([q, k, v], axis=-1)
            mixed = jax.nn.silu(causal_dwconv(mixed, conv_w))
            q, k, v = jnp.split(mixed, [KEY_DIM, 2 * KEY_DIM], axis=-1)
            q = q.reshape(B, S, HK, DK)
            k = k.reshape(B, S, HK, DK)
            v = v.reshape(B, S, HV, DV)
            rep = HV // HK
            q = jnp.repeat(q, rep, axis=2)
            k = jnp.repeat(k, rep, axis=2)
            q = q * jax.lax.rsqrt(jnp.sum(q * q, -1, keepdims=True) + EPS)
            k = k * jax.lax.rsqrt(jnp.sum(k * k, -1, keepdims=True) + EPS)
            q = q * DK ** (-0.5)
            core = gated_delta_rule(q, k, v, g, beta)
            core = core * jax.lax.rsqrt(jnp.mean(core * core, -1, keepdims=True) + EPS) * gate_norm_w
            core = core * jax.nn.silu(z.reshape(B, S, HV, DV))
            h = resid + core.reshape(B, S, VAL_DIM) @ W_out
            resid = h
            x = zrms(h, w_ln2)
            probs = jax.nn.softmax(x @ W_router, axis=-1)
            topv, topi = jax.lax.top_k(probs, TOPK)
            topv = topv / jnp.sum(topv, -1, keepdims=True)
            route = jnp.sum(jax.nn.one_hot(topi, NEXP, dtype=x.dtype) * topv[..., None], axis=-2)
            gate_h = jnp.einsum('bsh,ehi->bsei', x, W_gate_e)
            up_h = jnp.einsum('bsh,ehi->bsei', x, W_up_e)
            exp_out = jnp.einsum('bsei,eih->bseh', jax.nn.silu(gate_h) * up_h, W_down_e)
            moe_out = jnp.einsum('bseh,bse->bsh', exp_out, route)
            return (resid + moe_out, topi)
        key = jax.random.key(seed)
        ks = jax.random.split(key, 12)

        def lin(k, shape, fan_in):
            return jax.random.normal(k, shape, jnp.float32) * fan_in ** (-0.5)
        return {'hidden_states': jax.random.normal(ks[0], (1, 256, HID), jnp.float32), 'w_ln1': jnp.zeros((HID,), jnp.float32), 'w_ln2': jnp.zeros((HID,), jnp.float32), 'W_qkvz': lin(ks[1], (HID, 2 * KEY_DIM + 2 * VAL_DIM), HID), 'W_ba': lin(ks[2], (HID, 2 * HV), HID), 'conv_w': jax.random.normal(ks[3], (CONV_DIM, KCONV), jnp.float32) * KCONV ** (-0.5), 'dt_bias': jax.random.normal(ks[4], (HV,), jnp.float32) * 0.1, 'A_log': jnp.log(jax.random.uniform(ks[5], (HV,), jnp.float32, 1.0, 16.0)), 'gate_norm_w': jnp.ones((DV,), jnp.float32), 'W_out': lin(ks[6], (VAL_DIM, HID), VAL_DIM), 'W_router': lin(ks[7], (HID, NEXP), HID), 'W_gate_e': lin(ks[8], (NEXP, HID, INTER), HID), 'W_up_e': lin(ks[9], (NEXP, HID, INTER), HID), 'W_down_e': lin(ks[10], (NEXP, INTER, HID), INTER)}
    _L1_attn_in = _L1_attn_setup()

    def _L1_ffn_setup():
        import jax, jax.numpy as jnp
        import numpy as np
        EMBED_DIM = 128
        HIDDEN_DIM = 512
        NUM_EXPERTS = 8
        TOP_K = 2
        key = jax.random.key(seed)
        ks = jax.random.split(key, 4)
        std1 = float(np.sqrt(2.0 / EMBED_DIM))
        std2 = float(np.sqrt(2.0 / HIDDEN_DIM))
        x = jax.random.normal(ks[0], (1, 256, EMBED_DIM), dtype=jnp.float32)
        w_router = jax.random.normal(ks[1], (EMBED_DIM, NUM_EXPERTS), dtype=jnp.float32) * 0.02
        w1 = jax.random.normal(ks[2], (NUM_EXPERTS, EMBED_DIM, HIDDEN_DIM), dtype=jnp.float32) * std1
        b1 = jnp.zeros((NUM_EXPERTS, HIDDEN_DIM), dtype=jnp.float32)
        w2 = jax.random.normal(ks[3], (NUM_EXPERTS, HIDDEN_DIM, EMBED_DIM), dtype=jnp.float32) * std2
        b2 = jnp.zeros((NUM_EXPERTS, EMBED_DIM), dtype=jnp.float32)
        return {'x': x, 'w_router': w_router, 'w1': w1, 'b1': b1, 'w2': w2, 'b2': b2}
    _L1_ffn_in = _L1_ffn_setup()
    _d = {'L0_attn_x': _L0_attn_in['x'], 'L0_attn_W_q': _L0_attn_in['W_q'], 'L0_attn_W_dkv': _L0_attn_in['W_dkv'], 'L0_attn_W_uk': _L0_attn_in['W_uk'], 'L0_attn_W_uv': _L0_attn_in['W_uv'], 'L0_attn_W_o': _L0_attn_in['W_o'], 'L0_attn_ln_gamma': _L0_attn_in['ln_gamma'], 'L0_attn_ln_beta': _L0_attn_in['ln_beta'], 'L0_ffn_router_weight': _L0_ffn_in['router_weight'], 'L0_ffn_router_bias': _L0_ffn_in['router_bias'], 'L0_ffn_gate_w': _L0_ffn_in['gate_w'], 'L0_ffn_up_w': _L0_ffn_in['up_w'], 'L0_ffn_down_w': _L0_ffn_in['down_w'], 'L0_ffn_shared_gate_w': _L0_ffn_in['shared_gate_w'], 'L0_ffn_shared_up_w': _L0_ffn_in['shared_up_w'], 'L0_ffn_shared_down_w': _L0_ffn_in['shared_down_w'], 'L1_attn_w_ln1': _L1_attn_in['w_ln1'], 'L1_attn_w_ln2': _L1_attn_in['w_ln2'], 'L1_attn_W_qkvz': _L1_attn_in['W_qkvz'], 'L1_attn_W_ba': _L1_attn_in['W_ba'], 'L1_attn_conv_w': _L1_attn_in['conv_w'], 'L1_attn_dt_bias': _L1_attn_in['dt_bias'], 'L1_attn_A_log': _L1_attn_in['A_log'], 'L1_attn_gate_norm_w': _L1_attn_in['gate_norm_w'], 'L1_attn_W_out': _L1_attn_in['W_out'], 'L1_attn_W_router': _L1_attn_in['W_router'], 'L1_attn_W_gate_e': _L1_attn_in['W_gate_e'], 'L1_attn_W_up_e': _L1_attn_in['W_up_e'], 'L1_attn_W_down_e': _L1_attn_in['W_down_e'], 'L1_ffn_w_router': _L1_ffn_in['w_router'], 'L1_ffn_w1': _L1_ffn_in['w1'], 'L1_ffn_b1': _L1_ffn_in['b1'], 'L1_ffn_w2': _L1_ffn_in['w2'], 'L1_ffn_b2': _L1_ffn_in['b2']}
    _x0 = _d['L0_attn_x']
    _d['L0_attn_x'] = jax.random.normal(jax.random.fold_in(jax.random.key(seed), 1), (8, 512, 128), dtype=_x0.dtype)
    del _x0
    return _d

def reference(L0_attn_x, L0_attn_W_q, L0_attn_W_dkv, L0_attn_W_uk, L0_attn_W_uv, L0_attn_W_o, L0_attn_ln_gamma, L0_attn_ln_beta, L0_ffn_router_weight, L0_ffn_router_bias, L0_ffn_gate_w, L0_ffn_up_w, L0_ffn_down_w, L0_ffn_shared_gate_w, L0_ffn_shared_up_w, L0_ffn_shared_down_w, L1_attn_w_ln1, L1_attn_w_ln2, L1_attn_W_qkvz, L1_attn_W_ba, L1_attn_conv_w, L1_attn_dt_bias, L1_attn_A_log, L1_attn_gate_norm_w, L1_attn_W_out, L1_attn_W_router, L1_attn_W_gate_e, L1_attn_W_up_e, L1_attn_W_down_e, L1_ffn_w_router, L1_ffn_w1, L1_ffn_b1, L1_ffn_w2, L1_ffn_b2):

    def _L0_attn_ref(x, W_q, W_dkv, W_uk, W_uv, W_o, ln_gamma, ln_beta):
        import jax, jax.numpy as jnp
        import numpy as np
        D_MODEL = 128
        N_HEADS = 16
        HEAD_DIM = D_MODEL // N_HEADS
        KV_LATENT = 32
        LN_EPS = 1e-05

        def apply_rope(x):
            b, h, t, d = x.shape
            half = d // 2
            pos = jnp.arange(t, dtype=x.dtype)[:, None]
            inv_freq = 1.0 / 10000.0 ** (jnp.arange(half, dtype=x.dtype) / half)
            angles = pos * inv_freq[None, :]
            sin = jnp.sin(angles)[None, None]
            cos = jnp.cos(angles)[None, None]
            x1, x2 = (x[..., :half], x[..., half:])
            return jnp.concatenate([x1 * cos - x2 * sin, x1 * sin + x2 * cos], axis=-1)
        b, t, _ = x.shape
        q = (x @ W_q).reshape(b, t, N_HEADS, HEAD_DIM).transpose(0, 2, 1, 3)
        lat = x @ W_dkv
        mu = jnp.mean(lat, axis=-1, keepdims=True)
        var = jnp.mean(jnp.square(lat - mu), axis=-1, keepdims=True)
        lat = (lat - mu) * jax.lax.rsqrt(var + LN_EPS) * ln_gamma + ln_beta
        k = (lat @ W_uk).reshape(b, t, N_HEADS, HEAD_DIM).transpose(0, 2, 1, 3)
        v = (lat @ W_uv).reshape(b, t, N_HEADS, HEAD_DIM).transpose(0, 2, 1, 3)
        q = apply_rope(q)
        k = apply_rope(k)
        scores = jnp.einsum('bhqd,bhkd->bhqk', q, k) / jnp.sqrt(jnp.float32(HEAD_DIM))
        causal = jnp.tril(jnp.ones((t, t), dtype=bool))
        scores = jnp.where(causal[None, None], scores, -jnp.inf)
        attn = jax.nn.softmax(scores, axis=-1)
        out = jnp.einsum('bhqk,bhkd->bhqd', attn, v)
        out = out.transpose(0, 2, 1, 3).reshape(b, t, D_MODEL)
        return out @ W_o

    def _L0_ffn_ref(hidden_states, router_weight, router_bias, gate_w, up_w, down_w, shared_gate_w, shared_up_w, shared_down_w):
        import jax, jax.numpy as jnp
        import numpy as np
        from jax import lax
        B, S, H = (2, 128, 128)
        I = 64
        E = 32
        TOP_K = 4
        N_GROUP = 4
        TOPK_GROUP = 2
        SCALE = 2.5
        N_SHARED = 2
        SH_I = I * N_SHARED

        def _route(tokens, router_weight, router_bias):
            logits = tokens.astype(jnp.float32) @ router_weight.astype(jnp.float32).T
            scores = jax.nn.sigmoid(logits)
            sfc = scores + router_bias[None, :]
            T = tokens.shape[0]
            grp = sfc.reshape(T, N_GROUP, E // N_GROUP)
            group_scores = lax.top_k(grp, 2)[0].sum(-1)
            _, gidx = lax.top_k(group_scores, TOPK_GROUP)
            gmask = jax.nn.one_hot(gidx, N_GROUP, dtype=sfc.dtype).sum(1)
            smask = jnp.broadcast_to(gmask[:, :, None], (T, N_GROUP, E // N_GROUP)).reshape(T, E)
            tmp = jnp.where(smask > 0, sfc, 0.0)
            _, topk_idx = lax.top_k(tmp, TOP_K)
            topk_w = jnp.take_along_axis(scores, topk_idx, axis=1)
            topk_w = topk_w / (topk_w.sum(-1, keepdims=True) + 1e-20)
            topk_w = topk_w * SCALE
            return (topk_idx, topk_w)
        tokens = hidden_states.reshape(-1, H)
        topk_idx, topk_w = _route(tokens, router_weight, router_bias)
        gate_vals = jax.nn.silu(jnp.einsum('th,eih->tei', tokens, gate_w))
        up_vals = jnp.einsum('th,eih->tei', tokens, up_w)
        hidden_vals = gate_vals * up_vals
        expert_out = jnp.einsum('tei,ehi->teh', hidden_vals, down_w)
        sel = jnp.take_along_axis(expert_out, topk_idx[:, :, None], axis=1)
        mixed = (sel * topk_w[:, :, None].astype(sel.dtype)).sum(1)
        mixed = mixed.reshape(hidden_states.shape)
        sg = jax.nn.silu(jnp.einsum('bsh,ih->bsi', hidden_states, shared_gate_w))
        su = jnp.einsum('bsh,ih->bsi', hidden_states, shared_up_w)
        shared = jnp.einsum('bsi,hi->bsh', sg * su, shared_down_w)
        return mixed + shared

    def _L1_attn_ref(hidden_states, w_ln1, w_ln2, W_qkvz, W_ba, conv_w, dt_bias, A_log, gate_norm_w, W_out, W_router, W_gate_e, W_up_e, W_down_e):
        import jax, jax.numpy as jnp
        import numpy as np
        HID = 128
        HK, HV = (4, 8)
        DK, DV = (128, 128)
        KEY_DIM = HK * DK
        VAL_DIM = HV * DV
        CONV_DIM = 2 * KEY_DIM + VAL_DIM
        KCONV = 4
        NEXP, TOPK, INTER = (8, 2, 64)
        EPS = 1e-06

        def zrms(x, w):
            v = jnp.mean(x * x, axis=-1, keepdims=True)
            return x * jax.lax.rsqrt(v + EPS) * (1.0 + w)

        def causal_dwconv(x, w):
            xp = jnp.pad(x, ((0, 0), (KCONV - 1, 0), (0, 0)))
            kern = w.T[:, None, :]
            return jax.lax.conv_general_dilated(xp, kern, (1,), 'VALID', dimension_numbers=('NHC', 'HIO', 'NHC'), feature_group_count=CONV_DIM)

        def gated_delta_rule(q, k, v, g, beta):
            B = q.shape[0]
            S0 = jnp.zeros((B, HV, DK, DV), q.dtype)

            def step(S, inp):
                qt, kt, vt, gt, bt = inp
                S = S * jnp.exp(gt)[..., None, None]
                kv = jnp.einsum('bhk,bhkv->bhv', kt, S)
                delta = (vt - kv) * bt[..., None]
                S = S + jnp.einsum('bhk,bhv->bhkv', kt, delta)
                o = jnp.einsum('bhk,bhkv->bhv', qt, S)
                return (S, o)
            xs = tuple((jnp.moveaxis(a, 1, 0) for a in (q, k, v, g, beta)))
            _, o = jax.lax.scan(step, S0, xs)
            return jnp.moveaxis(o, 0, 1)

        def _reference_tuple_inner(hidden_states, w_ln1, w_ln2, W_qkvz, W_ba, conv_w, dt_bias, A_log, gate_norm_w, W_out, W_router, W_gate_e, W_up_e, W_down_e):
            B, S, _ = hidden_states.shape
            resid = hidden_states
            x = zrms(hidden_states, w_ln1)
            qkvz = x @ W_qkvz
            q, k, v, z = jnp.split(qkvz, [KEY_DIM, 2 * KEY_DIM, 2 * KEY_DIM + VAL_DIM], axis=-1)
            b, a = jnp.split(x @ W_ba, 2, axis=-1)
            beta = jax.nn.sigmoid(b)
            g = -jnp.exp(A_log) * jax.nn.softplus(a + dt_bias)
            mixed = jnp.concatenate([q, k, v], axis=-1)
            mixed = jax.nn.silu(causal_dwconv(mixed, conv_w))
            q, k, v = jnp.split(mixed, [KEY_DIM, 2 * KEY_DIM], axis=-1)
            q = q.reshape(B, S, HK, DK)
            k = k.reshape(B, S, HK, DK)
            v = v.reshape(B, S, HV, DV)
            rep = HV // HK
            q = jnp.repeat(q, rep, axis=2)
            k = jnp.repeat(k, rep, axis=2)
            q = q * jax.lax.rsqrt(jnp.sum(q * q, -1, keepdims=True) + EPS)
            k = k * jax.lax.rsqrt(jnp.sum(k * k, -1, keepdims=True) + EPS)
            q = q * DK ** (-0.5)
            core = gated_delta_rule(q, k, v, g, beta)
            core = core * jax.lax.rsqrt(jnp.mean(core * core, -1, keepdims=True) + EPS) * gate_norm_w
            core = core * jax.nn.silu(z.reshape(B, S, HV, DV))
            h = resid + core.reshape(B, S, VAL_DIM) @ W_out
            resid = h
            x = zrms(h, w_ln2)
            probs = jax.nn.softmax(x @ W_router, axis=-1)
            topv, topi = jax.lax.top_k(probs, TOPK)
            topv = topv / jnp.sum(topv, -1, keepdims=True)
            route = jnp.sum(jax.nn.one_hot(topi, NEXP, dtype=x.dtype) * topv[..., None], axis=-2)
            gate_h = jnp.einsum('bsh,ehi->bsei', x, W_gate_e)
            up_h = jnp.einsum('bsh,ehi->bsei', x, W_up_e)
            exp_out = jnp.einsum('bsei,eih->bseh', jax.nn.silu(gate_h) * up_h, W_down_e)
            moe_out = jnp.einsum('bseh,bse->bsh', exp_out, route)
            return (resid + moe_out, topi)
        return _reference_tuple_inner(hidden_states, w_ln1, w_ln2, W_qkvz, W_ba, conv_w, dt_bias, A_log, gate_norm_w, W_out, W_router, W_gate_e, W_up_e, W_down_e)[0]

    def _L1_ffn_ref(x, w_router, w1, b1, w2, b2):
        import jax, jax.numpy as jnp
        import numpy as np
        EMBED_DIM = 128
        HIDDEN_DIM = 512
        NUM_EXPERTS = 8
        TOP_K = 2
        orig_shape = x.shape
        xf = x.reshape(-1, EMBED_DIM)
        logits = xf @ w_router
        probs = jax.nn.softmax(logits, axis=-1)
        topk_w, topk_idx = jax.lax.top_k(probs, TOP_K)
        mask = jax.nn.one_hot(topk_idx, NUM_EXPERTS, dtype=xf.dtype)
        weights = jnp.sum(topk_w[..., None] * mask, axis=1)
        h = jnp.einsum('te,ieh->tih', xf, w1) + b1
        h = jax.nn.gelu(h)
        out = jnp.einsum('tih,ihe->tie', h, w2) + b2
        out = jnp.sum(out * weights[..., None], axis=1)
        return out.reshape(orig_shape)
    x = L0_attn_x
    xn = _layernorm(x, axis=-1)
    x = x + _L0_attn_ref(xn, L0_attn_W_q, L0_attn_W_dkv, L0_attn_W_uk, L0_attn_W_uv, L0_attn_W_o, L0_attn_ln_gamma, L0_attn_ln_beta) + _L0_ffn_ref(xn, L0_ffn_router_weight, L0_ffn_router_bias, L0_ffn_gate_w, L0_ffn_up_w, L0_ffn_down_w, L0_ffn_shared_gate_w, L0_ffn_shared_up_w, L0_ffn_shared_down_w)
    xn = _layernorm(x, axis=-1)
    x = x + _L1_attn_ref(xn, L1_attn_w_ln1, L1_attn_w_ln2, L1_attn_W_qkvz, L1_attn_W_ba, L1_attn_conv_w, L1_attn_dt_bias, L1_attn_A_log, L1_attn_gate_norm_w, L1_attn_W_out, L1_attn_W_router, L1_attn_W_gate_e, L1_attn_W_up_e, L1_attn_W_down_e) + _L1_ffn_ref(xn, L1_ffn_w_router, L1_ffn_w1, L1_ffn_b1, L1_ffn_w2, L1_ffn_b2)
    return x

_drawn_inputs = setup_inputs


def setup_inputs(seed=0):
    import zlib

    import numpy as np

    out = dict(_drawn_inputs(seed))
    spreads = {'L0_attn_ln_gamma': (1.0, 0.577),
     'L0_attn_ln_beta': (0.0, 0.1),
     'L0_ffn_router_bias': (0.0, 0.481),
     'L1_attn_w_ln1': (0.0, 0.1),
     'L1_attn_w_ln2': (0.0, 0.1),
     'L1_attn_gate_norm_w': (1.0, 0.2),
     'L1_ffn_b1': (0.0, 0.737),
     'L1_ffn_b2': (0.0, 0.73)}
    factors = {'L0_ffn_router_weight': 4.194,
     'L0_ffn_gate_w': 3.629,
     'L0_ffn_up_w': 3.84,
     'L0_ffn_down_w': 3.7,
     'L0_ffn_shared_gate_w': 3.504,
     'L0_ffn_shared_up_w': 3.273,
     'L0_ffn_shared_down_w': 3.16,
     'L1_attn_dt_bias': 3.718}
    for name, (base, spread) in spreads.items():
        noise = np.random.default_rng([zlib.crc32(name.encode()), seed]).standard_normal(out[name].shape)
        drawn = base * np.exp(spread * noise) if base else spread * noise
        out[name] = jnp.asarray(drawn.astype(out[name].dtype))
    for name, factor in factors.items():
        out[name] = (out[name] * factor).astype(out[name].dtype)
    return out
```

```python
from contextlib import ExitStack

import numpy as np

import concourse.bass as bass
from concourse import mybir

F32 = mybir.dt.float32
BF16 = mybir.dt.bfloat16
ALU = mybir.AluOpType
ACT = mybir.ActivationFunctionType
AX = mybir.AxisListType.X

P = 128
LOOPS = 8
B, S, D = 8, 512, 128
NT = S // P
NH, HD = 16, 8
NP = NH // 2
NQ = NH // 4
LAT = 32
E0, I0, G0 = 32, 64, 4
PR0 = E0 * I0 // P
HK, HV = 4, 8
NQKV = 2 * HK + HV
E1, I1 = 8, 64
PR1 = E1 * I1 // P
EF, IF = 8, 512
FC = IF // P
NEG = -1.0e30
PAD = -3.0e38
QSPLIT = (0, 0, 1, 0, 2, 1)
KSPLIT = (0, 1, 0, 2, 0, 1)
KROWS = 6 * HD
MROWS = KROWS + 3
EPS0, EPS1 = 1e-5, 1e-6
SCALE0 = 2.5

WEIGHTS = {
    "Wq": ([D, D], F32), "Wqr": ([D, D], F32), "Wdkv": ([D, LAT], F32), "Wuk": ([LAT, D], F32),
    "Wukr": ([LAT, D], F32), "Wuv": ([LAT, D], F32), "Wo": ([D, D], F32), "gam": ([LAT, 1], F32),
    "bet": ([LAT, 1], F32), "rw0": ([D, E0], F32), "rb0": ([P, E0], F32),
    "cosq": ([P, S], F32), "sinq": ([P, S], F32), "cosk": ([P, S], F32), "sink": ([P, S], F32),
    "ident": ([P, P], F32), "identb": ([P, P], BF16), "maskq": ([P, S], F32), "maskt": ([P, P], BF16),
    "grank": ([P, 2, NT, G0, G0], F32), "sel0": ([96, PR0, P], BF16),
    "gate0": ([D, PR0, P], F32), "up0": ([D, PR0, P], F32), "down0": ([P, PR0, D], F32),
    "sg": ([D, P], F32), "su": ([D, P], F32), "sd": ([P, D], F32),
    "ln1": ([D, 1], F32), "ln2": ([D, 1], F32), "Wqkvz": ([D, (NQKV + HV) * P], F32), "Wba": ([D, 2 * HV], F32),
    "convw": ([P, NQKV, 4], F32), "dtb": ([P, HV], F32), "alog": ([P, HV], F32), "gnw": ([P, 1], F32),
    "Wout": ([P, HV, D], F32), "r1": ([D, E1], F32), "ge1": ([D, PR1, P], F32), "ue1": ([D, PR1, P], F32),
    "de1": ([P, PR1, D], F32), "sel1": ([96, PR1, P], BF16), "rf": ([D, EF], F32),
    "b1": ([P, EF * FC], F32), "b2": ([EF, D], F32),
    "upto": ([P, P], F32), "after": ([P, P], F32), "ones": ([P, P], F32),
    "below": ([P, P], BF16), "notabove": ([P, P], BF16), "blk": ([P, 4, P], F32),
}
EARLY = 19


class Signal:

    def __init__(self, name, sem, per):
        self.name, self.sem, self.per, self.n = name, sem, per, 0

    def at(self, b, n):
        return self.sem, b * self.per + n

    @property
    def up(self):
        self.n += 1
        return self.sem, 1

    @property
    def up16(self):
        self.n += 16
        return self.sem, 16


def schedule_l0():
    order, n = [("s0",)], 0
    for p in range(PR0 + 1):
        order.append(("moe0", p))
        if p >= 1:
            for _ in range(4):
                order.append(("max", n))
                n += 1
    order.append(("moe0_last",))
    order.append(("maxrows",))
    for g in range(NQ):
        order += [("exp", g, i) for i in range(12)]
        if g:
            order.append(("pv", g - 1))
    order.append(("pv", NQ - 1))
    order.append(("attn_out",))
    return order


TSTEPS = 16


def schedule_l1():
    order, f = [("qkv", m) for m in range(NQKV + 1)], 0
    for c in range(NT):
        order.append(("chunk", c))
        for s in range(TSTEPS):
            for half in range(2):
                order.append(("inv", c, half, s))
            if s % 2 == 1:
                order.append(("ffn", f))
                f += 1
        order.append(("state", c))
    order.append(("hidden",))
    for p in range(PR1):
        order.append(("moe1", p))
    order.append(("moe1_last",))
    return order


def build(nc, x_in, w_last, out, weights, scratch, per, sizes):
    scrq, scrk, scrm, scro = scratch
    x_v = x_in.rearrange("b (t p) d -> b p t d", p=P)
    out_v = out.rearrange("b (t p) d -> b p t d", p=P)
    with ExitStack() as ctx:
        def sb(name, shape, dt=F32):
            return ctx.enter_context(nc.sbuf_tensor(name, shape, dt))

        signals = {}

        def sig(name):
            signals[name] = Signal(name, ctx.enter_context(nc.semaphore(name)), per.get(name, 1))
            return signals[name]

        W = {n: sb("w_" + n, shape, dt) for n, (shape, dt) in WEIGHTS.items()}
        bank = [ctx.enter_context(nc.psum_tensor(f"bank{i}", [P, 512], F32)) for i in range(8)]

        x = sb("x", [P, NT, D])
        x1 = sb("x1", [P, NT, D])
        nhalf = sb("nhalf", [P, 32])
        junk = sb("junk", [P, 8, P])
        ARENA = 27600
        arena = sb("arena", [P, ARENA])
        at = [0]

        def cut(shape, dt=F32, parts=P):
            n = int(np.prod(shape))
            words = n if dt == F32 else n // 2
            a = arena[0:parts, at[0]:at[0] + words]
            at[0] += words
            assert at[0] <= ARENA, at
            if dt != F32:
                a = a.bitcast(dt)
            if len(shape) == 2:
                a = a.rearrange("p (a b) -> p a b", a=shape[0])
            if len(shape) == 3:
                a = a.rearrange("p (a b c) -> p a b c", a=shape[0], b=shape[1])
            return a

        W96 = sb("W96", [96, S], BF16)
        W96b = sb("W96b", [96, S], BF16)
        wring = sb("wring", [P, 2, FC * P + FC * D])
        stats = sb("stats", [P, NT, 6])
        mv = sb("mv", [P, NT, 2])
        var4 = sb("var4", [P, NT])
        rstd = sb("rstd", [P, NT])
        top = sb("top", [P, NT, 8])
        top4 = sb("top4", [P, NT, 8])
        top2 = sb("top2", [P, NT, 8])
        tmp36 = sb("tmp36", [P, NT, E0 + 4])
        pad8 = sb("pad8", [P, NT, EF + 6])
        neg_a = sb("neg_a", [P, HV])
        tick = sb("tick", [P, 96])

        xn = cut([NT, D]); xnT = cut([S]); qf = cut([S]); qf2 = cut([S]); kf = cut([S]); kf2 = cut([S])
        QS = cut([NP, S], BF16); KS = cut([NP, S], BF16); V32 = cut([NT, NH, 32])
        latn = cut([NT, LAT]); latT = cut([S], parts=LAT); stats2 = cut([NT, 6]); mv2 = cut([NT, 2])
        var42 = cut([NT]); rstd2 = cut([NT])
        sc0 = cut([NT, E0]); sfc = cut([NT, E0]); gtop = cut([NT * G0, 8]); gs = cut([NT * G0])
        cmp0 = cut([NT * G0 * G0]); cmp1 = cut([NT * G0 * G0]); rank = cut([NT * G0])
        HID = cut([2, S])
        mr = cut([NT, E0 + 4]); w0 = cut([NT, E0]); wsum = cut([NT]); wrec = cut([NT])
        mx = cut([NH * NT]); nmx = cut([2 * NH * NT]); nmt = cut([P], parts=64); nm3 = cut([3, P], BF16, parts=64)
        nmr = cut([P], parts=64)
        OS = cut([NQ, S])
        num, den, rden, att = xn.rearrange("p a b -> p (a b)"), xnT, qf, qf2
        PT = cut([20, S])
        l0_end = at[0]
        at[0] = l0_end - 10 * S
        qs3 = cut([3, S], BF16); ks3 = cut([3, S], BF16)
        wt = cut([S], parts=E0); wtm = cut([S], BF16, parts=E0); wtr = cut([S], parts=E0)
        SG = cut([2, S]); HDT = cut([2, S])
        assert at[0] <= l0_end

        at[0] = 0
        xn1 = cut([NT, D]); zz = cut([NT, D]); xn1T = cut([S]); zT = cut([S])
        ssq = cut([NT]); rz = cut([NT])
        ba = cut([NT, 2 * HV]); aab = cut([NT, HV]); sp = cut([NT, HV]); beta = cut([NT, HV]); gg = cut([NT, HV])
        eG = cut([3, NT * HV])
        lf = cut([NT, EF]); pf = cut([NT, EF]); mrf = cut([NT, EF + 6]); wf = cut([NT, EF]); red4 = cut([NT]); rec4 = cut([NT])
        wfT = cut([S], parts=EF)
        CV = arena[0:P, at[0]:at[0] + 3 * S].rearrange("p (a b) -> p a b", a=3)
        GM = cut([2, 4 * P]); DU = cut([4 * P])
        qkT = cut([2 * HK, S])
        vT = cut([HV, S])
        ktok = cut([HK, P]); vb = cut([HV, P]); sz = cut([HV, P])
        ss8 = cut([8]); rr8 = cut([8]); rk2 = cut([HK]); nlam = cut([HV]); rkb = cut([HV]); s1 = cut([HV])
        rq2 = cut([HK]); rqs = cut([HK]); so8 = cut([HV]); rc8 = cut([HV])
        DL = [cut([4 * P]) for _ in range(2)]
        N_ = [cut([4 * P]) for _ in range(2)]
        QKD = cut([HV, P])
        State = cut([HV, P])
        R = cut([HV, P]); o1s = cut([HV, P]); dl = cut([HV, P]); DLS = cut([HV, P]); coreT = cut([HV, P])
        NTT = [cut([4 * P]) for _ in range(2)]
        halves = lambda a: [a[:, 4 * i:4 * i + 4, :].rearrange("p a b -> p (a b)") for i in range(2)]
        T = {"NT": NTT, "TT": NTT, "M2": N_, "X": DL, "M": halves(o1s), "MT": halves(R), "L32": halves(dl),
             "L64": halves(coreT), "L128": halves(DLS)}
        GH = cut([2, S]); facc = cut([NT, D])
        hbuf = zz
        oo, core = R, junk
        l1_end = at[0]
        assert max(l0_end, l1_end) <= ARENA, (l0_end, l1_end)
        hT = xn1T
        SG1, HDT1, HID1 = CV, coreT.rearrange("p (u a) b -> p u (a b)", u=2), GH
        wr = lf; wt1 = wfT

        names = """x_in g_init weights_a weights_b setup_v setup_a out_ready out_dma
            v_link v_var g_rstd v_xn p_xnT a_xnT p_q p_lat v_q v_k v_lat p_latT v_latT p_k p_v a_v
            v_lvar g_lrstd a_lexp v_lsfc v_w0 p_w0T v_w96 v_qs3 v_ks3 d_scrq d_scrk d_q d_k
            p_gate p_up p_wb a_sg v_t v_hid p_down p_max v_max v_nm p_mT v_nm3 d_scrm d_m
            p_score a_p p_o v_os d_scro d_nd v_att p_acc v_x1
            v_var1 g_rstd1 v_xn1 v_ms1 g_rz v_z p_xn1T a_xn1T p_zT v_zT p_ba a_eb v_ab a_eab a_sp v_g p_gc a_eG
            v_lm a_fe v_wf p_wfT v_wfT p_qkv a_cv v_cv a_qkv
            p_kt p_qt p_vt p_z a_kt a_ss a_sz v_sse g_rr v_sc a_vb p_kk g_gm p_d a_d v_N v_qkd
            p_inv0 p_inv1 v_inv0 v_inv1 a_inv0 a_inv1 g_inv0 g_inv1
            p_w v_R p_o1 a_o1 p_dl a_dl v_dls p_o2 v_o p_s v_S a_so v_sr g_rc v_core p_ct a_ct p_wout
            v_h v_ms2 g_rz2 v_h2 p_hT v_hT p_r1 v_lm1 a_fe1 v_w1r p_w1T v_w96b
            p_gate1 p_up1 p_wb1 a_sg1 v_hid1 p_down1 d_w0 d_w1 p_fh a_gh p_fo v_fo""".split()
        s = {n: sig(n) for n in names}
        L0, L1 = schedule_l0(), schedule_l1()

        ticks = []

        def wait_alone(engine, sem, value):
            engine.wait_ge(sem, value)
            engine.tensor_tensor(tick[:, len(ticks):len(ticks) + 1], nhalf[:, 0:1], nhalf[:, 0:1], ALU.add)
            ticks.append(engine)

        block = ctx.enter_context(nc.Block())

        @block.sync
        def _(sp_):
            for i, n in enumerate(WEIGHTS):
                lot = s["weights_a"] if i < EARLY else s["weights_b"]
                sp_.dma_start(W[n][:], weights[n]).then_inc(lot.sem, 16)
            with sp_.Fori(0, LOOPS) as b:
                for e in range(2):
                    sp_.wait_ge(*s["p_fo"].at(b, 0))
                    sp_.dma_start(wring[:, e, :], w_last[e]).then_inc(*s[f"d_w{e}"].up16)
                sp_.wait_ge(*s["v_x1"].at(b, 0))
                sp_.dma_start(x[:, :, :], x_v[bass.ds(b, 1)].rearrange("a p t d -> p (a t) d")).then_inc(*s["x_in"].up16)
                for name, src, scr, dst, kinds in (("q", qs3, scrq, QS, QSPLIT), ("k", ks3, scrk, KS, KSPLIT)):
                    sp_.wait_ge(*s[f"v_{name}s3"].at(b, 1))
                    sp_.dma_start(scr.rearrange("s p n -> p s n"), src).then_inc(*s["d_scr" + name].up16)
                    sp_.wait_ge(*s["d_scr" + name].at(b, 16))
                    sp_.wait_ge(*s["g_init"].at(b, 3))
                    for hh in range(2):
                        for t, kind in enumerate(kinds):
                            rows = 64 * hh + HD * t
                            part = bass.AP(tensor=scr.tensor, offset=kind * P * S + hh * HD * S,
                                           ap=[[S, HD], [2 * HD * S, NP], [1, S]])
                            sp_.dma_start(dst[rows:rows + HD, :, :], part).then_inc(*s["d_" + name].up16)
                sp_.wait_ge(*s["v_nm3"].at(b, 1))
                sp_.dma_start(scrm.rearrange("s p n -> p s n"), nm3).then_inc(*s["d_scrm"].up16)
                sp_.wait_ge(*s["d_scrm"].at(b, 16))
                for hh in range(2):
                    part = bass.AP(tensor=scrm.tensor, offset=hh * S, ap=[[64 * P, 3], [2 * S, NP], [1, S]])
                    sp_.dma_start(QS[64 * hh + KROWS:64 * hh + MROWS, :, :], part).then_inc(*s["d_m"].up16)
                sp_.wait_ge(*s["v_os"].at(b, NQ))
                for j in range(4):
                    part = bass.AP(tensor=scro.tensor, offset=j * 9 * S, ap=[[S, 9], [4 * 9 * S, NQ], [1, S]])
                    sp_.dma_start(part, OS[32 * j:32 * j + 9, :, :]).then_inc(*s["d_scro"].up16)
                sp_.wait_ge(*s["d_scro"].at(b, 64))
                sp_.dma_start(num, bass.AP(tensor=scro.tensor, offset=0, ap=[[9 * S, NH], [S, HD], [1, S]])
                              ).then_inc(*s["d_nd"].up16)
                sp_.dma_start(den, bass.AP(tensor=scro.tensor, offset=HD * S, ap=[[9 * S, NH], [0, HD], [1, S]])
                              ).then_inc(*s["d_nd"].up16)
                for e in range(2, EF):
                    sp_.wait_ge(*s["p_fo"].at(b, FC * (e - 1)))
                    sp_.dma_start(wring[:, e % 2, :], w_last[e]).then_inc(*s[f"d_w{e % 2}"].up16)
            sp_.wait_ge(*s["out_dma"].at(LOOPS, 0))

        @block.tensor
        def _(pe):
            mm = nc.tensor.matmul
            pe.wait_ge(s["weights_a"].sem, 16 * EARLY)
            pe.wait_ge(s["weights_b"].sem, 16 * (len(WEIGHTS) - EARLY))
            pe.wait_ge(s["setup_v"].sem, 2)
            with pe.Fori(0, LOOPS) as b:
                met = {}

                def need(name, n):
                    if met.get(name, 0) < n:
                        pe.wait_ge(*s[name].at(b, n))
                        met[name] = n

                def after(name, n, i):
                    need(name, n)
                    return bank[i]

                def tr(dst, src, k=P):
                    return nc.tensor.transpose(dst, src, W["ident"][0:k, 0:k])

                pe.wait_ge(*s["out_ready"].at(b, 0))
                bk = bank[0]
                for t in range(NT):
                    pe.wait_ge(*s["v_xn"].at(b, t + 1))
                    last = tr(bk[:, t * P:(t + 1) * P], xn[:, t, :])
                last.then_inc(*s["p_xnT"].up)
                pe.wait_ge(*s["a_xnT"].at(b, 1))
                q1, q2 = bank[1], bank[2]
                mm(q1[:, :], W["Wq"][:], xnT, start=True, stop=True)
                mm(q2[:, :], W["Wqr"][:], xnT, start=True, stop=True).then_inc(*s["p_q"].up)
                bk = bank[3]
                for t in range(NT):
                    mm(bk[:, t * LAT:(t + 1) * LAT], xnT[:, t * P:(t + 1) * P], W["Wdkv"][:], start=True, stop=True)
                for t in range(NT):
                    last = mm(bk[:, 128 + t * E0:128 + (t + 1) * E0], xnT[:, t * P:(t + 1) * P], W["rw0"][:],
                              start=True, stop=True)
                last.then_inc(*s["p_lat"].up)
                pe.wait_ge(*s["v_lat"].at(b, 1))
                bk = bank[4]
                for t in range(NT):
                    last = tr(bk[0:LAT, t * P:(t + 1) * P], latn[:, t, :])
                last.then_inc(*s["p_latT"].up)
                pe.wait_ge(*s["v_latT"].at(b, 1))
                k1, k2 = after("v_q", 1, 1), bank[2]
                mm(k1[:, :], W["Wuk"][:], latT, start=True, stop=True)
                mm(k2[:, :], W["Wukr"][:], latT, start=True, stop=True).then_inc(*s["p_k"].up)
                bk = bank[5]
                for t in range(NT):
                    last = mm(bk[:, t * P:(t + 1) * P], latT[:, t * P:(t + 1) * P], W["Wuv"][:], start=True, stop=True)
                last.then_inc(*s["p_v"].up)

                def s0():
                    pe.wait_ge(*s["v_w0"].at(b, 1))
                    bk = after("v_latT", 1, 4)
                    for t in range(NT):
                        last = tr(bk[0:E0, t * P:(t + 1) * P], w0[:, t, :])
                    last.then_inc(*s["p_w0T"].up)

                def down0(p):
                    pe.wait_ge(*s["v_hid"].at(b, p + 1))
                    for t in range(NT):
                        last = mm(bank[7][:, t * P:(t + 1) * P], HID[:, p % 2, t * P:(t + 1) * P],
                                  W["down0"][:, p, :] if p < PR0 else W["sd"][:],
                                  start=(p == 0 and t == 0), stop=False, skip_group_check=True)
                    last.then_inc(*s["p_down"].up)

                def moe0(p):
                    bk = after(*(("v_k", 1) if p < 2 else ("a_sg", p - 1)), 1 + p % 2)
                    mm(bk[:, :], W["gate0"][:, p, :] if p < PR0 else W["sg"][:], xnT, start=True, stop=True
                       ).then_inc(*s["p_gate"].up)
                    bk = after(*((("v_lsfc", 1), ("a_v", 1))[p] if p < 2 else ("v_t", p - 1)), 3 + 2 * (p % 2))
                    mm(bk[:, :], W["up0"][:, p, :] if p < PR0 else W["su"][:], xnT, start=True, stop=True
                       ).then_inc(*s["p_up"].up)
                    if p < PR0:
                        if p == 0:
                            pe.wait_ge(*s["v_w96"].at(b, 1))
                        bk = after("v_hid", p - 1, 4 + 2 * (p % 2)) if p >= 2 else bank[4 + 2 * p]
                        mm(bk[:, :], W["sel0"][:, p, :], W96[:, :], start=True, stop=True).then_inc(*s["p_wb"].up)
                    if p:
                        down0(p - 1)

                def smax(n):
                    h, qt = n // NT, n % NT
                    o, w = 64 * (h % 2), P * (qt + 1)
                    if n == 0:
                        pe.wait_ge(*s["d_q"].at(b, 16 * 12))
                        pe.wait_ge(*s["d_k"].at(b, 16 * 12))
                    bk = after(*(("v_max", n) if n else ("a_xnT", 1)), 0)
                    mm(bk[:, 0:w], QS[o:o + KROWS, h // 2, qt * P:(qt + 1) * P], KS[o:o + KROWS, h // 2, 0:w],
                       start=True, stop=True, tile_position=(o, 0)).then_inc(*s["p_max"].up)

                def maxrows():
                    pe.wait_ge(*s["v_nm"].at(b, 1))
                    bk = after("v_max", NH * NT, 0)
                    tr(bk[:, 0:P], nmx).then_inc(*s["p_mT"].up)

                def score(g, i):
                    n = 12 * g + i
                    if n == 0:
                        pe.wait_ge(*s["d_m"].at(b, 32))
                    pair, k = 2 * g + i // 6, i % 6
                    last = (("a_sg", PR0 + 1), ("a_sg", PR0), ("v_hid", PR0 + 1), ("v_hid", PR0 - 1), ("v_t", PR0))
                    bk = after(*(last[n] if n < 5 else ("a_p", n - 4)), 1 + n % 5)
                    parts = {0: [(0, 0, 0)], 1: [(1, 0, 0)], 2: [(0, 1, 0), (0, 3, 384)], 3: [(1, 1, 0), (1, 3, 384)],
                             4: [(0, 2, 0)], 5: [(1, 2, 0)]}[k]
                    for hh, kt, col in parts:
                        o, w = 64 * hh, S - P * kt
                        mm(bk[:, col:col + w], KS[o:o + MROWS, pair, kt * P:(kt + 1) * P],
                           QS[o:o + MROWS, pair, kt * P:S], start=True, stop=False, tile_position=(o, 0),
                           skip_group_check=True)
                        last = mm(bk[:, col:col + P], W["identb"][:], W["maskt"][:], start=False, stop=True,
                                  skip_group_check=True)
                    last.then_inc(*s["p_score"].up)

                def pv(g):
                    pe.wait_ge(*s["a_p"].at(b, 12 * g + 12))
                    if g == 0:
                        pe.wait_ge(*s["a_v"].at(b, 1))
                    bk = after(*((("v_hid", PR0), ("v_nm3", 1))[g] if g < 2 else ("v_os", g - 1)), 0 if g % 2 else 6)
                    for kt in range(NT):
                        for j in range(4):
                            slot, col = {0: (j % 2, 0), 1: (2 + j % 2, 0), 2: (4, 256 * (j % 2)), 3: (2 + j % 2, 384)}[kt]
                            slot += 5 * (j // 2) + 10 * (g % 2)
                            last = mm(bk[32 * j:32 * j + 32, kt * P:S], V32[:, kt, 4 * g + j, :],
                                      PT[:, slot, col:col + S - kt * P], start=(kt == 0), stop=(kt == NT - 1),
                                      tile_position=(0, 32 * j), skip_group_check=True)
                    last.then_inc(*s["p_o"].up)

                def attn_out():
                    pe.wait_ge(*s["v_att"].at(b, 1))
                    for t in range(NT):
                        last = mm(bank[7][:, t * P:(t + 1) * P], att[:, t * P:(t + 1) * P], W["Wo"][:],
                                  start=False, stop=True, skip_group_check=True)
                    last.then_inc(*s["p_acc"].up)

                steps = {"s0": s0, "moe0": moe0, "max": smax, "moe0_last": lambda: down0(PR0), "maxrows": maxrows,
                         "exp": score, "pv": pv, "attn_out": attn_out}
                for step in L0:
                    steps[step[0]](*step[1:])

                bk = after("v_os", NQ, 0)
                for t in range(NT):
                    pe.wait_ge(*s["v_xn1"].at(b, t + 1))
                    last = tr(bk[:, t * P:(t + 1) * P], xn1[:, t, :])
                last.then_inc(*s["p_xn1T"].up)
                bk = after("a_p", 12 * NQ - 2, 1)
                for t in range(NT):
                    pe.wait_ge(*s["v_z"].at(b, t + 1))
                    last = tr(bk[:, t * P:(t + 1) * P], zz[:, t, :])
                last.then_inc(*s["p_zT"].up)
                pe.wait_ge(*s["a_xn1T"].at(b, 1))
                pe.wait_ge(*s["v_zT"].at(b, 1))
                bk = after("a_p", 12 * NQ - 1, 2)
                for t in range(NT):
                    mm(bk[:, t * 16:(t + 1) * 16], zT[:, t * P:(t + 1) * P], W["Wba"][:], start=True, stop=True)
                for t in range(NT):
                    last = mm(bk[:, 64 + t * EF:64 + (t + 1) * EF], xn1T[:, t * P:(t + 1) * P], W["rf"][:],
                              start=True, stop=True)
                last.then_inc(*s["p_ba"].up)

                def qkv(m):
                    if m < NQKV:
                        first = (("a_p", 12 * NQ - 4), ("a_p", 12 * NQ - 3), ("v_os", NQ - 1))
                        bk = after(*(first[m] if m < 3 else ("v_cv", m - 2)), 4 + m % 3)
                        mm(bk[:, :], W["Wqkvz"][:, m * P:(m + 1) * P], zT, start=True, stop=True
                           ).then_inc(*s["p_qkv"].up)
                    if m == 4:
                        pe.wait_ge(*s["v_g"].at(b, 1))
                        bk = after("a_p", 12 * NQ, 3)
                        g2 = gg.rearrange("p a b -> p (a b)")
                        mm(bk[:, 0:32], W["upto"][:], g2, start=True, stop=True)
                        mm(bk[:, 32:64], W["after"][:], g2, start=True, stop=True)
                        mm(bk[:, 64:96], W["ones"][:], g2, start=True, stop=True).then_inc(*s["p_gc"].up)
                    if m == 6:
                        pe.wait_ge(*s["v_wf"].at(b, 1))
                        bk = after("a_xn1T", 1, 0)
                        for t in range(NT):
                            last = tr(bk[0:EF, t * P:(t + 1) * P], wf[:, t, :])
                        last.then_inc(*s["p_wfT"].up)

                def chunk(c):
                    cs = slice(c * P, (c + 1) * P)
                    if c == 0:
                        pe.wait_ge(*s["a_qkv"].at(b, NQKV))
                    bk = after(*(("a_ct", 2 * c) if c else ("v_cv", NQKV)), 4)
                    for h in range(HK):
                        last = tr(bk[:, h * P:(h + 1) * P], qkT[:, HK + h, cs])
                    last.then_inc(*s["p_kt"].up)
                    bk = after(*(("v_dls", 8 * c) if c else ("v_cv", NQKV - 2)), 5)
                    for h in range(HK):
                        last = tr(bk[:, h * P:(h + 1) * P], qkT[:, h, cs])
                    last.then_inc(*s["p_qt"].up)
                    for i in range(2):
                        bk = after(*((("v_o", 2 * c - 1), ("v_S", 8 * c - 4))[i] if c else (("v_cv", NQKV - 1), ("v_zT", 1))[i]),
                                   (6, 1)[i])
                        for h in range(4):
                            last = tr(bk[:, h * P:(h + 1) * P], vT[:, 4 * i + h, cs])
                        last.then_inc(*s["p_vt"].up)
                    for i in range(2):
                        bk = after(*((("v_S", 8 * c), ("a_ct", 2 * c - 1))[i] if c else (("v_lm", 1), ("a_eG", 1))[i]), 2 + i)
                        w = (NQKV + 4 * i) * P
                        mm(bk[:, :], zT[:, cs], W["Wqkvz"][:, w:w + 4 * P], start=True, stop=True
                           ).then_inc(*s["p_z"].up)
                    for i in range(2):
                        bk = after("a_ss", 8 * c + 4 * i + 4, 4 + i)
                        for kh in range(2):
                            rhs = qkT[:, 2 * i + kh:2 * i + kh + HK + 1:HK, cs]
                            last = mm(bk[:, kh * 2 * P:(kh + 1) * 2 * P], qkT[:, HK + 2 * i + kh, cs], rhs,
                                      start=True, stop=True)
                        last.then_inc(*s["p_kk"].up)
                    for half in range(2):
                        pe.wait_ge(*s["g_gm"].at(b, 4 * c + 2 * half + 2))
                        for i, (tri, mask) in enumerate((("upto", "below"), ("after", "notabove"))):
                            if half:
                                bk = after("a_d", 4 * c + i + 1, (0, 7)[i])
                            elif c:
                                bk = after(*(("v_o", 2 * c), ("v_h", c))[i], (0, 7)[i])
                            else:
                                bk = after(*(("v_wfT", 1), ("v_x1", 1))[i], (0, 7)[i])
                            mm(bk[:, :], W[tri][:], GM[:, i, :], start=True, stop=False)
                            mk = W[mask][:].unsqueeze(1).broadcast_to((P, 4, P))
                            last = mm(bk[:, :], W["identb"][:], mk, start=False, stop=True)
                            last.then_inc(*s["p_d"].up)

                def four(bk, half, lhs, rhs, transpose=False):
                    for j in range(4):
                        c4 = slice(j * P, (j + 1) * P)
                        last = tr(bk[:, c4], lhs[:, c4]) if transpose else \
                            mm(bk[:, c4], lhs[:, c4], rhs[:, c4], start=True, stop=True)
                    last.then_inc(*s[f"p_inv{half}"].up)

                def inv(c, half, st):
                    A, V = f"a_inv{half}", f"v_inv{half}"
                    a0, v0 = INV_A * c, INV_V * c
                    ba_, bb, bc = ((0, 1, 4), (2, 3, 5))[half]
                    t = {k: v[half] for k, v in T.items()}
                    wa = lambda n: need(A, a0 + n)
                    wv = lambda n: need(V, v0 + n)
                    if st == 0:
                        pe.wait_ge(*s["v_N"].at(b, 8 * c + 4 * half + 4))
                        four(after(*((("a_d", 4 * c + 3) if half == 0 else ("a_sz", 2 * c + 1))), ba_), half, N_[half], None, True)
                    elif st == 2:
                        wv(2)
                        pe.wait_ge(*s[f"g_inv{half}"].at(b, 4 * c + 1))
                        four(after(*(("a_vb", 8 * c + 8) if half == 0 else ("a_sz", 2 * c + 2)), bb), half, t["M"], t["MT"])
                        four(after("v_qkd", 2 * c + half + 1, bc), half, t["MT"], t["M"])
                    elif st == 3:
                        wv(3); wa(2)
                        four(after(A, a0 + 1, ba_), half, t["MT"], t["X"])
                        four(after(V, v0 + 3, bb), half, t["M2"], t["MT"])
                        four(after(A, a0 + 2, bc), half, t["MT"], t["M2"])
                    elif st == 4:
                        wv(5); wa(3)
                        four(after(V, v0 + 4, ba_), half, t["MT"], t["X"])
                        four(after(A, a0 + 3, bc), half, t["M2"], t["MT"])
                    elif st == 5:
                        wv(6); wa(4)
                        four(after(V, v0 + 6, ba_), half, t["MT"], t["X"])
                    elif st == 6:
                        wv(7)
                        four(after(V, v0 + 5, bb), half, t["X"], None, True)
                    elif st in (7, 10):
                        wa(5 if st == 7 else 7)
                        pe.wait_ge(*s[f"g_inv{half}"].at(b, 4 * c + (2 if st == 7 else 3)))
                        four(after(*((V, v0 + 7) if st == 7 else (A, a0 + 6)), ba_), half,
                             t["L32" if st == 7 else "L64"], t["X"])
                    elif st in (8, 11):
                        wa(6 if st == 8 else 8)
                        four(after(*((A, a0 + 4) if st == 8 else (V, v0 + 8)), bc), half, t["TT"], t["M2"])
                    elif st in (9, 12):
                        wv(8 if st == 9 else 9)
                        four(after(A, a0 + (5 if st == 9 else 7), bb), half, t["X"], None, True)
                    elif st == 13:
                        wa(9)
                        pe.wait_ge(*s[f"g_inv{half}"].at(b, 4 * c + 4))
                        four(after(A, a0 + 8, ba_), half, t["L128"], t["X"])
                    elif st == 14:
                        wa(10)
                        four(after(V, v0 + 9, bc), half, t["M2"], t["TT"])

                def state(c):
                    cs = slice(c * P, (c + 1) * P)
                    if c:
                        pe.wait_ge(*s["v_S"].at(b, 8 * c))
                        for i in range(2):
                            bk = after("a_inv0", INV_A * (c + 1) - i, (0, 1)[i])
                            for kh in range(2):
                                last = mm(bk[:, kh * 2 * P:(kh + 1) * 2 * P], qkT[:, HK + 2 * i + kh, cs],
                                          State[:, 4 * i + 2 * kh:4 * i + 2 * kh + 2, :], start=True, stop=True)
                            last.then_inc(*s["p_w"].up)
                        for i in range(2):
                            bk = after("a_inv1", INV_A * (c + 1) - i, (2, 3)[i])
                            for kh in range(2):
                                last = mm(bk[:, kh * 2 * P:(kh + 1) * 2 * P], qkT[:, 2 * i + kh, cs],
                                          State[:, 4 * i + 2 * kh:4 * i + 2 * kh + 2, :], start=True, stop=True)
                            last.then_inc(*s["p_o1"].up)
                    rhs = R if c else vb
                    pe.wait_ge(*s["a_vb"].at(b, 8 * c + 8))
                    for i in range(2):
                        if c:
                            pe.wait_ge(*s["v_R"].at(b, 8 * (c - 1) + 4 * i + 4))
                        need(f"v_inv{i}", INV_V * (c + 1))
                        bk = after(f"v_inv{i}", INV_V * (c + 1), (4, 5)[i])
                        for j in range(4):
                            last = mm(bk[:, j * P:(j + 1) * P], T["TT"][i][:, j * P:(j + 1) * P], rhs[:, 4 * i + j, :],
                                      start=True, stop=True)
                        last.then_inc(*s["p_dl"].up)
                    for i in range(2):
                        pe.wait_ge(*s["a_dl"].at(b, 2 * c + i + 1))
                        pe.wait_ge(*s["v_qkd"].at(b, 2 * c + i + 1))
                        if i == 0:
                            bk = after("v_fo", 8 * c + 8, 6)
                        else:
                            bk = after(*(("v_R", 8 * c - 4) if c else ("a_inv0", INV_A)), 0)
                        for j in range(4):
                            last = mm(bk[:, j * P:(j + 1) * P], QKD[:, 4 * i + j, :], dl[:, 4 * i + j, :],
                                      start=True, stop=True)
                        last.then_inc(*s["p_o2"].up)
                    if c < NT - 1:
                        for i in range(2):
                            pe.wait_ge(*s["v_dls"].at(b, 8 * c + 4 * i + 4))
                            if c:
                                bk = after(*(("v_R", 8 * c), ("a_o1", 8 * c - 4))[i], (1, 2)[i])
                            else:
                                bk = after(*(("a_inv0", INV_A - 1), ("a_inv1", INV_A))[i], (1, 2)[i])
                            for kh in range(2):
                                last = mm(bk[:, kh * 2 * P:(kh + 1) * 2 * P], ktok[:, 2 * i + kh, :],
                                          DLS[:, 4 * i + 2 * kh:4 * i + 2 * kh + 2, :], start=True, stop=True)
                            last.then_inc(*s["p_s"].up)
                    for i in range(2):
                        pe.wait_ge(*s["v_core"].at(b, 8 * c + 4 * i + 4))
                        if i == 0:
                            bk = after(*(("a_o1", 8 * c) if c else ("a_inv1", INV_A - 1)), 3)
                        else:
                            bk = after(*(("v_dls", 8 * c + 4) if c < NT - 1 else ("a_dl", 2 * c + 1)), 4)
                        for j in range(4):
                            last = tr(bk[:, j * P:(j + 1) * P], core[:, 4 * i + j, :])
                        last.then_inc(*s["p_ct"].up)
                    pe.wait_ge(*s["a_ct"].at(b, 2 * c + 2))
                    bk = after("a_gh", 8 * c + 8, 7)
                    for h in range(HV):
                        last = mm(bk[:, 0:P], coreT[:, h, :], W["Wout"][:, h, :], start=(h == 0), stop=(h == HV - 1))
                    last.then_inc(*s["p_wout"].up)

                def ffn_out(f):
                    e, k = f // FC, f % FC
                    pe.wait_ge(*s["a_gh"].at(b, f + 1))
                    if k == 0:
                        need(*(("v_fo", 4 * e) if e % 2 else ("a_vb", 4 * e + 4)))
                    for t in range(NT):
                        last = mm(bank[6][:, t * P:(t + 1) * P], GH[:, f % 2, t * P:(t + 1) * P],
                                  wring[:, e % 2, FC * P + k * D:FC * P + (k + 1) * D],
                                  start=(k == 0 and t == 0), stop=(k == FC - 1), skip_group_check=True)
                    last.then_inc(*s["p_fo"].up)

                def ffn(f):
                    bk = after(*(("a_gh", f) if f % 8 else ("a_d", f // 2 + 4)), 7)
                    e, k = f // FC, f % FC
                    if k == 0:
                        pe.wait_ge(*s[f"d_w{e % 2}"].at(b, 16 * (e // 2 + 1)))
                    mm(bk[:, :], wring[:, e % 2, k * P:(k + 1) * P], xn1T, start=True, stop=True
                       ).then_inc(*s["p_fh"].up)
                    if f % FC:
                        ffn_out(f - 1)
                    if f % FC == FC - 1:
                        ffn_out(f)

                def hidden():
                    bk = after("v_o", 2 * NT, 0)
                    for t in range(NT):
                        pe.wait_ge(*s["v_h2"].at(b, t + 1))
                        last = tr(bk[:, t * P:(t + 1) * P], hbuf[:, t, :])
                    last.then_inc(*s["p_hT"].up)
                    pe.wait_ge(*s["v_hT"].at(b, 1))
                    bk = after("v_R", 8 * (NT - 1), 1)
                    for t in range(NT):
                        last = mm(bk[:, t * E1:(t + 1) * E1], hT[:, t * P:(t + 1) * P], W["r1"][:], start=True, stop=True)
                    last.then_inc(*s["p_r1"].up)
                    need("v_h", NT)
                    for t in range(NT):
                        mm(bank[7][:, t * P:(t + 1) * P], wfT[:, t * P:(t + 1) * P], W["b2"][:], start=(t == 0),
                           stop=False, skip_group_check=True)
                    pe.wait_ge(*s["v_w1r"].at(b, 1))
                    bk = after("v_hT", 1, 0)
                    for t in range(NT):
                        last = tr(bk[0:E1, t * P:(t + 1) * P], wr[:, t, :])
                    last.then_inc(*s["p_w1T"].up)

                def down1(p):
                    pe.wait_ge(*s["v_hid1"].at(b, 2 * p + 2))
                    for t in range(NT):
                        last = mm(bank[7][:, t * P:(t + 1) * P], HID1[:, p % 2, t * P:(t + 1) * P], W["de1"][:, p, :],
                                  start=False, stop=(p == PR1 - 1), skip_group_check=True)
                    last.then_inc(*s["p_down1"].up)

                def moe1(p):
                    bk = after(*((("v_lm1", 1), ("a_o1", 8 * (NT - 1) - 4))[p] if p < 2 else ("a_sg1", p - 1)), 1 + p % 2)
                    mm(bk[:, :], W["ge1"][:, p, :], hT, start=True, stop=True).then_inc(*s["p_gate1"].up)
                    bk = after(*((("a_ct", 2 * NT - 1), ("a_dl", 2 * NT))[p] if p < 2 else ("v_hid1", 2 * p - 3)), 3 + 2 * (p % 2))
                    mm(bk[:, :], W["ue1"][:, p, :], hT, start=True, stop=True).then_inc(*s["p_up1"].up)
                    if p == 0:
                        pe.wait_ge(*s["v_w96b"].at(b, 1))
                    bk = after(*((("a_ct", 2 * NT), ("v_o", 2 * NT - 1))[p] if p < 2 else ("v_hid1", 2 * p - 2)), 4 + 2 * (p % 2))
                    mm(bk[:, :], W["sel1"][:, p, :], W96b[:, :], start=True, stop=True).then_inc(*s["p_wb1"].up)
                    if p:
                        down1(p - 1)

                steps = {"qkv": qkv, "chunk": chunk, "inv": inv, "ffn": ffn, "state": state, "hidden": hidden, "moe1": moe1, "moe1_last": lambda: down1(PR1 - 1)}
                for step in L1:
                    steps[step[0]](*step[1:])

        @block.scalar
        def _(act):
            fn = nc.scalar.activation

            act.wait_ge(s["weights_a"].sem, 16 * EARLY)
            act.wait_ge(s["weights_b"].sem, 16 * (len(WEIGHTS) - EARLY))
            fn(neg_a[:, :], W["alog"][:], ACT.Exp).then_inc(s["setup_a"].sem, 1)
            act.wait_ge(s["setup_v"].sem, 2)
            with act.Fori(0, LOOPS) as b:
                act.wait_ge(*s["out_ready"].at(b, 0))
                act.wait_ge(*s["p_xnT"].at(b, 1))
                fn(xnT, bank[0][:, :], ACT.Copy).then_inc(*s["a_xnT"].up)
                act.wait_ge(*s["v_lat"].at(b, 1))
                fn(sc0.rearrange("p a b -> p (a b)"), bank[3][:, 128:256], ACT.Exp, scale=-1.0).then_inc(*s["a_lexp"].up)
                act.wait_ge(*s["p_v"].at(b, 1))
                act.wait_ge(*s["g_init"].at(b, 3))
                fn(V32[:, :, :, 0:HD], bank[5][:, :].rearrange("p (t h d) -> p t h d", t=NT, h=NH), ACT.Copy
                   ).then_inc(*s["a_v"].up)

                def moe0(p):
                    act.wait_ge(*s["p_gate"].at(b, p + 1))
                    if p >= 2:
                        act.wait_ge(*s["v_t"].at(b, p - 1))
                    fn(SG[:, p % 2, :], bank[1 + p % 2][:, :], ACT.Silu).then_inc(*s["a_sg"].up)

                def expo(g, i):
                    n = 12 * g + i
                    act.wait_ge(*s["p_score"].at(b, n + 1))
                    if g >= 2 and i == 0:
                        act.wait_ge(*s["p_o"].at(b, g - 1))
                    k, w = i % 6, 512 if i % 6 < 4 else 256
                    slot, col = 10 * (g % 2) + 5 * (i // 6) + min(k, 4), 256 * (k == 5)
                    fn(PT[:, slot, col:col + w], bank[1 + n % 5][:, 0:w], ACT.Exp).then_inc(*s["a_p"].up)

                nothing = lambda *a: None
                steps = {"moe0": moe0, "exp": expo}
                for step in L0:
                    steps.get(step[0], nothing)(*step[1:])

                act.wait_ge(*s["v_x1"].at(b, 1))
                act.wait_ge(*s["p_xn1T"].at(b, 1))
                fn(xn1T, bank[0][:, :], ACT.Copy).then_inc(*s["a_xn1T"].up)
                act.wait_ge(*s["p_ba"].at(b, 1))
                fn(ba, bank[2][:, 0:64].rearrange("p (t n) -> p t n", t=NT), ACT.Exp, scale=-1.0).then_inc(*s["a_eb"].up)
                act.wait_ge(*s["v_ab"].at(b, 1))
                fn(sp, sp, ACT.Exp, scale=-1.0).then_inc(*s["a_eab"].up)
                act.wait_ge(*s["v_lm"].at(b, 1))
                fn(lf, lf, ACT.Exp).then_inc(*s["a_fe"].up)
                act.wait_ge(*s["a_eab"].at(b, 1))
                fn(sp, sp, ACT.Ln, bias=1.0).then_inc(*s["a_sp"].up)

                def qkv(m):
                    if m < NQKV:
                        act.wait_ge(*s["p_qkv"].at(b, m + 1))
                        if m >= 3:
                            act.wait_ge(*s["a_qkv"].at(b, m - 2))
                        fn(CV[:, m % 3, :], bank[4 + m % 3][:, :], ACT.Copy, scale=W["convw"][:, m, 3:4]
                           ).then_inc(*s["a_cv"].up)
                    if m >= 1:
                        act.wait_ge(*s["v_cv"].at(b, m))
                        dst = qkT[:, m - 1, :] if m - 1 < 2 * HK else vT[:, m - 1 - 2 * HK, :]
                        fn(dst, CV[:, (m - 1) % 3, :], ACT.Silu).then_inc(*s["a_qkv"].up)
                    if m == 4:
                        act.wait_ge(*s["p_gc"].at(b, 1))
                        fn(eG.rearrange("p a b -> p (a b)"), bank[3][:, 0:96], ACT.Exp).then_inc(*s["a_eG"].up)

                def chunk(c):
                    act.wait_ge(*s["p_kt"].at(b, c + 1))
                    if c:
                        act.wait_ge(*s["p_s"].at(b, 2 * c))
                        act.wait_ge(*s["p_ct"].at(b, 2 * c))
                        act.wait_ge(*s["v_core"].at(b, 8 * c))
                        act.wait_ge(*s["a_so"].at(b, 8 * c))
                    fn(ktok.rearrange("p a b -> p (a b)"), bank[4][:, :], ACT.Copy).then_inc(*s["a_kt"].up)
                    for i in range(2):
                        if i:
                            act.wait_ge(*s["p_qt"].at(b, c + 1))
                        for h in range(HK):
                            n = 4 * i + h
                            fn(junk[:, n, :], bank[4 + i][:, h * P:(h + 1) * P], ACT.Square, accum_out=ss8[:, n:n + 1]
                               ).then_inc(*s["a_ss"].up)
                    for half in range(2):
                        for i in range(2):
                            n = 4 * c + 2 * half + i
                            act.wait_ge(*s["p_d"].at(b, n + 1))
                            if i == 1 and half == 1:
                                act.wait_ge(*s["v_qkd"].at(b, 2 * c + 1))
                            elif i == 1 and c:
                                act.wait_ge(*s["v_qkd"].at(b, 2 * c))
                            fn((DL[half], DU)[i], bank[(0, 7)[i]][:, :], ACT.Exp).then_inc(*s["a_d"].up)
                    for i in range(2):
                        act.wait_ge(*s["p_z"].at(b, 2 * c + i + 1))
                        fn(sz.rearrange("p a b -> p (a b)")[:, i * 512:(i + 1) * 512], bank[2 + i][:, :], ACT.Silu
                           ).then_inc(*s["a_sz"].up)
                    act.wait_ge(*s["v_sc"].at(b, c + 1))
                    if c:
                        act.wait_ge(*s["p_dl"].at(b, 2 * c))
                    for i in range(2):
                        act.wait_ge(*s["p_vt"].at(b, 2 * c + i + 1))
                        for j in range(4):
                            h = 4 * i + j
                            fn(vb[:, h, :], bank[(6, 1)[i]][:, j * P:(j + 1) * P], ACT.Copy, scale=rkb[:, h:h + 1]
                               ).then_inc(*s["a_vb"].up)

                def inv(c, half, st):
                    t = {k: v[half] for k, v in T.items()}
                    ba_, bb, bc = ((0, 1, 4), (2, 3, 5))[half]
                    p0, a0 = INV_P * c, INV_A * c
                    todo = {0: (1, "NT", ba_), 2: (3, "M2", bc), 3: (6, "M2", bc), 4: (8, "MT", bc),
                            6: (10, "TT", bb), 7: (11, "M2", ba_), 9: (13, "TT", bb), 10: (14, "M2", ba_),
                            12: (16, "TT", bb), 13: (17, "M2", ba_)}
                    if st in todo:
                        n, dst, i = todo[st]
                        act.wait_ge(*s[f"p_inv{half}"].at(b, p0 + n))
                        if st == 0 and c:
                            act.wait_ge(*s[f"g_inv{half}"].at(b, 4 * c))
                        if st == 6:
                            act.wait_ge(*s[f"g_inv{half}"].at(b, 4 * c + 4))
                        fn(t[dst], bank[i][:, :], ACT.Copy).then_inc(*s[f"a_inv{half}"].up)

                def state(c):
                    if c:
                        for i in range(2):
                            act.wait_ge(*s["p_o1"].at(b, 2 * (c - 1) + i + 1))
                            for j in range(4):
                                h = 4 * i + j
                                fn(o1s[:, h, :], bank[(2, 3)[i]][:, j * P:(j + 1) * P], ACT.Copy,
                                   scale=eG[:, 0, c * HV + h:c * HV + h + 1]).then_inc(*s["a_o1"].up)
                    for i in range(2):
                        act.wait_ge(*s["p_dl"].at(b, 2 * c + i + 1))
                        fn(dl[:, 4 * i:4 * i + 4, :].rearrange("p a b -> p (a b)"), bank[(4, 5)[i]][:, :], ACT.Copy
                           ).then_inc(*s["a_dl"].up)
                    if c:
                        act.wait_ge(*s["p_wout"].at(b, c))
                    for i in range(2):
                        act.wait_ge(*s["v_o"].at(b, 2 * c + i + 1))
                        for j in range(4):
                            h = 4 * i + j
                            fn(coreT[:, h, :], oo[:, h, :], ACT.Square, accum_out=so8[:, h:h + 1]
                               ).then_inc(*s["a_so"].up)
                    act.wait_ge(*s["a_so"].at(b, 8 * c + 8))
                    for i in range(2):
                        act.wait_ge(*s["p_ct"].at(b, 2 * c + i + 1))
                        fn(coreT[:, 4 * i:4 * i + 4, :].rearrange("p a b -> p (a b)"), bank[(3, 4)[i]][:, :], ACT.Copy
                           ).then_inc(*s["a_ct"].up)

                def ffn(f):
                    act.wait_ge(*s["p_fh"].at(b, f + 1))
                    if f >= 2:
                        act.wait_ge(*s["p_fo"].at(b, f - 1))
                    fn(GH[:, f % 2, :], bank[7][:, :], ACT.Gelu_apprx_tanh, bias=W["b1"][:, f:f + 1]
                       ).then_inc(*s["a_gh"].up)

                def hidden():
                    act.wait_ge(*s["v_lm1"].at(b, 1))
                    fn(lf, lf, ACT.Exp).then_inc(*s["a_fe1"].up)

                def moe1(p):
                    act.wait_ge(*s["p_gate1"].at(b, p + 1))
                    if p >= 2:
                        act.wait_ge(*s["v_hid1"].at(b, 2 * (p - 2) + 1))
                    fn(SG1[:, p % 2, :], bank[1 + p % 2][:, :], ACT.Silu).then_inc(*s["a_sg1"].up)

                steps = {"qkv": qkv, "chunk": chunk, "inv": inv, "state": state, "ffn": ffn, "hidden": hidden,
                         "moe1": moe1}
                for step in L1:
                    steps.get(step[0], nothing)(*step[1:])
                act.wait_ge(*s["out_ready"].at(b, 1))
                act.dma_start(out_v[bass.ds(b, 1)].rearrange("a p t d -> p (a t) d"), facc).then_inc(*s["out_dma"].up16)
                act.wait_ge(*s["out_dma"].at(b, 16))

        @block.gpsimd
        def _(pool):
            tt = nc.gpsimd.tensor_tensor
            pool.wait_ge(s["weights_b"].sem, 16 * (len(WEIGHTS) - EARLY))
            pool.wait_ge(s["setup_v"].sem, 2)

            def flat(a):
                return a
            with pool.Fori(0, LOOPS) as b:
                wait_alone(pool, *s["out_dma"].at(b, 0))
                nc.gpsimd.memset(V32, 0.0).then_inc(*s["g_init"].up)
                nc.gpsimd.memset(KS, 1.0).then_inc(*s["g_init"].up)
                wait_alone(pool, *s["g_init"].at(b, 1))
                nc.gpsimd.memset(V32[:, :, :, HD:HD + 1], 1.0).then_inc(*s["g_init"].up)
                pool.wait_ge(*s["v_var"].at(b, 1))
                tt(rstd[:, :], var4[:, :], nhalf[:, 0:NT], ALU.pow).then_inc(*s["g_rstd"].up)
                pool.wait_ge(*s["v_lvar"].at(b, 1))
                tt(rstd2, var42, nhalf[:, 0:NT], ALU.pow).then_inc(*s["g_lrstd"].up)
                pool.wait_ge(*s["v_var1"].at(b, 1))
                tt(rstd[:, :], var4[:, :], nhalf[:, 0:NT], ALU.pow).then_inc(*s["g_rstd1"].up)
                pool.wait_ge(*s["v_ms1"].at(b, 1))
                tt(rz, ssq, nhalf[:, 0:NT], ALU.pow).then_inc(*s["g_rz"].up)

                def chunk(c):
                    if c == 0:
                        pool.wait_ge(*s["v_g"].at(b, 1))
                        pool.wait_ge(*s["a_qkv"].at(b, NQKV))
                    for half in range(2):
                        if c or half:
                            pool.wait_ge(*s["p_d"].at(b, 4 * c + 2 * half))
                        gb = gg[:, c, 4 * half:4 * half + 4].unsqueeze(2).broadcast_to((P, 4, P))
                        for i, tri in enumerate(("after", "upto")):
                            m = W[tri][:].unsqueeze(1).broadcast_to((P, 4, P))
                            tt(GM[:, i, :].rearrange("p (a b) -> p a b", a=4), gb, m, ALU.mult).then_inc(*s["g_gm"].up)
                    pool.wait_ge(*s["v_sse"].at(b, c + 1))
                    tt(rr8, ss8, nhalf[:, 0:8], ALU.pow).then_inc(*s["g_rr"].up)

                def inv(c, half, st):
                    t = {k: v[half] for k, v in T.items()}
                    four = lambda a: a.rearrange("p (a b) -> p a b", a=4)
                    mask = lambda i: W["blk"][:, i, :].unsqueeze(1).broadcast_to((P, 4, P))
                    if st == 0:
                        pool.wait_ge(*s["v_N"].at(b, 8 * c + 4 * half + 4))
                        if c:
                            pool.wait_ge(*s[f"p_inv{half}"].at(b, INV_P * c))
                        tt(four(t["M"]), four(N_[half]), mask(0), ALU.mult).then_inc(*s[f"g_inv{half}"].up)
                    if st == 1:
                        pool.wait_ge(*s[f"a_inv{half}"].at(b, INV_A * c + 1))
                        for i, n in enumerate(("L32", "L64", "L128")):
                            tt(four(t[n]), four(t["NT"]), mask(1 + i), ALU.mult).then_inc(*s[f"g_inv{half}"].up)

                def state(c):
                    pool.wait_ge(*s["v_sr"].at(b, c + 1))
                    tt(rc8, so8, nhalf[:, 0:8], ALU.pow).then_inc(*s["g_rc"].up)

                def hidden():
                    pool.wait_ge(*s["v_ms2"].at(b, 1))
                    tt(rz, ssq, nhalf[:, 0:NT], ALU.pow).then_inc(*s["g_rz2"].up)

                steps = {"chunk": chunk, "inv": inv, "state": state, "hidden": hidden}
                for step in L1:
                    steps.get(step[0], lambda *a: None)(*step[1:])

        @block.vector
        def _(dve):
            v = nc.vector
            for buf, value in ((W96, 0.0), (W96b, 0.0), (nhalf, -0.5), (top4, PAD), (top2, PAD),
                               (tmp36, PAD), (pad8, PAD)):
                v.memset(buf[:], value)
            v.memset(junk[:], 0.0).then_inc(s["setup_v"].sem, 1)
            dve.wait_ge(s["setup_v"].sem, 1)
            dve.wait_ge(s["weights_a"].sem, 16 * EARLY)
            dve.wait_ge(s["weights_b"].sem, 16 * (len(WEIGHTS) - EARLY))
            dve.wait_ge(s["setup_a"].sem, 1)
            v.tensor_scalar(neg_a[:, :], neg_a[:, :], -1.0, None, ALU.mult)
            v.tensor_scalar(W["ln1"][:], W["ln1"][:], 1.0, None, ALU.add)
            v.tensor_scalar(W["ln2"][:], W["ln2"][:], 1.0, None, ALU.add)
            v.tensor_scalar(W["Wout"][:], W["Wout"][:], W["gnw"][:, 0:1], None, ALU.mult).then_inc(s["setup_v"].sem, 1)
            dve.wait_ge(s["setup_v"].sem, 2)
            with dve.Fori(0, LOOPS) as b:
                def link(ins, alone=False):
                    ins.then_inc(*s["v_link"].up)
                    if alone:
                        wait_alone(dve, *s["v_link"].at(b, s["v_link"].n))
                    else:
                        dve.wait_ge(*s["v_link"].at(b, s["v_link"].n))

                def norm_stats(src, st, m, out4, eps):
                    for t in range(NT):
                        last = v.bn_stats(st[:, t, :], src[:, t, :])
                    link(last, alone=True)
                    for t in range(NT):
                        last = v.bn_aggr(m[:, t, :], st[:, t, :])
                    link(last)
                    return v.tensor_scalar(out4, m[:, :, 1], eps, None, ALU.add)

                def split3(src, rest, dst):
                    link(v.tensor_copy(dst[:, 0, :], src))
                    link(v.tensor_tensor(rest, src, dst[:, 0, :], ALU.subtract))
                    link(v.tensor_copy(dst[:, 1, :], rest))
                    return v.tensor_tensor(dst[:, 2, :], rest, dst[:, 1, :], ALU.subtract)

                def split_rows(src, rest, mid, dst, k):
                    link(v.tensor_copy(dst[0:k, :], src))
                    link(v.tensor_tensor(rest, src, dst[0:k, :], ALU.subtract))
                    v.tensor_copy(dst[32:32 + k, :], rest)
                    link(v.tensor_copy(mid, rest))
                    return v.tensor_tensor(dst[64:64 + k, :], rest, mid, ALU.subtract)

                def pick(src, k, topk, padded, n, res):
                    for t in range(NT):
                        last = v.max(top[:, t, :], padded[:, t, 0:n])
                    link(last)
                    link(v.tensor_copy(topk[:, :, 0:k], top[:, :, 0:k]), alone=True)
                    for t in range(NT):
                        last = v.match_replace(res[:, t, :], topk[:, t, :], padded[:, t, :], 1.0e30)
                    link(last)
                    link(v.tensor_tensor(res[:, :, 0:n], res[:, :, 0:n], padded[:, :, 0:n], ALU.not_equal))

                def per_tile(a):
                    return a.unsqueeze(2)

                dve.wait_ge(*s["out_dma"].at(b, 0))
                dve.wait_ge(*s["x_in"].at(b, 16))
                norm_stats(x, stats, mv, var4[:, :], EPS0).then_inc(*s["v_var"].up)
                dve.wait_ge(*s["g_rstd"].at(b, 1))
                for t in range(NT):
                    v.tensor_scalar(xn[:, t, :], x[:, t, :], mv[:, t, 0:1], rstd[:, t:t + 1], ALU.subtract, ALU.mult
                                    ).then_inc(*s["v_xn"].up)
                dve.wait_ge(*s["p_q"].at(b, 1))
                v.tensor_tensor(qf, bank[1][:, :], W["cosq"][:], ALU.mult)
                link(v.tensor_tensor(qf2, bank[2][:, :], W["sinq"][:], ALU.mult))
                v.tensor_tensor(qf, qf, qf2, ALU.add).then_inc(*s["v_q"].up)
                dve.wait_ge(*s["p_lat"].at(b, 1))
                norm_stats(bank[3][:, 0:128].rearrange("p (t n) -> p t n", t=NT), stats2, mv2, var42, EPS0
                           ).then_inc(*s["v_lvar"].up)
                dve.wait_ge(*s["g_lrstd"].at(b, 1))
                for t in range(NT):
                    last = v.tensor_scalar(latn[:, t, :], bank[3][:, t * LAT:(t + 1) * LAT], mv2[:, t, 0:1],
                                           rstd2[:, t:t + 1], ALU.subtract, ALU.mult)
                last.then_inc(*s["v_lat"].up)
                dve.wait_ge(*s["a_lexp"].at(b, 1))
                link(v.tensor_scalar(sc0, sc0, 1.0, None, ALU.add))
                link(v.reciprocal(sc0, sc0))
                v.tensor_tensor(sfc, sc0, W["rb0"][:].unsqueeze(1).broadcast_to((P, NT, E0)), ALU.add
                                ).then_inc(*s["v_lsfc"].up)
                dve.wait_ge(*s["p_latT"].at(b, 1))
                v.tensor_scalar(latT, bank[4][0:LAT, :], W["gam"][:, 0:1], W["bet"][:, 0:1], ALU.mult, ALU.add
                                ).then_inc(*s["v_latT"].up)
                dve.wait_ge(*s["v_q"].at(b, 1))
                split3(qf, qf2, qs3).then_inc(*s["v_qs3"].up)
                dve.wait_ge(*s["p_k"].at(b, 1))
                v.tensor_tensor(kf, bank[1][:, :], W["cosk"][:], ALU.mult)
                link(v.tensor_tensor(kf2, bank[2][:, :], W["sink"][:], ALU.mult))
                v.tensor_tensor(kf, kf, kf2, ALU.add).then_inc(*s["v_k"].up)
                dve.wait_ge(*s["v_k"].at(b, 1))
                split3(kf, kf2, ks3).then_inc(*s["v_ks3"].up)

                def s0():
                    wait_alone(dve, *s["v_lsfc"].at(b, 1))
                    for t in range(NT):
                        for g in range(G0):
                            last = v.max(gtop[:, t * G0 + g, :], sfc[:, t, g * 8:(g + 1) * 8])
                    link(last)
                    link(v.tensor_tensor(gs, gtop[:, :, 0], gtop[:, :, 1], ALU.add))
                    g3 = gs.rearrange("p (t g) -> p t g", t=NT)
                    other = g3.unsqueeze(2).broadcast_to((P, NT, G0, G0))
                    own = g3.unsqueeze(3).broadcast_to((P, NT, G0, G0))
                    c0 = cmp0.rearrange("p (t g o) -> p t g o", t=NT, g=G0)
                    c1 = cmp1.rearrange("p (t g o) -> p t g o", t=NT, g=G0)
                    v.tensor_tensor(c0, other, own, ALU.is_ge)
                    link(v.tensor_tensor(c1, other, own, ALU.is_gt))
                    v.tensor_tensor(c0, c0, W["grank"][:, 0], ALU.mult)
                    link(v.tensor_tensor(c1, c1, W["grank"][:, 1], ALU.mult))
                    link(v.tensor_tensor(c0, c0, c1, ALU.add))
                    link(v.tensor_reduce(rank, cmp0.rearrange("p (a o) -> p a o", o=G0), AX, ALU.add))
                    link(v.tensor_scalar(rank, rank, 2.0, None, ALU.is_lt))
                    keep = rank.rearrange("p (t g) -> p t g", t=NT).unsqueeze(3).broadcast_to((P, NT, G0, 8))
                    link(v.tensor_tensor(tmp36[:, :, 0:E0].rearrange("p t (g e) -> p t g e", g=G0),
                                         sfc.rearrange("p t (g e) -> p t g e", g=G0), keep, ALU.mult), alone=True)
                    pick(None, 4, top4, tmp36, E0, mr)
                    link(v.tensor_tensor(w0, sc0, mr[:, :, 0:E0], ALU.mult))
                    link(v.tensor_reduce(wsum, w0, AX, ALU.add))
                    link(v.tensor_scalar(wsum, wsum, 1e-20, None, ALU.add))
                    link(v.reciprocal(wrec, wsum))
                    link(v.tensor_scalar(wrec, wrec, SCALE0, None, ALU.mult))
                    v.tensor_tensor(w0, w0, wrec.unsqueeze(2).broadcast_to((P, NT, E0)), ALU.mult
                                    ).then_inc(*s["v_w0"].up)
                    dve.wait_ge(*s["p_w0T"].at(b, 1))
                    link(v.tensor_copy(wt, bank[4][0:E0, :]))
                    split_rows(wt, wtr, wtm, W96, E0).then_inc(*s["v_w96"].up)

                def moe0(p):
                    dve.wait_ge(*s["a_sg"].at(b, p + 1))
                    dve.wait_ge(*s["p_up"].at(b, p + 1))
                    if p >= 2:
                        dve.wait_ge(*s["p_down"].at(b, p - 1))
                    up = bank[3 + 2 * (p % 2)][:, :]
                    if p == PR0:
                        v.tensor_tensor(HID[:, p % 2, :], SG[:, p % 2, :], up, ALU.mult).then_inc(*s["v_hid"].up)
                        return
                    if p >= 2:
                        dve.wait_ge(*s["v_hid"].at(b, p - 1))
                    v.tensor_tensor(HDT[:, p % 2, :], SG[:, p % 2, :], up, ALU.mult).then_inc(*s["v_t"].up)
                    dve.wait_ge(*s["v_t"].at(b, p + 1))
                    dve.wait_ge(*s["p_wb"].at(b, p + 1))
                    v.tensor_tensor(HID[:, p % 2, :], HDT[:, p % 2, :], bank[4 + 2 * (p % 2)][:, :], ALU.mult
                                    ).then_inc(*s["v_hid"].up)

                def smax(n):
                    w = P * (n % NT + 1)
                    wait_alone(dve, *s["p_max"].at(b, n + 1))
                    v.tensor_tensor_reduce(bank[0][:, 0:w], bank[0][:, 0:w], W["maskq"][:, S - w:S], 1.0, PAD,
                                           ALU.add, ALU.max, mx[:, n:n + 1]).then_inc(*s["v_max"].up)

                def maxrows():
                    dve.wait_ge(*s["v_max"].at(b, NH * NT))
                    v.tensor_scalar(nmx.rearrange("p (r n) -> p r n", r=2), mx.unsqueeze(1).broadcast_to((P, 2, NH * NT)),
                                    -1.0, None, ALU.mult).then_inc(*s["v_nm"].up)
                    dve.wait_ge(*s["p_mT"].at(b, 1))
                    link(v.tensor_copy(nmt, bank[0][0:64, 0:P]))
                    split3(nmt, nmr, nm3).then_inc(*s["v_nm3"].up)

                def pv(g):
                    dve.wait_ge(*s["p_o"].at(b, g + 1))
                    v.tensor_copy(OS[:, g, :], bank[0 if g % 2 else 6][:, :]).then_inc(*s["v_os"].up)

                def attn_out():
                    dve.wait_ge(*s["d_nd"].at(b, 32))
                    link(v.reciprocal(rden, den))
                    v.tensor_tensor(att, num, rden, ALU.mult).then_inc(*s["v_att"].up)
                    dve.wait_ge(*s["p_acc"].at(b, 1))
                    v.tensor_tensor(x1[:, :, :], x[:, :, :], bank[7][:, :].rearrange("p (t d) -> p t d", t=NT), ALU.add
                                    ).then_inc(*s["v_x1"].up)

                nothing = lambda *a: None
                steps = {"s0": s0, "moe0": moe0, "max": smax, "maxrows": maxrows, "pv": pv, "attn_out": attn_out}
                for step in L0:
                    steps.get(step[0], nothing)(*step[1:])

                def ms(src, ready):
                    for t in range(NT):
                        last = v.tensor_tensor_reduce(junk[:, t, :], src[:, t, :], src[:, t, :], 1.0, 0.0, ALU.mult, ALU.add,
                                                      ssq[:, t:t + 1])
                    link(last)
                    v.tensor_scalar(ssq, ssq, 1.0 / D, EPS1, ALU.mult, ALU.add).then_inc(*s[ready].up)

                dve.wait_ge(*s["v_x1"].at(b, 1))
                norm_stats(x1, stats, mv, var4[:, :], EPS0).then_inc(*s["v_var1"].up)
                dve.wait_ge(*s["g_rstd1"].at(b, 1))
                for t in range(NT):
                    v.tensor_scalar(xn1[:, t, :], x1[:, t, :], mv[:, t, 0:1], rstd[:, t:t + 1], ALU.subtract, ALU.mult
                                    ).then_inc(*s["v_xn1"].up)
                dve.wait_ge(*s["v_xn1"].at(b, NT))
                ms(xn1, "v_ms1")
                dve.wait_ge(*s["g_rz"].at(b, 1))
                for t in range(NT):
                    v.tensor_scalar(zz[:, t, :], xn1[:, t, :], rz[:, t:t + 1], None, ALU.mult).then_inc(*s["v_z"].up)
                dve.wait_ge(*s["p_zT"].at(b, 1))
                v.tensor_scalar(zT, bank[1][:, :], W["ln1"][:, 0:1], None, ALU.mult).then_inc(*s["v_zT"].up)
                dve.wait_ge(*s["a_eb"].at(b, 1))
                ps = bank[2][:, 0:64].rearrange("p (t n) -> p t n", t=NT)
                link(v.tensor_tensor(aab, ps[:, :, HV:2 * HV], W["dtb"][:].unsqueeze(1).broadcast_to((P, NT, HV)), ALU.add))
                link(v.tensor_scalar(sp, aab, -1.0, None, ALU.mult))
                v.tensor_tensor(sp, sp, aab, ALU.max).then_inc(*s["v_ab"].up)

                def softmax_shift(ps, src_ready, ready):
                    link(v.tensor_reduce(red4, ps, AX, ALU.max))
                    v.tensor_tensor(lf, ps, red4.unsqueeze(2).broadcast_to((P, NT, EF)), ALU.subtract
                                    ).then_inc(*s[ready].up)

                def softmax_end():
                    link(v.tensor_reduce(red4, lf, AX, ALU.add))
                    link(v.reciprocal(rec4, red4))
                    link(v.tensor_tensor(pad8[:, :, 0:EF], lf, rec4.unsqueeze(2).broadcast_to((P, NT, EF)), ALU.mult),
                         alone=True)
                    pick(None, 2, top2, pad8, EF, mrf)

                softmax_shift(bank[2][:, 64:96].rearrange("p (t n) -> p t n", t=NT), None, "v_lm")
                link(v.tensor_scalar(beta, ba[:, :, 0:HV], 1.0, None, ALU.add))
                v.reciprocal(beta, beta)
                link(v.tensor_scalar(aab, aab, 0.0, None, ALU.max))
                dve.wait_ge(*s["a_sp"].at(b, 1))
                link(v.tensor_tensor(aab, aab, sp, ALU.add))
                v.tensor_tensor(gg, aab, neg_a[:, :].unsqueeze(1).broadcast_to((P, NT, HV)), ALU.mult
                                ).then_inc(*s["v_g"].up)
                dve.wait_ge(*s["a_fe"].at(b, 1))
                softmax_end()
                v.tensor_tensor(wf, pad8[:, :, 0:EF], mrf[:, :, 0:EF], ALU.mult).then_inc(*s["v_wf"].up)

                def qkv(m):
                    if m == NQKV:
                        return
                    ps, cv = bank[4 + m % 3], CV[:, m % 3, :]
                    dve.wait_ge(*s["a_cv"].at(b, m + 1))
                    for k in (1, 2, 3):
                        ins = v.scalar_tensor_tensor(out=cv[:, k:S], in0=ps[:, 0:S - k], scalar=W["convw"][:, m, 3 - k:4 - k],
                                                     in1=cv[:, k:S], op0=ALU.mult, op1=ALU.add)
                        if k < 3:
                            link(ins)
                    ins.then_inc(*s["v_cv"].up)
                    if m == 6:
                        dve.wait_ge(*s["p_wfT"].at(b, 1))
                        v.tensor_copy(wfT, bank[0][0:EF, :]).then_inc(*s["v_wfT"].up)

                def chunk(c):
                    g8 = slice(c * HV, (c + 1) * HV)
                    pairs = lambda a: a.unsqueeze(2).broadcast_to((P, HK, 2))
                    v8 = lambda a: a.rearrange("p (k r) -> p k r", r=2)
                    dve.wait_ge(*s["a_ss"].at(b, 8 * c + 8))
                    if c:
                        dve.wait_ge(*s["v_core"].at(b, 8 * c))
                    v.tensor_scalar(ss8, ss8, EPS1, None, ALU.add).then_inc(*s["v_sse"].up)
                    dve.wait_ge(*s["v_sse"].at(b, c + 1))
                    v.reciprocal(rk2, ss8[:, 0:HK])
                    link(v.reciprocal(rq2, ss8[:, HK:8]))
                    bt = v8(beta[:, c, :])
                    link(v.scalar_tensor_tensor(out=v8(nlam), in0=pairs(rk2), scalar=-1.0, in1=bt, op0=ALU.mult, op1=ALU.mult))
                    dve.wait_ge(*s["a_eG"].at(b, 1))
                    v.tensor_tensor(s1, nlam, eG[:, 0, g8], ALU.mult)
                    dve.wait_ge(*s["g_rr"].at(b, c + 1))
                    v.tensor_scalar(rqs, rr8[:, HK:8], float(P) ** -0.5, None, ALU.mult)
                    v.tensor_tensor(v8(rkb), pairs(rr8[:, 0:HK]), bt, ALU.mult).then_inc(*s["v_sc"].up)
                    dve.wait_ge(*s["v_sc"].at(b, c + 1))
                    for half in range(2):
                        ps = bank[4 + half][:, :].rearrange("p (k r n) -> p k r n", k=2, r=2)
                        dve.wait_ge(*s["p_kk"].at(b, 2 * c + half + 1))
                        dve.wait_ge(*s["a_d"].at(b, 4 * c + 2 * half + 1))
                        if c:
                            dve.wait_ge(*s[f"g_inv{half}"].at(b, 4 * c))
                        for j in range(4):
                            h = 4 * half + j
                            v.scalar_tensor_tensor(out=N_[half][:, j * P:(j + 1) * P], in0=ps[:, j // 2, 1, :],
                                                   scalar=nlam[:, h:h + 1], in1=DL[half][:, j * P:(j + 1) * P],
                                                   op0=ALU.mult, op1=ALU.mult).then_inc(*s["v_N"].up)
                        dve.wait_ge(*s["a_d"].at(b, 4 * c + 2 * half + 2))
                        if c:
                            dve.wait_ge(*s["p_o2"].at(b, 2 * c))
                        v.tensor_tensor(QKD[:, 4 * half:4 * half + 4, :].rearrange("p (k r) n -> p k r n", k=2),
                                        ps[:, :, 0, :].unsqueeze(2).broadcast_to((P, 2, 2, P)),
                                        DU.rearrange("p (k r n) -> p k r n", k=2, r=2), ALU.mult
                                        ).then_inc(*s["v_qkd"].up)

                def inv(c, half, st):
                    t = {k: u[half] for k, u in T.items()}
                    ba_, bb, bc = ((0, 1, 4), (2, 3, 5))[half]
                    p0, v0 = INV_P * c, INV_V * c
                    four = lambda a: a.rearrange("p (a b) -> p a b", a=4)
                    up = s[f"v_inv{half}"]
                    pw = lambda n: dve.wait_ge(*s[f"p_inv{half}"].at(b, p0 + n))
                    vw = lambda n: dve.wait_ge(*up.at(b, v0 + n))
                    if st == 1:
                        dve.wait_ge(*s[f"g_inv{half}"].at(b, 4 * c + 1))
                        v.tensor_tensor(four(t["X"]), four(t["M"]), W["ident"][:].unsqueeze(1).broadcast_to((P, 4, P)),
                                        ALU.add).then_inc(*up.up)
                        dve.wait_ge(*s[f"a_inv{half}"].at(b, INV_A * c + 1))
                        v.tensor_tensor(four(t["MT"]), four(t["NT"]), W["blk"][:, 0, :].unsqueeze(1).broadcast_to((P, 4, P)),
                                        ALU.mult).then_inc(*up.up)
                    elif st == 2:
                        pw(3)
                        v.tensor_copy(t["MT"], bank[bb][:, :]).then_inc(*up.up)
                    elif st == 3:
                        pw(4); vw(1)
                        v.tensor_tensor(t["X"], t["X"], bank[ba_][:, :], ALU.add).then_inc(*up.up)
                        pw(6)
                        v.tensor_copy(t["MT"], bank[bb][:, :]).then_inc(*up.up)
                    elif st == 4:
                        pw(7); vw(4)
                        v.tensor_tensor(t["X"], t["X"], bank[ba_][:, :], ALU.add).then_inc(*up.up)
                    elif st == 5:
                        pw(9); vw(6)
                        v.tensor_tensor(t["X"], t["X"], bank[ba_][:, :], ALU.add).then_inc(*up.up)
                    elif st in (8, 11):
                        pw(12 if st == 8 else 15); vw(7 if st == 8 else 8)
                        v.tensor_tensor(t["X"], t["X"], bank[bc][:, :], ALU.add).then_inc(*up.up)
                    elif st == 14:
                        pw(18)
                        dve.wait_ge(*s[f"a_inv{half}"].at(b, INV_A * c + 9))
                        v.tensor_tensor(t["TT"], t["TT"], bank[bc][:, :], ALU.add).then_inc(*up.up)

                def state(c):
                    if c:
                        for i in range(2):
                            dve.wait_ge(*s["p_w"].at(b, 2 * (c - 1) + i + 1))
                            if i == 0:
                                dve.wait_ge(*s["a_vb"].at(b, 8 * c + 8))
                                dve.wait_ge(*s["a_so"].at(b, 8 * c))
                            for j in range(4):
                                h = 4 * i + j
                                v.scalar_tensor_tensor(out=R[:, h, :], in0=bank[(0, 1)[i]][:, j * P:(j + 1) * P],
                                                       scalar=s1[:, h:h + 1], in1=vb[:, h, :], op0=ALU.mult, op1=ALU.add
                                                       ).then_inc(*s["v_R"].up)
                    if c < NT - 1:
                        for i in range(2):
                            dve.wait_ge(*s["a_dl"].at(b, 2 * c + i + 1))
                            if c:
                                dve.wait_ge(*s["p_s"].at(b, 2 * c))
                            for j in range(4):
                                h = 4 * i + j
                                v.tensor_scalar(DLS[:, h, :], dl[:, h, :], eG[:, 1, c * HV + h:c * HV + h + 1], None,
                                                ALU.mult).then_inc(*s["v_dls"].up)
                    for i in range(2):
                        dve.wait_ge(*s["p_o2"].at(b, 2 * c + i + 1))
                        dve.wait_ge(*s["p_dl"].at(b, 2 * c + 2))
                        dst = oo[:, 4 * i:4 * i + 4, :].rearrange("p a b -> p (a b)")
                        if c:
                            dve.wait_ge(*s["a_o1"].at(b, 8 * (c - 1) + 4 * i + 4))
                            v.tensor_tensor(dst, o1s[:, 4 * i:4 * i + 4, :].rearrange("p a b -> p (a b)"),
                                            bank[(6, 0)[i]][:, :], ALU.add).then_inc(*s["v_o"].up)
                        else:
                            v.tensor_copy(dst, bank[(6, 0)[i]][:, :]).then_inc(*s["v_o"].up)
                    if c < NT - 1:
                        for i in range(2):
                            dve.wait_ge(*s["p_s"].at(b, 2 * c + i + 1))
                            for j in range(4):
                                h = 4 * i + j
                                ps = bank[(1, 2)[i]][:, j * P:(j + 1) * P]
                                if c:
                                    v.scalar_tensor_tensor(out=State[:, h, :], in0=State[:, h, :],
                                                           scalar=eG[:, 2, c * HV + h:c * HV + h + 1], in1=ps,
                                                           op0=ALU.mult, op1=ALU.add).then_inc(*s["v_S"].up)
                                else:
                                    v.tensor_copy(State[:, h, :], ps).then_inc(*s["v_S"].up)
                    dve.wait_ge(*s["a_so"].at(b, 8 * c + 8))
                    pairs = lambda a: a.unsqueeze(2).broadcast_to((P, HK, 2))
                    v8 = lambda a: a.rearrange("p (k r) -> p k r", r=2)
                    link(v.tensor_tensor(v8(so8), v8(so8), pairs(rq2), ALU.mult))
                    v.tensor_scalar(so8, so8, 1.0 / (P * P), EPS1, ALU.mult, ALU.add).then_inc(*s["v_sr"].up)
                    dve.wait_ge(*s["g_rc"].at(b, c + 1))
                    link(v.tensor_tensor(v8(rc8), v8(rc8), pairs(rqs), ALU.mult))
                    dve.wait_ge(*s["a_sz"].at(b, 2 * c + 2))
                    for h in range(HV):
                        v.scalar_tensor_tensor(out=core[:, h, :], in0=oo[:, h, :], scalar=rc8[:, h:h + 1], in1=sz[:, h, :],
                                               op0=ALU.mult, op1=ALU.mult).then_inc(*s["v_core"].up)
                    dve.wait_ge(*s["p_wout"].at(b, c + 1))
                    v.tensor_tensor(zz[:, c, :], xn1[:, c, :], bank[7][:, 0:P], ALU.add).then_inc(*s["v_h"].up)

                def ffn(f):
                    e = f // FC
                    if f % FC < FC - 1:
                        return
                    dve.wait_ge(*s["p_fo"].at(b, f + 1))
                    for t in range(NT):
                        ps = bank[6][:, t * P:(t + 1) * P]
                        if e == 0:
                            v.tensor_scalar(facc[:, t, :], ps, wf[:, t, 0:1], None, ALU.mult).then_inc(*s["v_fo"].up)
                        else:
                            if t == 0:
                                dve.wait_ge(*s["v_fo"].at(b, 4 * e))
                            v.scalar_tensor_tensor(out=facc[:, t, :], in0=ps, scalar=wf[:, t, e:e + 1],
                                                   in1=facc[:, t, :], op0=ALU.mult, op1=ALU.add).then_inc(*s["v_fo"].up)

                def hidden():
                    dve.wait_ge(*s["v_h"].at(b, NT))
                    dve.wait_ge(*s["v_fo"].at(b, 4 * EF))
                    link(v.tensor_tensor(x1[:, :, :], x1[:, :, :], zz, ALU.add))
                    link(v.tensor_tensor(facc, facc, x1[:, :, :], ALU.add))
                    dve.wait_ge(*s["p_ct"].at(b, 2 * NT))
                    ms(zz, "v_ms2")
                    dve.wait_ge(*s["g_rz2"].at(b, 1))
                    for t in range(NT):
                        v.tensor_scalar(hbuf[:, t, :], zz[:, t, :], rz[:, t:t + 1], None, ALU.mult).then_inc(*s["v_h2"].up)
                    dve.wait_ge(*s["p_hT"].at(b, 1))
                    v.tensor_scalar(hT, bank[0][:, :], W["ln2"][:, 0:1], None, ALU.mult).then_inc(*s["v_hT"].up)
                    dve.wait_ge(*s["p_r1"].at(b, 1))
                    softmax_shift(bank[1][:, 0:NT * E1].rearrange("p (t n) -> p t n", t=NT), None, "v_lm1")
                    dve.wait_ge(*s["a_fe1"].at(b, 1))
                    softmax_end()
                    link(v.tensor_tensor(lf, pad8[:, :, 0:EF], mrf[:, :, 0:EF], ALU.mult))
                    link(v.tensor_reduce(red4, lf, AX, ALU.add))
                    link(v.reciprocal(rec4, red4))
                    v.tensor_tensor(lf, lf, rec4.unsqueeze(2).broadcast_to((P, NT, E1)), ALU.mult
                                    ).then_inc(*s["v_w1r"].up)
                    dve.wait_ge(*s["p_w1T"].at(b, 1))
                    rest, mid = CV[0:E1, 2, :], CV[0:E1, 1, 0:S // 2].bitcast(BF16)
                    link(v.tensor_copy(wt1, bank[0][0:E1, :]))
                    split_rows(wt1, rest, mid, W96b, E1).then_inc(*s["v_w96b"].up)

                def moe1(p):
                    dve.wait_ge(*s["a_sg1"].at(b, p + 1))
                    dve.wait_ge(*s["p_up1"].at(b, p + 1))
                    if p >= 2:
                        dve.wait_ge(*s["p_down1"].at(b, p - 1))
                    if p >= 2:
                        dve.wait_ge(*s["v_hid1"].at(b, 2 * (p - 1)))
                    v.tensor_tensor(HDT1[:, p % 2, :], SG1[:, p % 2, :], bank[3 + 2 * (p % 2)][:, :], ALU.mult
                                    ).then_inc(*s["v_hid1"].up)
                    dve.wait_ge(*s["v_hid1"].at(b, 2 * p + 1))
                    dve.wait_ge(*s["p_wb1"].at(b, p + 1))
                    v.tensor_tensor(HID1[:, p % 2, :], HDT1[:, p % 2, :], bank[4 + 2 * (p % 2)][:, :], ALU.mult
                                    ).then_inc(*s["v_hid1"].up)

                def moe1_last():
                    dve.wait_ge(*s["p_down1"].at(b, PR1))
                    v.tensor_tensor(facc, facc, bank[7][:, :].rearrange("p (t d) -> p t d", t=NT), ALU.add
                                    ).then_inc(*s["out_ready"].up)

                steps = {"qkv": qkv, "chunk": chunk, "inv": inv, "state": state, "ffn": ffn, "hidden": hidden,
                         "moe1": moe1, "moe1_last": moe1_last}
                for step in L1:
                    steps.get(step[0], nothing)(*step[1:])

        for name, g in signals.items():
            sizes[name] = g.n


INV_P, INV_V, INV_A = 18, 10, 10


def constants():
    c = {}
    d = np.arange(P) % HD
    half = HD // 2
    inv = (1.0 / 10000.0 ** (np.arange(half, dtype=np.float32) / half)).astype(np.float32)
    ang = np.arange(S, dtype=np.float32)[None, :] * inv[d % half][:, None]
    sign = np.where(d < half, -1.0, 1.0).astype(np.float32)[:, None]
    cos, sin = np.cos(ang).astype(np.float32), (np.sin(ang) * sign).astype(np.float32)
    scale = np.float32(1.0 / np.sqrt(HD))
    c["cosq"], c["sinq"], c["cosk"], c["sink"] = cos * scale, sin * scale, cos, sin
    i, j = np.arange(P)[:, None], np.arange(P)[None, :]
    c["ident"] = np.eye(P)
    c["identb"] = np.eye(P)
    mq = np.zeros((P, S))
    mq[:, S - P:] = np.where(j > i, NEG, 0.0)
    c["maskq"] = mq
    c["maskt"] = np.where(i > j, NEG, 0.0)
    g, o = np.arange(G0)[:, None], np.arange(G0)[None, :]
    rank = np.stack([(o < g), (o > g)]).astype(np.float32)
    c["grank"] = np.broadcast_to(rank[None, :, None], (P, 2, NT, G0, G0))

    def sel(experts, pairs):
        a = np.zeros((96, pairs, P))
        for e in range(experts):
            for part in range(3):
                a[32 * part + e, e // 2, (e % 2) * 64:(e % 2) * 64 + 64] = 1.0
        return a
    c["sel0"], c["sel1"] = sel(E0, PR0), sel(E1, PR1)
    c["upto"], c["after"], c["ones"] = (i <= j), (i > j), np.ones((P, P))
    c["below"] = np.where(j < i, 0.0, NEG)
    c["notabove"] = np.where(i <= j, 0.0, NEG)
    blk = [(i // 16 == j // 16)]
    for n in (16, 32, 64):
        blk.append((i // (2 * n) == j // (2 * n)) & (i // n != j // n))
    c["blk"] = np.stack(blk, 1)
    return c


def lay_out(a):
    perm = np.arange(D).reshape(NH, 2, HD // 2)[:, ::-1].reshape(D)
    rows = lambda v, n=P: np.broadcast_to(v[None, :], (n, v.shape[0]))
    t = {}
    t["Wq"], t["Wqr"] = a["L0_attn_W_q"], a["L0_attn_W_q"][:, perm]
    t["Wdkv"], t["Wuk"], t["Wukr"] = a["L0_attn_W_dkv"], a["L0_attn_W_uk"], a["L0_attn_W_uk"][:, perm]
    t["Wuv"], t["Wo"] = a["L0_attn_W_uv"], a["L0_attn_W_o"]
    t["gam"], t["bet"] = a["L0_attn_ln_gamma"][:, None], a["L0_attn_ln_beta"][:, None]
    t["rw0"], t["rb0"] = a["L0_ffn_router_weight"].T, rows(a["L0_ffn_router_bias"])
    t["gate0"] = a["L0_ffn_gate_w"].reshape(PR0, P, D).transpose(2, 0, 1)
    t["up0"] = a["L0_ffn_up_w"].reshape(PR0, P, D).transpose(2, 0, 1)
    t["down0"] = a["L0_ffn_down_w"].transpose(0, 2, 1).reshape(PR0, P, D).transpose(1, 0, 2)
    t["sg"], t["su"], t["sd"] = a["L0_ffn_shared_gate_w"].T, a["L0_ffn_shared_up_w"].T, a["L0_ffn_shared_down_w"].T
    t["ln1"], t["ln2"] = a["L1_attn_w_ln1"][:, None], a["L1_attn_w_ln2"][:, None]
    t["Wqkvz"], t["Wba"] = a["L1_attn_W_qkvz"], a["L1_attn_W_ba"]
    t["convw"] = a["L1_attn_conv_w"].reshape(NQKV, P, 4).transpose(1, 0, 2)
    t["dtb"], t["alog"], t["gnw"] = rows(a["L1_attn_dt_bias"]), rows(a["L1_attn_A_log"]), a["L1_attn_gate_norm_w"][:, None]
    t["Wout"] = a["L1_attn_W_out"].reshape(HV, P, D).transpose(1, 0, 2)
    t["r1"] = a["L1_attn_W_router"]
    t["ge1"] = a["L1_attn_W_gate_e"].transpose(1, 0, 2).reshape(D, PR1, P)
    t["ue1"] = a["L1_attn_W_up_e"].transpose(1, 0, 2).reshape(D, PR1, P)
    t["de1"] = a["L1_attn_W_down_e"].reshape(PR1, P, D).transpose(1, 0, 2)
    t["rf"] = a["L1_ffn_w_router"]
    t["b1"] = a["L1_ffn_b1"].reshape(EF * FC, P).T
    t["b2"] = a["L1_ffn_b2"]
    return t


def program(nc):
    x = nc.dram_tensor("in_x", (B, S, D), F32, kind="ExternalInput").ap()
    w = {n: nc.dram_tensor("in_" + n, tuple(shape), dt, kind="ExternalInput").ap() for n, (shape, dt) in WEIGHTS.items()}
    out = nc.dram_tensor("out", (B, S, D), F32, kind="ExternalOutput").ap()
    scratch = (nc.dram_tensor("scrq", (3, P, S), BF16, kind="Internal").ap(),
               nc.dram_tensor("scrk", (3, P, S), BF16, kind="Internal").ap(),
               nc.dram_tensor("scrm", (3, NH * NT, P), BF16, kind="Internal").ap(),
               nc.dram_tensor("scro", (NH, 9, S), F32, kind="Internal").ap())
    w_last = nc.dram_tensor("in_w_last", (EF, P, FC * P + FC * D), F32, kind="ExternalInput").ap()
    return x, w_last, out, w, scratch


def kernel(**inputs):
    import concourse.bacc as bacc
    from concourse.bass_utils import run_bass_kernel_spmd

    per, sizes = {}, {}
    nc = bacc.Bacc("TRN2", target_bir_lowering=False, num_devices=1)
    build(nc, *program(nc), {}, per)
    nc = bacc.Bacc("TRN2", target_bir_lowering=False, num_devices=1)
    build(nc, *program(nc), per, sizes)
    assert per == sizes

    a = {n: np.asarray(v) for n, v in inputs.items()}
    arrays = {"in_x": np.ascontiguousarray(a["L0_attn_x"])}
    w1 = a["L1_ffn_w1"]
    w2 = a["L1_ffn_w2"].reshape(EF, FC, P, D).transpose(0, 2, 1, 3).reshape(EF, P, FC * D)
    arrays["in_w_last"] = np.ascontiguousarray(np.concatenate([w1, w2], axis=2))
    laid = lay_out(a)
    for n, (shape, dt) in WEIGHTS.items():
        if n in laid:
            arrays["in_" + n] = np.ascontiguousarray(laid[n]).reshape(shape)
    for n, v in constants().items():
        arrays["in_" + n] = np.ascontiguousarray(v, dtype=mybir.dt.np(WEIGHTS[n][1]))
    r = run_bass_kernel_spmd(nc, [arrays], core_ids=[0])
    return r.results[0]["out"]
```

```python
from contextlib import ExitStack

import numpy as np

import concourse.bass as bass
from concourse import mybir

F32 = mybir.dt.float32
BF16 = mybir.dt.bfloat16
ALU = mybir.AluOpType
ACT = mybir.ActivationFunctionType
AX = mybir.AxisListType.X

P = 128
LOOPS = 8
B, S, D = 8, 512, 128
NT = S // P
NH, HD = 16, 8
NP = NH // 2
NQ = NH // 4
LAT = 32
E0, I0, G0 = 32, 64, 4
PR0 = E0 * I0 // P
HK, HV = 4, 8
NQKV = 2 * HK + HV
E1, I1 = 8, 64
PR1 = E1 * I1 // P
EF, IF = 8, 512
FC = IF // P
NEG = -1.0e30
PAD = -3.0e38
QSPLIT = (0, 0, 1, 0, 2, 1)
KSPLIT = (0, 1, 0, 2, 0, 1)
KROWS = 6 * HD
MROWS = KROWS + 3
EPS0, EPS1 = 1e-5, 1e-6
SCALE0 = 2.5

WEIGHTS = {
    "Wq": ([D, D], F32), "Wqr": ([D, D], F32), "Wdkv": ([D, LAT], F32), "Wuk": ([LAT, D], F32),
    "Wukr": ([LAT, D], F32), "Wuv": ([LAT, D], F32), "Wo": ([D, D], F32), "gam": ([LAT, 1], F32),
    "bet": ([LAT, 1], F32), "rw0": ([D, E0], F32), "rb0": ([P, E0], F32),
    "cos": ([P, S], F32), "sin": ([P, S], F32),
    "ident": ([P, P], F32), "identb": ([P, P], BF16), "maskq": ([P, S], F32), "maskt": ([P, P], BF16),
    "grank": ([P, 2, NT, G0, G0], F32), "sel0": ([96, PR0, P], BF16),
    "gate0": ([D, PR0, P], F32), "up0": ([D, PR0, P], F32), "down0": ([P, PR0, D], F32),
    "sg": ([D, P], F32), "su": ([D, P], F32), "sd": ([P, D], F32),
    "ln1": ([D, 1], F32), "ln2": ([D, 1], F32), "Wqkvz": ([D, (NQKV + HV) * P], F32), "Wba": ([D, 2 * HV], F32),
    "convw": ([P, NQKV, 4], F32), "dtb": ([P, HV], F32), "alog": ([P, HV], F32), "gnw": ([P, 1], F32),
    "Wout": ([P, HV, D], F32), "r1": ([D, E1], F32), "ge1": ([D, PR1, P], F32), "ue1": ([D, PR1, P], F32),
    "de1": ([P, PR1, D], F32), "sel1": ([96, PR1, P], BF16), "rf": ([D, EF], F32),
    "b1": ([P, EF * FC], F32), "b2": ([EF, D], F32),
    "upto": ([P, P], F32), "after": ([P, P], F32), "ones": ([P, P], F32),
    "below": ([P, P], BF16), "notabove": ([P, P], BF16), "blk": ([P, 4, P], F32), "pick": ([P, 2, 32], F32),
}
MIDDLE = ("gate0", "up0", "down0", "sg", "su", "sd", "sel0", "pick")
LATE = ("Wqkvz", "Wba", "convw", "r1", "ge1", "ue1", "de1", "sel1", "rf", "b1", "b2", "upto", "after", "ones", "below",
        "notabove", "blk")
EARLY = tuple(n for n in WEIGHTS if n not in MIDDLE + LATE)


class Signal:

    def __init__(self, name, sem, per):
        self.name, self.sem, self.per, self.n = name, sem, per, 0

    def at(self, b, n):
        return self.sem, b * self.per + n

    @property
    def up(self):
        self.n += 1
        return self.sem, 1

    @property
    def up16(self):
        self.n += 16
        return self.sem, 16


def schedule_l0():
    order, n = [("gu", 0), ("route",)], 0
    for p in range(1, PR0 + 1):
        order += [("gu", p), ("hid", p - 1), ("max", n), ("max", n + 1)]
        if p > 1:
            order.append(("wbd", p - 2))
        order += [("max", n + 2), ("max", n + 3)]
        n += 4
    order += [("maxrows",), ("hid", PR0), ("wbd", PR0 - 1), ("wbd", PR0)]
    for g in range(NQ):
        order += [("exp", g, i) for i in range(12)]
        if g:
            order.append(("pv", g - 1))
    order += [("pv", NQ - 1), ("nd",), ("attn_out",)]
    return order


TSTEPS = 15


def schedule_l1():
    order, f = [("qkv", m) for m in range(0, NQKV + 2, 2)], 0
    F = ("ffn",)
    for c in range(NT):
        order += [("ck", c), F, ("ckk", c), ("cd", c, 0), ("cd", c, 1), ("cz", c), ("cv", c)]
        for st in range(TSTEPS):
            order += [("inv", c, 0, st), ("inv", c, 1, st)]
            if st in (5, 9):
                order.append(F)
        order += [("sw", c), ("so1", c), F, ("sdl", c), F, ("so2", c), ("ss", c), ("sn1", c), F, F, ("sn2", c), F,
                  ("swo", c)]
    order += [("ffn_last",), ("hidden",)]
    order += [("moe1", p) for p in range(PR1)] + [("moe1_last",)]
    for i, step in enumerate(order):
        if step == F:
            order[i] = ("ffn", f)
            f += 1
    assert f == EF * FC
    return order


def build(nc, x_in, w_last, out, weights, scratch, per, sizes):
    scrq, scrk, scrm = scratch
    x_v = x_in.rearrange("b (t p) d -> b p t d", p=P)
    out_v = out.rearrange("b (t p) d -> b p t d", p=P)
    with ExitStack() as ctx:
        def sb(name, shape, dt=F32):
            return ctx.enter_context(nc.sbuf_tensor(name, shape, dt))

        signals = {}

        def sig(name):
            signals[name] = Signal(name, ctx.enter_context(nc.semaphore(name)), per.get(name, 1))
            return signals[name]

        W = {n: sb("w_" + n, shape, dt) for n, (shape, dt) in WEIGHTS.items()}
        bank = [ctx.enter_context(nc.psum_tensor(f"bank{i}", [P, 512], F32)) for i in range(8)]

        x = sb("x", [P, NT, D])
        x1 = sb("x1", [P, NT, D])
        nhalf = sb("nhalf", [P, 32])
        junk = sb("junk", [P, 8, P])
        ARENA = 27600
        arena = sb("arena", [P, ARENA])
        at = [0]

        def cut(shape, dt=F32, parts=P):
            n = int(np.prod(shape))
            words = n if dt == F32 else n // 2
            a = arena[0:parts, at[0]:at[0] + words]
            at[0] += words
            assert at[0] <= ARENA, at
            if dt != F32:
                a = a.bitcast(dt)
            if len(shape) == 2:
                a = a.rearrange("p (a b) -> p a b", a=shape[0])
            if len(shape) == 3:
                a = a.rearrange("p (a b c) -> p a b c", a=shape[0], b=shape[1])
            return a

        W96 = sb("W96", [96, S], BF16)
        W96b = sb("W96b", [96, S], BF16)
        wring = sb("wring", [P, 2, FC * P + FC * D])
        stats = sb("stats", [P, NT, 6])
        mv = sb("mv", [P, NT, 2])
        var4 = sb("var4", [P, NT])
        rstd = sb("rstd", [P, NT])
        top = sb("top", [P, NT, 8])
        top4 = sb("top4", [P, NT, 8])
        top2 = sb("top2", [P, NT, 8])
        tmp36 = sb("tmp36", [P, NT, E0 + 4])
        pad8 = sb("pad8", [P, NT, EF + 6])
        neg_a = sb("neg_a", [P, HV])
        tick = sb("tick", [P, 96])

        xn = cut([NT, D]); xnT = cut([S]); qf = cut([S]); qf2 = cut([S]); kf = cut([S]); kf2 = cut([S])
        QS = cut([NP, S], BF16); KS = cut([NP, S], BF16); V32 = cut([NT, NH, 32])
        latn = cut([NT, LAT]); latT = cut([S], parts=LAT); stats2 = cut([NT, 6]); mv2 = cut([NT, 2])
        var42 = cut([NT]); rstd2 = cut([NT])
        sc0 = cut([NT, E0]); sfc = cut([NT, E0]); gtop = cut([NT * G0, 8]); gs = cut([NT * G0])
        cmp0 = cut([NT * G0 * G0]); cmp1 = cut([NT * G0 * G0]); rank = cut([NT * G0])
        HID = cut([2, S])
        mr = cut([NT, E0 + 4]); w0 = cut([NT, E0]); wsum = cut([NT]); wrec = cut([NT])
        mx = cut([NH * NT]); nmx = cut([2 * NH * NT]); nmt = cut([P], parts=64); nm3 = cut([3, P], BF16, parts=64)
        nmr = cut([P], parts=64)
        OS = cut([NQ, S])
        rden, att = qf, qf2
        PT = cut([20, S])
        l0_end = at[0]
        at[0] = l0_end - 10 * S
        qs3 = cut([3, S], BF16); ks3 = cut([3, S], BF16)
        wt = cut([S], parts=E0); wtm = cut([S], BF16, parts=E0); wtr = cut([S], parts=E0)
        SG = cut([2, S]); HDT = cut([2, S])
        assert at[0] <= l0_end

        at[0] = 0
        xn1 = cut([NT, D]); zz = cut([NT, D]); xn1T = cut([S]); zT = cut([S])
        ssq = cut([NT]); rz = cut([NT])
        ba = cut([NT, 2 * HV]); aab = cut([NT, HV]); sp = cut([NT, HV]); beta = cut([NT, HV]); gg = cut([NT, HV])
        eG = cut([3, NT * HV])
        lf = cut([NT, EF]); pf = cut([NT, EF]); mrf = cut([NT, EF + 6]); wf = cut([NT, EF]); red4 = cut([NT]); rec4 = cut([NT])
        wfT = cut([S], parts=EF)
        CV = arena[0:P, at[0]:at[0] + 4 * S].rearrange("p (a b) -> p a b", a=4)
        GM = cut([2, 4 * P]); DU = cut([4 * P]); DL = [cut([4 * P]) for _ in range(2)]
        qkT = cut([2 * HK, S])
        vT = cut([HV, S])
        ktok = cut([HK, P]); vb = cut([HV, P]); sz = cut([HV, P])
        ss8 = cut([8]); rr8 = cut([8]); rk2 = cut([HK]); nlam = cut([HV]); rkb = cut([HV]); s1 = cut([HV])
        rq2 = cut([HK]); rqs = cut([HK]); so8 = cut([HV]); rc8 = cut([HV])
        N_ = [cut([4 * P]) for _ in range(2)]
        QKD = cut([HV, P])
        State = cut([HV, P])
        R = cut([HV, P]); o1s = cut([HV, P]); dl = cut([HV, P]); DLS = cut([HV, P]); coreT = cut([HV, P])
        NTT = [cut([4 * P]) for _ in range(2)]
        halves = lambda a: [a[:, 4 * i:4 * i + 4, :].rearrange("p a b -> p (a b)") for i in range(2)]
        T = {"NT": NTT, "TT": NTT, "M2": N_, "X": DL, "M": halves(o1s), "MT": halves(R), "L32": halves(dl),
             "L64": halves(coreT), "L128": halves(DLS)}
        GH = cut([2, S]); facc = cut([NT, D])
        hbuf = zz
        oo, core = R, junk
        l1_end = at[0]
        assert max(l0_end, l1_end) <= ARENA, (l0_end, l1_end)
        hT = xn1T
        SG1, HDT1, HID1 = CV, coreT.rearrange("p (u a) b -> p u (a b)", u=2), GH
        wr = lf; wt1 = wfT

        names = """x_in g_init weights_a weights_m weights_b setup_v setup_a out_ready out_dma
            v_link v_var g_rstd v_xn p_xnT a_xnT p_q p_lat v_q v_k v_lat p_latT v_latT p_k p_v a_v
            v_lvar g_lrstd a_lexp v_lsfc v_w0 p_w0T v_w96 v_qs3 v_ks3 d_scrq d_scrk d_q d_k
            p_gate p_up p_wb a_sg v_t v_hid p_down p_max v_max v_nm p_mT v_nm3 d_scrm d_m
            p_score a_p p_o v_os p_nd v_att p_acc v_x1
            v_var1 g_rstd1 v_xn1 v_ms1 g_rz v_z p_xn1T a_xn1T p_zT v_zT p_ba a_eb v_ab a_eab a_sp v_g p_gc a_eG
            v_lm a_fe v_wf p_wfT v_wfT p_qkv a_cv v_tap v_cv a_qkv
            p_kt p_qt p_vt p_z a_kt a_ss a_sz v_sse g_rr v_sc a_vb p_kk g_gm p_d a_d v_N v_qkd
            p_inv0 p_inv1 v_inv0 v_inv1 a_inv0 a_inv1 g_inv0 g_inv1
            p_w v_R p_o1 a_o1 p_dl a_dl v_dls p_o2 v_o p_s v_S a_so v_sr g_rc v_core p_ct a_ct p_wout
            v_h v_ms2 g_rz2 v_h2 p_hT v_hT p_r1 v_lm1 a_fe1 v_w1r p_w1T v_w96b
            p_gate1 p_up1 p_wb1 a_sg1 v_hid1 p_down1 d_w0 d_w1 p_fh a_gh p_fo v_fo""".split()
        s = {n: sig(n) for n in names}
        L0, L1 = schedule_l0(), schedule_l1()

        ticks = []

        def wait_alone(engine, sem, value):
            engine.wait_ge(sem, value)
            engine.tensor_tensor(tick[:, len(ticks):len(ticks) + 1], nhalf[:, 0:1], nhalf[:, 0:1], ALU.add)
            ticks.append(engine)

        nothing = lambda *a: None
        block = ctx.enter_context(nc.Block())

        @block.sync
        def _(sp_):
            for n in EARLY:
                sp_.dma_start(W[n][:], weights[n]).then_inc(s["weights_a"].sem, 16)
            with sp_.Fori(0, LOOPS) as b:
                for e in range(2):
                    sp_.wait_ge(*s["p_fo"].at(b, 0))
                    sp_.dma_start(wring[:, e, :], w_last[e]).then_inc(*s[f"d_w{e}"].up16)
                sp_.wait_ge(*s["v_x1"].at(b, 0))
                sp_.dma_start(x[:, :, :], x_v[bass.ds(b, 1)].rearrange("a p t d -> p (a t) d")).then_inc(*s["x_in"].up16)
                for name, src, scr, dst, kinds in (("q", qs3, scrq, QS, QSPLIT), ("k", ks3, scrk, KS, KSPLIT)):
                    sp_.wait_ge(*s[f"v_{name}s3"].at(b, 1))
                    sp_.dma_start(scr.rearrange("s p n -> p s n"), src).then_inc(*s["d_scr" + name].up16)
                    sp_.wait_ge(*s["d_scr" + name].at(b, 16))
                    sp_.wait_ge(*s["g_init"].at(b, 3))
                    for hh in range(2):
                        for t, kind in enumerate(kinds):
                            rows = 64 * hh + HD * t
                            part = bass.AP(tensor=scr.tensor, offset=kind * P * S + hh * HD * S,
                                           ap=[[S, HD], [2 * HD * S, NP], [1, S]])
                            sp_.dma_start(dst[rows:rows + HD, :, :], part).then_inc(*s["d_" + name].up16)
                sp_.wait_ge(*s["v_nm3"].at(b, 1))
                sp_.dma_start(scrm.rearrange("s p n -> p s n"), nm3).then_inc(*s["d_scrm"].up16)
                sp_.wait_ge(*s["d_scrm"].at(b, 16))
                for hh in range(2):
                    part = bass.AP(tensor=scrm.tensor, offset=hh * S, ap=[[64 * P, 3], [2 * S, NP], [1, S]])
                    sp_.dma_start(QS[64 * hh + KROWS:64 * hh + MROWS, :, :], part).then_inc(*s["d_m"].up16)
                for e in range(2, EF):
                    sp_.wait_ge(*s["p_fo"].at(b, FC * (e - 1)))
                    sp_.dma_start(wring[:, e % 2, :], w_last[e]).then_inc(*s[f"d_w{e % 2}"].up16)
            sp_.wait_ge(*s["out_dma"].at(LOOPS, 0))

        @block.tensor
        def _(pe):
            mm = nc.tensor.matmul
            pe.wait_ge(s["weights_a"].sem, 16 * len(EARLY))
            pe.wait_ge(s["setup_v"].sem, 2)
            with pe.Fori(0, LOOPS) as b:
                met = {}

                def need(name, n):
                    if met.get(name, 0) < n:
                        pe.wait_ge(*s[name].at(b, n))
                        met[name] = n

                def after(name, n, i):
                    need(name, n)
                    return bank[i]

                def tr(dst, src, k=P):
                    return nc.tensor.transpose(dst, src, W["ident"][0:k, 0:k])

                pe.wait_ge(*s["out_ready"].at(b, 0))
                bk = bank[0]
                for t in range(NT):
                    pe.wait_ge(*s["v_xn"].at(b, t + 1))
                    last = tr(bk[:, t * P:(t + 1) * P], xn[:, t, :])
                last.then_inc(*s["p_xnT"].up)
                pe.wait_ge(*s["a_xnT"].at(b, 1))
                q1, q2 = bank[1], bank[2]
                mm(q1[:, :], W["Wq"][:], xnT, start=True, stop=True)
                mm(q2[:, :], W["Wqr"][:], xnT, start=True, stop=True).then_inc(*s["p_q"].up)
                bk = bank[3]
                for t in range(NT):
                    mm(bk[:, t * LAT:(t + 1) * LAT], xnT[:, t * P:(t + 1) * P], W["Wdkv"][:], start=True, stop=True)
                for t in range(NT):
                    last = mm(bk[:, 128 + t * E0:128 + (t + 1) * E0], xnT[:, t * P:(t + 1) * P], W["rw0"][:],
                              start=True, stop=True)
                last.then_inc(*s["p_lat"].up)
                pe.wait_ge(*s["v_lat"].at(b, 1))
                bk = bank[4]
                for t in range(NT):
                    last = tr(bk[0:LAT, t * P:(t + 1) * P], latn[:, t, :])
                last.then_inc(*s["p_latT"].up)
                pe.wait_ge(*s["v_latT"].at(b, 1))
                k1, k2 = after("v_q", 1, 1), bank[2]
                mm(k1[:, :], W["Wuk"][:], latT, start=True, stop=True)
                mm(k2[:, :], W["Wukr"][:], latT, start=True, stop=True).then_inc(*s["p_k"].up)
                bk = bank[5]
                for t in range(NT):
                    last = mm(bk[:, t * P:(t + 1) * P], latT[:, t * P:(t + 1) * P], W["Wuv"][:], start=True, stop=True)
                last.then_inc(*s["p_v"].up)

                def route():
                    pe.wait_ge(*s["v_w0"].at(b, 1))
                    bk = after("v_latT", 1, 4)
                    for t in range(NT):
                        last = tr(bk[0:E0, t * P:(t + 1) * P], w0[:, t, :])
                    last.then_inc(*s["p_w0T"].up)

                def spread(p):
                    bk = after("v_hid", p - 1, 4 + 2 * (p % 2)) if p >= 2 else bank[4 + 2 * p]
                    mm(bk[:, :], W["sel0"][:, p, :], W96[:, :], start=True, stop=True).then_inc(*s["p_wb"].up)

                def gu(p):
                    if p == 0:
                        pe.wait_ge(s["weights_m"].sem, 16 * len(MIDDLE))
                    if p > 1:
                        spread(p - 1)
                    bk = after(*(("a_sg", p) if p else ("v_k", 1)), 1)
                    mm(bk[:, :], W["gate0"][:, p, :] if p < PR0 else W["sg"][:], xnT, start=True, stop=True
                       ).then_inc(*s["p_gate"].up)
                    bk = after(*((("v_lsfc", 1), ("a_v", 1))[p] if p < 2 else ("v_t", p - 1)), 3 + 2 * (p % 2))
                    mm(bk[:, :], W["up0"][:, p, :] if p < PR0 else W["su"][:], xnT, start=True, stop=True
                       ).then_inc(*s["p_up"].up)
                    if p == 1:
                        pe.wait_ge(*s["v_w96"].at(b, 1))
                        spread(0)

                def wbd(p):
                    pe.wait_ge(*s["v_hid"].at(b, p + 1))
                    for t in range(NT):
                        last = mm(bank[7][:, t * P:(t + 1) * P], HID[:, p % 2, t * P:(t + 1) * P],
                                  W["down0"][:, p, :] if p < PR0 else W["sd"][:],
                                  start=(p == 0 and t == 0), stop=False, skip_group_check=True)
                    last.then_inc(*s["p_down"].up)

                def smax(n):
                    h, qt = n // NT, n % NT
                    o, w = 64 * (h % 2), P * (qt + 1)
                    if n == 0:
                        pe.wait_ge(*s["d_q"].at(b, 16 * 12))
                        pe.wait_ge(*s["d_k"].at(b, 16 * 12))
                    bk = after(*((("a_xnT", 1), ("v_k", 1))[n] if n < 2 else ("v_max", n - 1)), (0, 2)[n % 2])
                    mm(bk[:, 0:w], QS[o:o + KROWS, h // 2, qt * P:(qt + 1) * P], KS[o:o + KROWS, h // 2, 0:w],
                       start=True, stop=True, tile_position=(o, 0)).then_inc(*s["p_max"].up)

                def maxrows():
                    pe.wait_ge(*s["v_nm"].at(b, 1))
                    bk = after("v_max", NH * NT - 1, 0)
                    tr(bk[:, 0:P], nmx).then_inc(*s["p_mT"].up)

                def score(g, i):
                    n = 12 * g + i
                    if n == 0:
                        pe.wait_ge(*s["d_m"].at(b, 32))
                    pair, k = 2 * g + i // 6, i % 6
                    last = (("a_sg", PR0 + 1), ("v_max", NH * NT), ("v_hid", PR0 + 1), ("v_hid", PR0 - 1), ("v_t", PR0))
                    bk = after(*(last[n] if n < 5 else ("a_p", n - 4)), 1 + n % 5)
                    parts = {0: [(0, 0, 0)], 1: [(1, 0, 0)], 2: [(0, 1, 0), (0, 3, 384)], 3: [(1, 1, 0), (1, 3, 384)],
                             4: [(0, 2, 0)], 5: [(1, 2, 0)]}[k]
                    for hh, kt, col in parts:
                        o, w = 64 * hh, S - P * kt
                        mm(bk[:, col:col + w], KS[o:o + MROWS, pair, kt * P:(kt + 1) * P],
                           QS[o:o + MROWS, pair, kt * P:S], start=True, stop=False, tile_position=(o, 0),
                           skip_group_check=True)
                        last = mm(bk[:, col:col + P], W["identb"][:], W["maskt"][:], start=False, stop=True,
                                  skip_group_check=True)
                    last.then_inc(*s["p_score"].up)

                def pv(g):
                    pe.wait_ge(*s["a_p"].at(b, 12 * g + 12))
                    if g == 0:
                        pe.wait_ge(*s["a_v"].at(b, 1))
                    bk = after(*((("v_hid", PR0), ("v_nm3", 1))[g] if g < 2 else ("v_os", g - 1)), 0 if g % 2 else 6)
                    for kt in range(NT):
                        for j in range(4):
                            slot, col = {0: (j % 2, 0), 1: (2 + j % 2, 0), 2: (4, 256 * (j % 2)), 3: (2 + j % 2, 384)}[kt]
                            slot += 5 * (j // 2) + 10 * (g % 2)
                            last = mm(bk[32 * j:32 * j + 32, kt * P:S], V32[:, kt, 4 * g + j, :],
                                      PT[:, slot, col:col + S - kt * P], start=(kt == 0), stop=(kt == NT - 1),
                                      tile_position=(0, 32 * j), skip_group_check=True)
                    last.then_inc(*s["p_o"].up)

                def nd():
                    need("a_p", 12 * NQ - 3)
                    for i in (1, 0):
                        for g in range(NQ):
                            need("v_os", g + 1)
                            last = mm(bank[4 + i][32 * g:32 * g + 32, :], W["pick"][:, i, :], OS[:, g, :],
                                      start=True, stop=True, tile_position=(0, 32 * g), skip_group_check=True)
                        last.then_inc(*s["p_nd"].up)

                def attn_out():
                    pe.wait_ge(*s["v_att"].at(b, 1))
                    for t in range(NT):
                        last = mm(bank[7][:, t * P:(t + 1) * P], att[:, t * P:(t + 1) * P], W["Wo"][:],
                                  start=False, stop=True, skip_group_check=True)
                    last.then_inc(*s["p_acc"].up)

                steps = {"route": route, "gu": gu, "wbd": wbd, "max": smax, "maxrows": maxrows,
                         "exp": score, "pv": pv, "nd": nd, "attn_out": attn_out}
                for step in L0:
                    steps.get(step[0], nothing)(*step[1:])

                pe.wait_ge(s["weights_b"].sem, 16 * len(LATE))
                bk = after("v_os", NQ, 0)
                for t in range(NT):
                    pe.wait_ge(*s["v_xn1"].at(b, t + 1))
                    last = tr(bk[:, t * P:(t + 1) * P], xn1[:, t, :])
                last.then_inc(*s["p_xn1T"].up)
                pe.wait_ge(*s["a_xn1T"].at(b, 1))
                small = after("a_p", 12 * NQ - 1, 2)
                for t in range(NT):
                    mm(small[:, 64 + t * EF:64 + (t + 1) * EF], xn1T[:, t * P:(t + 1) * P], W["rf"][:], start=True, stop=True)
                bk = after("a_p", 12 * NQ - 2, 1)
                for t in range(NT):
                    pe.wait_ge(*s["v_z"].at(b, t + 1))
                    last = tr(bk[:, t * P:(t + 1) * P], zz[:, t, :])
                last.then_inc(*s["p_zT"].up)
                pe.wait_ge(*s["v_zT"].at(b, 1))
                for t in range(NT):
                    last = mm(small[:, t * 16:(t + 1) * 16], zT[:, t * P:(t + 1) * P], W["Wba"][:], start=True, stop=True)
                last.then_inc(*s["p_ba"].up)

                def qkv(m0):
                    for m in (m0, m0 + 1) if m0 < NQKV else ():
                        first = (("v_att", 1), ("v_att", 1), ("v_os", NQ - 1), ("v_x1", 1))
                        bk = after(*(first[m] if m < 4 else ("v_cv", m - 3)), 4 + m % 4)
                        mm(bk[:, :], W["Wqkvz"][:, m * P:(m + 1) * P], zT, start=True, stop=True
                           ).then_inc(*s["p_qkv"].up)
                    if m0 == 4:
                        pe.wait_ge(*s["v_g"].at(b, 1))
                        bk = after("a_p", 12 * NQ, 3)
                        g2 = gg.rearrange("p a b -> p (a b)")
                        mm(bk[:, 0:32], W["upto"][:], g2, start=True, stop=True)
                        mm(bk[:, 32:64], W["after"][:], g2, start=True, stop=True)
                        mm(bk[:, 64:96], W["ones"][:], g2, start=True, stop=True).then_inc(*s["p_gc"].up)
                    if m0 == 6:
                        pe.wait_ge(*s["v_wf"].at(b, 1))
                        bk = after("a_xn1T", 1, 0)
                        for t in range(NT):
                            last = tr(bk[0:EF, t * P:(t + 1) * P], wf[:, t, :])
                        last.then_inc(*s["p_wfT"].up)

                def ck(c):
                    cs = slice(c * P, (c + 1) * P)
                    if c == 0:
                        pe.wait_ge(*s["a_qkv"].at(b, NQKV))
                    bk = after(*(("a_ct", 2 * c - 1) if c else ("v_cv", NQKV - 3)), 4)
                    for h in range(HK):
                        last = tr(bk[:, h * P:(h + 1) * P], qkT[:, HK + h, cs])
                    last.then_inc(*s["p_kt"].up)
                    bk = after(*(("a_ct", 2 * c) if c else ("v_cv", NQKV - 2)), 5)
                    for h in range(HK):
                        last = tr(bk[:, h * P:(h + 1) * P], qkT[:, h, cs])
                    last.then_inc(*s["p_qt"].up)

                def ckk(c):
                    cs = slice(c * P, (c + 1) * P)
                    for i in range(2):
                        bk = after(*(("v_o", 2 * c - 1 + i) if c else (("v_wfT", 1), ("v_zT", 1))[i]), i)
                        for kh in range(2):
                            rhs = qkT[:, 2 * i + kh:2 * i + kh + HK + 1:HK, cs]
                            last = mm(bk[:, kh * 2 * P:(kh + 1) * 2 * P], qkT[:, HK + 2 * i + kh, cs], rhs,
                                      start=True, stop=True)
                        last.then_inc(*s["p_kk"].up)

                def cd(c, half):
                    for i, (tri, mask) in enumerate((("upto", "below"), ("after", "notabove"))):
                        if i == 0:
                            bk = after(*(("v_S", 8 * c - 4 + 4 * half) if c else (("v_lm", 1), ("a_eG", 1))[half]), 2 + half)
                        else:
                            bk = after(*(("a_d", 4 * c + 2) if half else ("a_gh", 8 * c + 1)), 7)
                        pe.wait_ge(*s["g_gm"].at(b, 4 * c + 2 * half + i + 1))
                        mm(bk[:, :], W[tri][:], GM[:, i, :], start=True, stop=False)
                        mk = W[mask][:].unsqueeze(1).broadcast_to((P, 4, P))
                        last = mm(bk[:, :], W["identb"][:], mk, start=False, stop=True)
                        last.then_inc(*s["p_d"].up)

                def cz(c):
                    for i in range(2):
                        bk = after("a_ss", 8 * c + 4 * i + 4, 4 + i)
                        w = (NQKV + 4 * i) * P
                        mm(bk[:, :], zT[:, c * P:(c + 1) * P], W["Wqkvz"][:, w:w + 4 * P], start=True, stop=True
                           ).then_inc(*s["p_z"].up)

                def cv(c):
                    for i in range(2):
                        bk = after("a_sz", 2 * c + i + 1, 4 + i)
                        for h in range(4):
                            last = tr(bk[:, h * P:(h + 1) * P], vT[:, 4 * i + h, c * P:(c + 1) * P])
                        last.then_inc(*s["p_vt"].up)

                def four(bk, half, lhs, rhs, transpose=False):
                    for j in range(4):
                        c4 = slice(j * P, (j + 1) * P)
                        last = tr(bk[:, c4], lhs[:, c4]) if transpose else \
                            mm(bk[:, c4], lhs[:, c4], rhs[:, c4], start=True, stop=True)
                    last.then_inc(*s[f"p_inv{half}"].up)

                def inv(c, half, st):
                    A, V = f"a_inv{half}", f"v_inv{half}"
                    a0, v0 = INV_A * c, INV_V * c
                    ba_, bb, bc = ((0, 1, 4), (2, 3, 5))[half]
                    t = {k: v[half] for k, v in T.items()}
                    wa = lambda n: need(A, a0 + n)
                    wv = lambda n: need(V, v0 + n)
                    if st == 0:
                        pe.wait_ge(*s["v_N"].at(b, 8 * c + 4 * half + 4))
                        four(after(*(("v_qkd", 2 * c + 1) if half == 0 else ("a_d", 4 * c + 1)), ba_), half, N_[half], None, True)
                    elif st == 2:
                        wv(2)
                        pe.wait_ge(*s[f"g_inv{half}"].at(b, 4 * c + 1))
                        four(after(*(("v_qkd", 2 * c + 2) if half == 0 else ("a_d", 4 * c + 3)), bb), half, t["M"], t["MT"])
                        four(after("a_vb", 8 * c + 4 * half + 4, bc), half, t["MT"], t["M"])
                    elif st == 3:
                        wv(3); wa(2)
                        four(after(A, a0 + 1, ba_), half, t["MT"], t["X"])
                        four(after(V, v0 + 3, bb), half, t["M2"], t["MT"])
                        four(after(A, a0 + 2, bc), half, t["MT"], t["M2"])
                    elif st == 4:
                        wv(5); wa(3)
                        four(after(V, v0 + 4, ba_), half, t["MT"], t["X"])
                        four(after(A, a0 + 3, bc), half, t["M2"], t["MT"])
                    elif st == 5:
                        wv(6); wa(4)
                        four(after(V, v0 + 6, ba_), half, t["MT"], t["X"])
                    elif st == 6:
                        wv(7)
                        four(after(V, v0 + 5, bb), half, t["X"], None, True)
                    elif st in (7, 10):
                        wa(5 if st == 7 else 7)
                        pe.wait_ge(*s[f"g_inv{half}"].at(b, 4 * c + (2 if st == 7 else 3)))
                        four(after(*((V, v0 + 7) if st == 7 else (A, a0 + 6)), ba_), half,
                             t["L32" if st == 7 else "L64"], t["X"])
                    elif st in (8, 11):
                        wa(6 if st == 8 else 8)
                        four(after(*((A, a0 + 4) if st == 8 else (V, v0 + 8)), bc), half, t["TT"], t["M2"])
                    elif st in (9, 12):
                        wv(8 if st == 9 else 9)
                        four(after(A, a0 + (5 if st == 9 else 7), bb), half, t["X"], None, True)
                    elif st == 13:
                        wa(9)
                        pe.wait_ge(*s[f"g_inv{half}"].at(b, 4 * c + 4))
                        four(after(A, a0 + 8, ba_), half, t["L128"], t["X"])
                    elif st == 14:
                        wa(10)
                        four(after(V, v0 + 9, bc), half, t["M2"], t["TT"])

                def sw(c):
                    if c:
                        pe.wait_ge(*s["v_S"].at(b, 8 * c))
                        for i in range(2):
                            bk = after("a_inv0", INV_A * (c + 1) - i, (0, 1)[i])
                            for kh in range(2):
                                last = mm(bk[:, kh * 2 * P:(kh + 1) * 2 * P], qkT[:, HK + 2 * i + kh, c * P:(c + 1) * P],
                                          State[:, 4 * i + 2 * kh:4 * i + 2 * kh + 2, :], start=True, stop=True)
                            last.then_inc(*s["p_w"].up)

                def so1(c):
                    if c:
                        for i in range(2):
                            bk = after("a_inv1", INV_A * (c + 1) - i, (2, 3)[i])
                            for kh in range(2):
                                last = mm(bk[:, kh * 2 * P:(kh + 1) * 2 * P], qkT[:, 2 * i + kh, c * P:(c + 1) * P],
                                          State[:, 4 * i + 2 * kh:4 * i + 2 * kh + 2, :], start=True, stop=True)
                            last.then_inc(*s["p_o1"].up)

                def sdl(c):
                    rhs = R if c else vb
                    pe.wait_ge(*s["a_vb"].at(b, 8 * c + 8))
                    for i in range(2):
                        if c:
                            need("v_R", 8 * (c - 1) + 4 * i + 4)
                        need(f"v_inv{i}", INV_V * (c + 1))
                        bk = after(f"v_inv{i}", INV_V * (c + 1), (4, 5)[i])
                        for j in range(4):
                            last = mm(bk[:, j * P:(j + 1) * P], T["TT"][i][:, j * P:(j + 1) * P], rhs[:, 4 * i + j, :],
                                      start=True, stop=True)
                        last.then_inc(*s["p_dl"].up)

                def so2(c):
                    for i in range(2):
                        need("a_dl", 2 * c + i + 1)
                        need("v_qkd", 2 * c + i + 1)
                        bk = after(*(("v_R", 8 * c - 4 + 4 * i) if c else ("a_inv0", INV_A - i)), (0, 1)[i])
                        for j in range(4):
                            last = mm(bk[:, j * P:(j + 1) * P], QKD[:, 4 * i + j, :], dl[:, 4 * i + j, :],
                                      start=True, stop=True)
                        last.then_inc(*s["p_o2"].up)

                def ss(c):
                    if c < NT - 1:
                        for i in range(2):
                            pe.wait_ge(*s["v_dls"].at(b, 8 * c + 4 * i + 4))
                            bk = after(*(("a_o1", 8 * c - 4 + 4 * i) if c else ("a_inv1", INV_A - i)), (2, 3)[i])
                            for kh in range(2):
                                last = mm(bk[:, kh * 2 * P:(kh + 1) * 2 * P], ktok[:, 2 * i + kh, :],
                                          DLS[:, 4 * i + 2 * kh:4 * i + 2 * kh + 2, :], start=True, stop=True)
                            last.then_inc(*s["p_s"].up)

                def sn2(c):
                    for i in range(2):
                        pe.wait_ge(*s["v_core"].at(b, 8 * c + 4 * i + 4))
                        bk = after("a_dl", 2 * c + i + 1, (4, 5)[i])
                        for j in range(4):
                            last = tr(bk[:, j * P:(j + 1) * P], core[:, 4 * i + j, :])
                        last.then_inc(*s["p_ct"].up)

                def swo(c):
                    pe.wait_ge(*s["a_ct"].at(b, 2 * c + 2))
                    bk = after("a_gh", 8 * c + 8, 7)
                    for h in range(HV):
                        last = mm(bk[:, 0:P], coreT[:, h, :], W["Wout"][:, h, :], start=(h == 0), stop=(h == HV - 1))
                    last.then_inc(*s["p_wout"].up)

                def ffn_out(f):
                    e, k = f // FC, f % FC
                    pe.wait_ge(*s["a_gh"].at(b, f + 1))
                    if k == 0:
                        need(*(("v_fo", 4 * e) if e else ("v_cv", NQKV - 1)))
                    for t in range(NT):
                        last = mm(bank[6][:, t * P:(t + 1) * P], GH[:, f % 2, t * P:(t + 1) * P],
                                  wring[:, e % 2, FC * P + k * D:FC * P + (k + 1) * D],
                                  start=(k == 0 and t == 0), stop=(k == FC - 1), skip_group_check=True)
                    last.then_inc(*s["p_fo"].up)

                def ffn(f):
                    if f == 0:
                        bk = after("v_cv", NQKV, 7)
                    else:
                        bk = after(*(("v_h", f // 8) if f % 8 == 0 else ("a_d", f // 2 + 4) if f % 8 == 1 else ("a_gh", f)), 7)
                    e, k = f // FC, f % FC
                    if k == 0:
                        pe.wait_ge(*s[f"d_w{e % 2}"].at(b, 16 * (e // 2 + 1)))
                    mm(bk[:, :], wring[:, e % 2, k * P:(k + 1) * P], xn1T, start=True, stop=True
                       ).then_inc(*s["p_fh"].up)
                    if f:
                        ffn_out(f - 1)

                def hidden():
                    bk = after("v_o", 2 * NT - 1, 0)
                    for t in range(NT):
                        pe.wait_ge(*s["v_h2"].at(b, t + 1))
                        last = tr(bk[:, t * P:(t + 1) * P], hbuf[:, t, :])
                    last.then_inc(*s["p_hT"].up)
                    pe.wait_ge(*s["v_hT"].at(b, 1))
                    bk = after("v_o", 2 * NT, 1)
                    for t in range(NT):
                        last = mm(bk[:, t * E1:(t + 1) * E1], hT[:, t * P:(t + 1) * P], W["r1"][:], start=True, stop=True)
                    last.then_inc(*s["p_r1"].up)
                    need("v_h", NT)
                    for t in range(NT):
                        mm(bank[7][:, t * P:(t + 1) * P], wfT[:, t * P:(t + 1) * P], W["b2"][:], start=(t == 0),
                           stop=False, skip_group_check=True)
                    pe.wait_ge(*s["v_w1r"].at(b, 1))
                    bk = after("v_hT", 1, 0)
                    for t in range(NT):
                        last = tr(bk[0:E1, t * P:(t + 1) * P], wr[:, t, :])
                    last.then_inc(*s["p_w1T"].up)

                def down1(p):
                    pe.wait_ge(*s["v_hid1"].at(b, 2 * p + 2))
                    for t in range(NT):
                        last = mm(bank[7][:, t * P:(t + 1) * P], HID1[:, p % 2, t * P:(t + 1) * P], W["de1"][:, p, :],
                                  start=False, stop=(p == PR1 - 1), skip_group_check=True)
                    last.then_inc(*s["p_down1"].up)

                def moe1(p):
                    bk = after(*((("v_lm1", 1), ("a_o1", 8 * (NT - 1) - 4))[p] if p < 2 else ("a_sg1", p - 1)), 1 + p % 2)
                    mm(bk[:, :], W["ge1"][:, p, :], hT, start=True, stop=True).then_inc(*s["p_gate1"].up)
                    bk = after(*((("a_o1", 8 * (NT - 1)), ("a_ct", 2 * NT))[p] if p < 2 else ("v_hid1", 2 * p - 3)), 3 + 2 * (p % 2))
                    mm(bk[:, :], W["ue1"][:, p, :], hT, start=True, stop=True).then_inc(*s["p_up1"].up)
                    if p == 0:
                        pe.wait_ge(*s["v_w96b"].at(b, 1))
                    bk = after(*((("a_ct", 2 * NT - 1), ("v_fo", 4 * EF))[p] if p < 2 else ("v_hid1", 2 * p - 2)), 4 + 2 * (p % 2))
                    mm(bk[:, :], W["sel1"][:, p, :], W96b[:, :], start=True, stop=True).then_inc(*s["p_wb1"].up)
                    if p:
                        down1(p - 1)

                steps = {"qkv": qkv, "ck": ck, "ckk": ckk, "cd": cd, "cz": cz, "cv": cv, "inv": inv, "ffn": ffn, "sw": sw,
                         "ffn_last": lambda: ffn_out(EF * FC - 1),
                         "so1": so1, "sdl": sdl, "so2": so2, "ss": ss, "sn2": sn2, "swo": swo, "hidden": hidden, "moe1": moe1, "moe1_last": lambda: down1(PR1 - 1)}
                for step in L1:
                    steps.get(step[0], nothing)(*step[1:])

        @block.scalar
        def _(act):
            fn = nc.scalar.activation

            for lot, group in (("weights_m", MIDDLE), ("weights_b", LATE)):
                for n in group:
                    act.dma_start(W[n][:], weights[n]).then_inc(s[lot].sem, 16)
            act.wait_ge(s["weights_a"].sem, 16 * len(EARLY))
            fn(neg_a[:, :], W["alog"][:], ACT.Exp).then_inc(s["setup_a"].sem, 1)
            act.wait_ge(s["setup_v"].sem, 2)
            with act.Fori(0, LOOPS) as b:
                act.wait_ge(*s["out_ready"].at(b, 0))
                act.wait_ge(*s["p_xnT"].at(b, 1))
                fn(xnT, bank[0][:, :], ACT.Copy).then_inc(*s["a_xnT"].up)
                act.wait_ge(*s["v_lat"].at(b, 1))
                fn(sc0.rearrange("p a b -> p (a b)"), bank[3][:, 128:256], ACT.Exp, scale=-1.0).then_inc(*s["a_lexp"].up)
                act.wait_ge(*s["p_v"].at(b, 1))
                act.wait_ge(*s["g_init"].at(b, 3))
                fn(V32[:, :, :, 0:HD], bank[5][:, :].rearrange("p (t h d) -> p t h d", t=NT, h=NH), ACT.Copy
                   ).then_inc(*s["a_v"].up)

                def gu(p):
                    act.wait_ge(*s["p_gate"].at(b, p + 1))
                    if p >= 2:
                        act.wait_ge(*s["v_t"].at(b, p - 1))
                    fn(SG[:, p % 2, :], bank[1][:, :], ACT.Silu).then_inc(*s["a_sg"].up)

                def expo(g, i):
                    n = 12 * g + i
                    act.wait_ge(*s["p_score"].at(b, n + 1))
                    if g >= 2 and i == 0:
                        act.wait_ge(*s["p_o"].at(b, g - 1))
                    k, w = i % 6, 512 if i % 6 < 4 else 256
                    slot, col = 10 * (g % 2) + 5 * (i // 6) + min(k, 4), 256 * (k == 5)
                    fn(PT[:, slot, col:col + w], bank[1 + n % 5][:, 0:w], ACT.Exp, scale=float(HD) ** -0.5).then_inc(*s["a_p"].up)

                steps = {"gu": gu, "exp": expo}
                for step in L0:
                    steps.get(step[0], nothing)(*step[1:])

                act.wait_ge(s["weights_b"].sem, 16 * len(LATE))
                act.wait_ge(*s["v_x1"].at(b, 1))
                act.wait_ge(*s["p_xn1T"].at(b, 1))
                fn(xn1T, bank[0][:, :], ACT.Copy).then_inc(*s["a_xn1T"].up)
                act.wait_ge(*s["p_ba"].at(b, 1))
                fn(ba, bank[2][:, 0:64].rearrange("p (t n) -> p t n", t=NT), ACT.Exp, scale=-1.0).then_inc(*s["a_eb"].up)
                act.wait_ge(*s["v_ab"].at(b, 1))
                fn(sp, sp, ACT.Exp, scale=-1.0).then_inc(*s["a_eab"].up)
                act.wait_ge(*s["v_lm"].at(b, 1))
                fn(lf, lf, ACT.Exp).then_inc(*s["a_fe"].up)
                act.wait_ge(*s["a_eab"].at(b, 1))
                fn(sp, sp, ACT.Ln, bias=1.0).then_inc(*s["a_sp"].up)

                def qkv(m0):
                    for m in (m0, m0 + 1) if m0 < NQKV else ():
                        act.wait_ge(*s["p_qkv"].at(b, m + 1))
                        if m >= 4:
                            act.wait_ge(*s["a_qkv"].at(b, m - 3))
                        fn(CV[:, m % 4, :], bank[4 + m % 4][:, :], ACT.Copy, scale=W["convw"][:, m, 3:4]
                           ).then_inc(*s["a_cv"].up)
                    for m in (m0 - 2, m0 - 1) if m0 else ():
                        act.wait_ge(*s["v_cv"].at(b, m + 1))
                        dst = qkT[:, m, :] if m < 2 * HK else vT[:, m - 2 * HK, :]
                        fn(dst, CV[:, m % 4, :], ACT.Silu).then_inc(*s["a_qkv"].up)
                    if m0 == 4:
                        act.wait_ge(*s["p_gc"].at(b, 1))
                        fn(eG.rearrange("p a b -> p (a b)"), bank[3][:, 0:96], ACT.Exp).then_inc(*s["a_eG"].up)

                def ck(c):
                    act.wait_ge(*s["p_kt"].at(b, c + 1))
                    if c:
                        act.wait_ge(*s["p_s"].at(b, 2 * c))
                        act.wait_ge(*s["p_ct"].at(b, 2 * c))
                        act.wait_ge(*s["v_core"].at(b, 8 * c))
                    fn(ktok.rearrange("p a b -> p (a b)"), bank[4][:, :], ACT.Copy).then_inc(*s["a_kt"].up)
                    for i in range(2):
                        if i:
                            act.wait_ge(*s["p_qt"].at(b, c + 1))
                        for h in range(HK):
                            n = 4 * i + h
                            fn(junk[:, n, :], bank[4 + i][:, h * P:(h + 1) * P], ACT.Square, accum_out=ss8[:, n:n + 1]
                               ).then_inc(*s["a_ss"].up)

                def cd(c, half):
                    for i in range(2):
                        act.wait_ge(*s["p_d"].at(b, 4 * c + 2 * half + i + 1))
                        if i == 1 and (c or half):
                            act.wait_ge(*s["v_qkd"].at(b, 2 * c + half))
                        fn((DL[half], DU)[i], bank[(2 + half, 7)[i]][:, :], ACT.Exp).then_inc(*s["a_d"].up)

                def cz(c):
                    for i in range(2):
                        act.wait_ge(*s["p_z"].at(b, 2 * c + i + 1))
                        fn(sz.rearrange("p a b -> p (a b)")[:, i * 512:(i + 1) * 512], bank[4 + i][:, :], ACT.Silu
                           ).then_inc(*s["a_sz"].up)

                def cv(c):
                    act.wait_ge(*s["v_sc"].at(b, c + 1))
                    if c:
                        act.wait_ge(*s["p_dl"].at(b, 2 * c))
                    for i in range(2):
                        act.wait_ge(*s["p_vt"].at(b, 2 * c + i + 1))
                        for j in range(4):
                            h = 4 * i + j
                            fn(vb[:, h, :], bank[4 + i][:, j * P:(j + 1) * P], ACT.Copy, scale=rkb[:, h:h + 1]
                               ).then_inc(*s["a_vb"].up)

                def inv(c, half, st):
                    t = {k: v[half] for k, v in T.items()}
                    ba_, bb, bc = ((0, 1, 4), (2, 3, 5))[half]
                    p0, a0 = INV_P * c, INV_A * c
                    todo = {0: (1, "NT", ba_), 2: (3, "M2", bc), 3: (6, "M2", bc), 4: (8, "MT", bc),
                            6: (10, "TT", bb), 7: (11, "M2", ba_), 9: (13, "TT", bb), 10: (14, "M2", ba_),
                            12: (16, "TT", bb), 13: (17, "M2", ba_)}
                    if st in todo:
                        n, dst, i = todo[st]
                        act.wait_ge(*s[f"p_inv{half}"].at(b, p0 + n))
                        if st == 0 and c:
                            act.wait_ge(*s[f"g_inv{half}"].at(b, 4 * c))
                        if st == 6:
                            act.wait_ge(*s[f"g_inv{half}"].at(b, 4 * c + 4))
                        fn(t[dst], bank[i][:, :], ACT.Copy).then_inc(*s[f"a_inv{half}"].up)

                def so1(c):
                    if c:
                        for i in range(2):
                            act.wait_ge(*s["p_o1"].at(b, 2 * (c - 1) + i + 1))
                            for j in range(4):
                                h = 4 * i + j
                                fn(o1s[:, h, :], bank[(2, 3)[i]][:, j * P:(j + 1) * P], ACT.Copy,
                                   scale=eG[:, 0, c * HV + h:c * HV + h + 1]).then_inc(*s["a_o1"].up)

                def sdl(c):
                    for i in range(2):
                        act.wait_ge(*s["p_dl"].at(b, 2 * c + i + 1))
                        fn(dl[:, 4 * i:4 * i + 4, :].rearrange("p a b -> p (a b)"), bank[(4, 5)[i]][:, :], ACT.Copy
                           ).then_inc(*s["a_dl"].up)

                def so2(c):
                    if c:
                        act.wait_ge(*s["p_wout"].at(b, c))
                    for i in range(2):
                        act.wait_ge(*s["v_o"].at(b, 2 * c + i + 1))
                        for j in range(4):
                            h = 4 * i + j
                            fn(coreT[:, h, :], oo[:, h, :], ACT.Square, accum_out=so8[:, h:h + 1]
                               ).then_inc(*s["a_so"].up)

                def sn2(c):
                    act.wait_ge(*s["a_so"].at(b, 8 * c + 8))
                    for i in range(2):
                        act.wait_ge(*s["p_ct"].at(b, 2 * c + i + 1))
                        fn(coreT[:, 4 * i:4 * i + 4, :].rearrange("p a b -> p (a b)"), bank[(4, 5)[i]][:, :], ACT.Copy
                           ).then_inc(*s["a_ct"].up)

                def ffn(f):
                    act.wait_ge(*s["p_fh"].at(b, f + 1))
                    if f >= 2:
                        act.wait_ge(*s["p_fo"].at(b, f - 1))
                    fn(GH[:, f % 2, :], bank[7][:, :], ACT.Gelu_apprx_tanh, bias=W["b1"][:, f:f + 1]
                       ).then_inc(*s["a_gh"].up)

                def hidden():
                    act.wait_ge(*s["v_lm1"].at(b, 1))
                    fn(lf, lf, ACT.Exp).then_inc(*s["a_fe1"].up)

                def moe1(p):
                    act.wait_ge(*s["p_gate1"].at(b, p + 1))
                    if p >= 2:
                        act.wait_ge(*s["v_hid1"].at(b, 2 * (p - 2) + 1))
                    fn(SG1[:, p % 2, :], bank[1 + p % 2][:, :], ACT.Silu).then_inc(*s["a_sg1"].up)

                steps = {"qkv": qkv, "ck": ck, "cd": cd, "cz": cz, "cv": cv, "inv": inv, "so1": so1, "sdl": sdl, "so2": so2,
                         "sn2": sn2, "ffn": ffn, "hidden": hidden, "moe1": moe1}
                for step in L1:
                    steps.get(step[0], nothing)(*step[1:])
                act.wait_ge(*s["out_ready"].at(b, 1))
                act.dma_start(out_v[bass.ds(b, 1)].rearrange("a p t d -> p (a t) d"), facc).then_inc(*s["out_dma"].up16)
                act.wait_ge(*s["out_dma"].at(b, 16))

        @block.gpsimd
        def _(pool):
            tt = nc.gpsimd.tensor_tensor
            pool.wait_ge(s["setup_v"].sem, 2)

            def flat(a):
                return a
            with pool.Fori(0, LOOPS) as b:
                wait_alone(pool, *s["out_dma"].at(b, 0))
                nc.gpsimd.memset(V32, 0.0).then_inc(*s["g_init"].up)
                nc.gpsimd.memset(KS, 1.0).then_inc(*s["g_init"].up)
                wait_alone(pool, *s["g_init"].at(b, 1))
                nc.gpsimd.memset(V32[:, :, :, HD:HD + 1], 1.0).then_inc(*s["g_init"].up)
                pool.wait_ge(*s["v_var"].at(b, 1))
                tt(rstd[:, :], var4[:, :], nhalf[:, 0:NT], ALU.pow).then_inc(*s["g_rstd"].up)
                pool.wait_ge(*s["v_lvar"].at(b, 1))
                tt(rstd2, var42, nhalf[:, 0:NT], ALU.pow).then_inc(*s["g_lrstd"].up)
                pool.wait_ge(s["weights_b"].sem, 16 * len(LATE))
                pool.wait_ge(*s["v_var1"].at(b, 1))
                tt(rstd[:, :], var4[:, :], nhalf[:, 0:NT], ALU.pow).then_inc(*s["g_rstd1"].up)
                pool.wait_ge(*s["v_ms1"].at(b, 1))
                tt(rz, ssq, nhalf[:, 0:NT], ALU.pow).then_inc(*s["g_rz"].up)

                def ck(c):
                    if c == 0:
                        pool.wait_ge(*s["v_g"].at(b, 1))
                        pool.wait_ge(*s["a_qkv"].at(b, NQKV))
                    gather(c, 0)
                    pool.wait_ge(*s["v_sse"].at(b, c + 1))
                    tt(rr8, ss8, nhalf[:, 0:8], ALU.pow).then_inc(*s["g_rr"].up)

                def gather(c, half):
                    gb = gg[:, c, 4 * half:4 * half + 4].unsqueeze(2).broadcast_to((P, 4, P))
                    for i, tri in enumerate(("after", "upto")):
                        m = W[tri][:].unsqueeze(1).broadcast_to((P, 4, P))
                        if c or half:
                            pool.wait_ge(*s["p_d"].at(b, 4 * c + 2 * half - 1 + i))
                        tt(GM[:, i, :].rearrange("p (a b) -> p a b", a=4), gb, m, ALU.mult).then_inc(*s["g_gm"].up)

                def cd(c, half):
                    if half == 0:
                        gather(c, 1)

                def inv(c, half, st):
                    t = {k: v[half] for k, v in T.items()}
                    four = lambda a: a.rearrange("p (a b) -> p a b", a=4)
                    mask = lambda i: W["blk"][:, i, :].unsqueeze(1).broadcast_to((P, 4, P))
                    if st == 0:
                        pool.wait_ge(*s["v_N"].at(b, 8 * c + 4 * half + 4))
                        if c:
                            pool.wait_ge(*s[f"p_inv{half}"].at(b, INV_P * c))
                        tt(four(t["M"]), four(N_[half]), mask(0), ALU.mult).then_inc(*s[f"g_inv{half}"].up)
                    if st == 1:
                        pool.wait_ge(*s[f"a_inv{half}"].at(b, INV_A * c + 1))
                        for i, n in enumerate(("L32", "L64", "L128")):
                            tt(four(t[n]), four(t["NT"]), mask(1 + i), ALU.mult).then_inc(*s[f"g_inv{half}"].up)

                def sn1(c):
                    pool.wait_ge(*s["v_sr"].at(b, c + 1))
                    tt(rc8, so8, nhalf[:, 0:8], ALU.pow).then_inc(*s["g_rc"].up)

                def hidden():
                    pool.wait_ge(*s["v_ms2"].at(b, 1))
                    tt(rz, ssq, nhalf[:, 0:NT], ALU.pow).then_inc(*s["g_rz2"].up)

                steps = {"ck": ck, "cd": cd, "inv": inv, "sn1": sn1, "hidden": hidden}
                for step in L1:
                    steps.get(step[0], nothing)(*step[1:])

        @block.vector
        def _(dve):
            v = nc.vector
            for buf, value in ((W96, 0.0), (W96b, 0.0), (nhalf, -0.5), (top4, PAD), (top2, PAD),
                               (tmp36, PAD), (pad8, PAD)):
                v.memset(buf[:], value)
            v.memset(junk[:], 0.0).then_inc(s["setup_v"].sem, 1)
            dve.wait_ge(s["setup_v"].sem, 1)
            dve.wait_ge(s["weights_a"].sem, 16 * len(EARLY))
            dve.wait_ge(s["setup_a"].sem, 1)
            v.tensor_scalar(neg_a[:, :], neg_a[:, :], -1.0, None, ALU.mult)
            v.tensor_scalar(W["ln1"][:], W["ln1"][:], 1.0, None, ALU.add)
            v.tensor_scalar(W["ln2"][:], W["ln2"][:], 1.0, None, ALU.add)
            v.tensor_scalar(W["Wout"][:], W["Wout"][:], W["gnw"][:, 0:1], None, ALU.mult).then_inc(s["setup_v"].sem, 1)
            dve.wait_ge(s["setup_v"].sem, 2)
            with dve.Fori(0, LOOPS) as b:
                def link(ins, alone=False):
                    ins.then_inc(*s["v_link"].up)
                    if alone:
                        wait_alone(dve, *s["v_link"].at(b, s["v_link"].n))
                    else:
                        dve.wait_ge(*s["v_link"].at(b, s["v_link"].n))

                def norm_stats(src, st, m, out4, eps):
                    for t in range(NT):
                        last = v.bn_stats(st[:, t, :], src[:, t, :])
                    link(last, alone=True)
                    for t in range(NT):
                        last = v.bn_aggr(m[:, t, :], st[:, t, :])
                    link(last)
                    return v.tensor_scalar(out4, m[:, :, 1], eps, None, ALU.add)

                def split3(src, rest, dst):
                    link(v.tensor_copy(dst[:, 0, :], src))
                    link(v.tensor_tensor(rest, src, dst[:, 0, :], ALU.subtract))
                    link(v.tensor_copy(dst[:, 1, :], rest))
                    return v.tensor_tensor(dst[:, 2, :], rest, dst[:, 1, :], ALU.subtract)

                def split_rows(src, rest, mid, dst, k):
                    link(v.tensor_copy(dst[0:k, :], src))
                    link(v.tensor_tensor(rest, src, dst[0:k, :], ALU.subtract))
                    v.tensor_copy(dst[32:32 + k, :], rest)
                    link(v.tensor_copy(mid, rest))
                    return v.tensor_tensor(dst[64:64 + k, :], rest, mid, ALU.subtract)

                def pick(src, k, topk, padded, n, res):
                    for t in range(NT):
                        last = v.max(top[:, t, :], padded[:, t, 0:n])
                    link(last)
                    link(v.tensor_copy(topk[:, :, 0:k], top[:, :, 0:k]), alone=True)
                    for t in range(NT):
                        last = v.match_replace(res[:, t, :], topk[:, t, :], padded[:, t, :], 1.0e30)
                    link(last)
                    link(v.tensor_tensor(res[:, :, 0:n], res[:, :, 0:n], padded[:, :, 0:n], ALU.not_equal))

                def per_tile(a):
                    return a.unsqueeze(2)

                dve.wait_ge(*s["out_dma"].at(b, 0))
                dve.wait_ge(*s["x_in"].at(b, 16))
                norm_stats(x, stats, mv, var4[:, :], EPS0).then_inc(*s["v_var"].up)
                dve.wait_ge(*s["g_rstd"].at(b, 1))
                for t in range(NT):
                    v.tensor_scalar(xn[:, t, :], x[:, t, :], mv[:, t, 0:1], rstd[:, t:t + 1], ALU.subtract, ALU.mult
                                    ).then_inc(*s["v_xn"].up)
                dve.wait_ge(*s["p_q"].at(b, 1))
                v.tensor_tensor(qf, bank[1][:, :], W["cos"][:], ALU.mult)
                link(v.tensor_tensor(qf2, bank[2][:, :], W["sin"][:], ALU.mult))
                v.tensor_tensor(qf, qf, qf2, ALU.add).then_inc(*s["v_q"].up)
                dve.wait_ge(*s["p_lat"].at(b, 1))
                norm_stats(bank[3][:, 0:128].rearrange("p (t n) -> p t n", t=NT), stats2, mv2, var42, EPS0
                           ).then_inc(*s["v_lvar"].up)
                dve.wait_ge(*s["g_lrstd"].at(b, 1))
                for t in range(NT):
                    last = v.tensor_scalar(latn[:, t, :], bank[3][:, t * LAT:(t + 1) * LAT], mv2[:, t, 0:1],
                                           rstd2[:, t:t + 1], ALU.subtract, ALU.mult)
                last.then_inc(*s["v_lat"].up)
                dve.wait_ge(*s["a_lexp"].at(b, 1))
                link(v.tensor_scalar(sc0, sc0, 1.0, None, ALU.add))
                link(v.reciprocal(sc0, sc0))
                v.tensor_tensor(sfc, sc0, W["rb0"][:].unsqueeze(1).broadcast_to((P, NT, E0)), ALU.add
                                ).then_inc(*s["v_lsfc"].up)
                dve.wait_ge(*s["p_latT"].at(b, 1))
                v.tensor_scalar(latT, bank[4][0:LAT, :], W["gam"][:, 0:1], W["bet"][:, 0:1], ALU.mult, ALU.add
                                ).then_inc(*s["v_latT"].up)
                dve.wait_ge(*s["v_q"].at(b, 1))
                split3(qf, qf2, qs3).then_inc(*s["v_qs3"].up)
                dve.wait_ge(*s["p_k"].at(b, 1))
                v.tensor_tensor(kf, bank[1][:, :], W["cos"][:], ALU.mult)
                link(v.tensor_tensor(kf2, bank[2][:, :], W["sin"][:], ALU.mult))
                v.tensor_tensor(kf, kf, kf2, ALU.add).then_inc(*s["v_k"].up)
                dve.wait_ge(*s["v_k"].at(b, 1))
                split3(kf, kf2, ks3).then_inc(*s["v_ks3"].up)

                def route():
                    wait_alone(dve, *s["v_lsfc"].at(b, 1))
                    for t in range(NT):
                        for g in range(G0):
                            last = v.max(gtop[:, t * G0 + g, :], sfc[:, t, g * 8:(g + 1) * 8])
                    link(last)
                    link(v.tensor_tensor(gs, gtop[:, :, 0], gtop[:, :, 1], ALU.add))
                    g3 = gs.rearrange("p (t g) -> p t g", t=NT)
                    other = g3.unsqueeze(2).broadcast_to((P, NT, G0, G0))
                    own = g3.unsqueeze(3).broadcast_to((P, NT, G0, G0))
                    c0 = cmp0.rearrange("p (t g o) -> p t g o", t=NT, g=G0)
                    c1 = cmp1.rearrange("p (t g o) -> p t g o", t=NT, g=G0)
                    v.tensor_tensor(c0, other, own, ALU.is_ge)
                    link(v.tensor_tensor(c1, other, own, ALU.is_gt))
                    v.tensor_tensor(c0, c0, W["grank"][:, 0], ALU.mult)
                    link(v.tensor_tensor(c1, c1, W["grank"][:, 1], ALU.mult))
                    link(v.tensor_tensor(c0, c0, c1, ALU.add))
                    link(v.tensor_reduce(rank, cmp0.rearrange("p (a o) -> p a o", o=G0), AX, ALU.add))
                    link(v.tensor_scalar(rank, rank, 2.0, None, ALU.is_lt))
                    keep = rank.rearrange("p (t g) -> p t g", t=NT).unsqueeze(3).broadcast_to((P, NT, G0, 8))
                    link(v.tensor_tensor(tmp36[:, :, 0:E0].rearrange("p t (g e) -> p t g e", g=G0),
                                         sfc.rearrange("p t (g e) -> p t g e", g=G0), keep, ALU.mult), alone=True)
                    pick(None, 4, top4, tmp36, E0, mr)
                    link(v.tensor_tensor(w0, sc0, mr[:, :, 0:E0], ALU.mult))
                    link(v.tensor_reduce(wsum, w0, AX, ALU.add))
                    link(v.tensor_scalar(wsum, wsum, 1e-20, None, ALU.add))
                    link(v.reciprocal(wrec, wsum))
                    link(v.tensor_scalar(wrec, wrec, SCALE0, None, ALU.mult))
                    v.tensor_tensor(w0, w0, wrec.unsqueeze(2).broadcast_to((P, NT, E0)), ALU.mult
                                    ).then_inc(*s["v_w0"].up)
                    dve.wait_ge(*s["p_w0T"].at(b, 1))
                    link(v.tensor_copy(wt, bank[4][0:E0, :]))
                    split_rows(wt, wtr, wtm, W96, E0).then_inc(*s["v_w96"].up)

                def hid(p):
                    dve.wait_ge(*s["a_sg"].at(b, p + 1))
                    dve.wait_ge(*s["p_up"].at(b, p + 1))
                    if p >= 2:
                        dve.wait_ge(*s["p_down"].at(b, p - 1))
                    up = bank[3 + 2 * (p % 2)][:, :]
                    if p == PR0:
                        v.tensor_tensor(HID[:, p % 2, :], SG[:, p % 2, :], up, ALU.mult).then_inc(*s["v_hid"].up)
                        return
                    if p >= 2:
                        dve.wait_ge(*s["v_hid"].at(b, p - 1))
                    v.tensor_tensor(HDT[:, p % 2, :], SG[:, p % 2, :], up, ALU.mult).then_inc(*s["v_t"].up)
                    dve.wait_ge(*s["v_t"].at(b, p + 1))
                    dve.wait_ge(*s["p_wb"].at(b, p + 1))
                    v.tensor_tensor(HID[:, p % 2, :], HDT[:, p % 2, :], bank[4 + 2 * (p % 2)][:, :], ALU.mult
                                    ).then_inc(*s["v_hid"].up)

                def smax(n):
                    w = P * (n % NT + 1)
                    wait_alone(dve, *s["p_max"].at(b, n + 1))
                    bk = bank[(0, 2)[n % 2]]
                    v.tensor_tensor_reduce(bk[:, 0:w], bk[:, 0:w], W["maskq"][:, S - w:S], 1.0, PAD,
                                           ALU.add, ALU.max, mx[:, n:n + 1]).then_inc(*s["v_max"].up)

                def maxrows():
                    dve.wait_ge(*s["v_max"].at(b, NH * NT))
                    v.tensor_scalar(nmx.rearrange("p (r n) -> p r n", r=2), mx.unsqueeze(1).broadcast_to((P, 2, NH * NT)),
                                    -1.0, None, ALU.mult).then_inc(*s["v_nm"].up)
                    dve.wait_ge(*s["p_mT"].at(b, 1))
                    link(v.tensor_copy(nmt, bank[0][0:64, 0:P]))
                    split3(nmt, nmr, nm3).then_inc(*s["v_nm3"].up)

                def pv(g):
                    dve.wait_ge(*s["p_o"].at(b, g + 1))
                    v.tensor_copy(OS[:, g, :], bank[0 if g % 2 else 6][:, :]).then_inc(*s["v_os"].up)

                def attn_out():
                    dve.wait_ge(*s["p_nd"].at(b, 1))
                    link(v.reciprocal(rden, bank[5][:, :]))
                    dve.wait_ge(*s["p_nd"].at(b, 2))
                    v.tensor_tensor(att, bank[4][:, :], rden, ALU.mult).then_inc(*s["v_att"].up)
                    dve.wait_ge(*s["p_acc"].at(b, 1))
                    v.tensor_tensor(x1[:, :, :], x[:, :, :], bank[7][:, :].rearrange("p (t d) -> p t d", t=NT), ALU.add
                                    ).then_inc(*s["v_x1"].up)

                steps = {"route": route, "hid": hid, "max": smax, "maxrows": maxrows, "pv": pv, "attn_out": attn_out}
                for step in L0:
                    steps.get(step[0], nothing)(*step[1:])

                def ms(src, ready):
                    for t in range(NT):
                        last = v.tensor_tensor_reduce(junk[:, t, :], src[:, t, :], src[:, t, :], 1.0, 0.0, ALU.mult, ALU.add,
                                                      ssq[:, t:t + 1])
                    link(last)
                    v.tensor_scalar(ssq, ssq, 1.0 / D, EPS1, ALU.mult, ALU.add).then_inc(*s[ready].up)

                dve.wait_ge(s["weights_b"].sem, 16 * len(LATE))
                dve.wait_ge(*s["v_x1"].at(b, 1))
                norm_stats(x1, stats, mv, var4[:, :], EPS0).then_inc(*s["v_var1"].up)
                dve.wait_ge(*s["g_rstd1"].at(b, 1))
                for t in range(NT):
                    v.tensor_scalar(xn1[:, t, :], x1[:, t, :], mv[:, t, 0:1], rstd[:, t:t + 1], ALU.subtract, ALU.mult
                                    ).then_inc(*s["v_xn1"].up)
                dve.wait_ge(*s["v_xn1"].at(b, NT))
                ms(xn1, "v_ms1")
                dve.wait_ge(*s["g_rz"].at(b, 1))
                for t in range(NT):
                    v.tensor_scalar(zz[:, t, :], xn1[:, t, :], rz[:, t:t + 1], None, ALU.mult).then_inc(*s["v_z"].up)
                dve.wait_ge(*s["p_zT"].at(b, 1))
                v.tensor_scalar(zT, bank[1][:, :], W["ln1"][:, 0:1], None, ALU.mult).then_inc(*s["v_zT"].up)
                dve.wait_ge(*s["a_eb"].at(b, 1))
                ps = bank[2][:, 0:64].rearrange("p (t n) -> p t n", t=NT)
                link(v.tensor_tensor(aab, ps[:, :, HV:2 * HV], W["dtb"][:].unsqueeze(1).broadcast_to((P, NT, HV)), ALU.add))
                link(v.tensor_scalar(sp, aab, -1.0, None, ALU.mult))
                v.tensor_tensor(sp, sp, aab, ALU.max).then_inc(*s["v_ab"].up)

                def softmax_shift(ps, src_ready, ready):
                    link(v.tensor_reduce(red4, ps, AX, ALU.max))
                    v.tensor_tensor(lf, ps, red4.unsqueeze(2).broadcast_to((P, NT, EF)), ALU.subtract
                                    ).then_inc(*s[ready].up)

                def softmax_end():
                    link(v.tensor_reduce(red4, lf, AX, ALU.add))
                    link(v.reciprocal(rec4, red4))
                    link(v.tensor_tensor(pad8[:, :, 0:EF], lf, rec4.unsqueeze(2).broadcast_to((P, NT, EF)), ALU.mult),
                         alone=True)
                    pick(None, 2, top2, pad8, EF, mrf)

                softmax_shift(bank[2][:, 64:96].rearrange("p (t n) -> p t n", t=NT), None, "v_lm")
                link(v.tensor_scalar(beta, ba[:, :, 0:HV], 1.0, None, ALU.add))
                v.reciprocal(beta, beta)
                link(v.tensor_scalar(aab, aab, 0.0, None, ALU.max))
                dve.wait_ge(*s["a_sp"].at(b, 1))
                link(v.tensor_tensor(aab, aab, sp, ALU.add))
                v.tensor_tensor(gg, aab, neg_a[:, :].unsqueeze(1).broadcast_to((P, NT, HV)), ALU.mult
                                ).then_inc(*s["v_g"].up)
                dve.wait_ge(*s["a_fe"].at(b, 1))
                softmax_end()
                v.tensor_tensor(wf, pad8[:, :, 0:EF], mrf[:, :, 0:EF], ALU.mult).then_inc(*s["v_wf"].up)

                def qkv(m0):
                    if m0 == NQKV:
                        return
                    for k in (1, 2, 3):
                        for m in (m0, m0 + 1):
                            if k == 1:
                                dve.wait_ge(*s["a_cv"].at(b, m + 1))
                            else:
                                dve.wait_ge(*s["v_tap"].at(b, 2 * m0 + 2 * (k - 2) + m - m0 + 1))
                            cv = CV[:, m % 4, :]
                            ins = v.scalar_tensor_tensor(out=cv[:, k:S], in0=bank[4 + m % 4][:, 0:S - k],
                                                         scalar=W["convw"][:, m, 3 - k:4 - k], in1=cv[:, k:S],
                                                         op0=ALU.mult, op1=ALU.add)
                            ins.then_inc(*(s["v_tap"] if k < 3 else s["v_cv"]).up)
                    if m0 == 6:
                        dve.wait_ge(*s["p_wfT"].at(b, 1))
                        v.tensor_copy(wfT, bank[0][0:EF, :]).then_inc(*s["v_wfT"].up)

                pairs = lambda a: a.unsqueeze(2).broadcast_to((P, HK, 2))
                v8 = lambda a: a.rearrange("p (k r) -> p k r", r=2)

                def ck(c):
                    dve.wait_ge(*s["a_ss"].at(b, 8 * c + 8))
                    if c:
                        dve.wait_ge(*s["v_core"].at(b, 8 * c))
                    v.tensor_scalar(ss8, ss8, EPS1, None, ALU.add).then_inc(*s["v_sse"].up)
                    dve.wait_ge(*s["v_sse"].at(b, c + 1))
                    v.reciprocal(rk2, ss8[:, 0:HK])
                    link(v.reciprocal(rq2, ss8[:, HK:8]))
                    link(v.scalar_tensor_tensor(out=v8(nlam), in0=pairs(rk2), scalar=-1.0, in1=v8(beta[:, c, :]),
                                                op0=ALU.mult, op1=ALU.mult))
                    dve.wait_ge(*s["a_eG"].at(b, 1))
                    v.tensor_tensor(s1, nlam, eG[:, 0, c * HV:(c + 1) * HV], ALU.mult)

                def cv(c):
                    dve.wait_ge(*s["g_rr"].at(b, c + 1))
                    v.tensor_scalar(rqs, rr8[:, HK:8], float(P) ** -0.5, None, ALU.mult)
                    v.tensor_tensor(v8(rkb), pairs(rr8[:, 0:HK]), v8(beta[:, c, :]), ALU.mult).then_inc(*s["v_sc"].up)
                    dve.wait_ge(*s["v_sc"].at(b, c + 1))

                def cd(c, half):
                    ps = bank[half][:, :].rearrange("p (k r n) -> p k r n", k=2, r=2)
                    dve.wait_ge(*s["p_kk"].at(b, 2 * c + half + 1))
                    dve.wait_ge(*s["a_d"].at(b, 4 * c + 2 * half + 1))
                    if c:
                        dve.wait_ge(*s[f"g_inv{half}"].at(b, 4 * c))
                    for j in range(4):
                        h = 4 * half + j
                        v.scalar_tensor_tensor(out=N_[half][:, j * P:(j + 1) * P], in0=ps[:, j // 2, 1, :],
                                               scalar=nlam[:, h:h + 1], in1=DL[half][:, j * P:(j + 1) * P],
                                               op0=ALU.mult, op1=ALU.mult).then_inc(*s["v_N"].up)
                    dve.wait_ge(*s["a_d"].at(b, 4 * c + 2 * half + 2))
                    if c:
                        dve.wait_ge(*s["p_o2"].at(b, 2 * c))
                    v.tensor_tensor(QKD[:, 4 * half:4 * half + 4, :].rearrange("p (k r) n -> p k r n", k=2),
                                    ps[:, :, 0, :].unsqueeze(2).broadcast_to((P, 2, 2, P)),
                                    DU.rearrange("p (k r n) -> p k r n", k=2, r=2), ALU.mult
                                    ).then_inc(*s["v_qkd"].up)

                def inv(c, half, st):
                    t = {k: u[half] for k, u in T.items()}
                    ba_, bb, bc = ((0, 1, 4), (2, 3, 5))[half]
                    p0, v0 = INV_P * c, INV_V * c
                    four = lambda a: a.rearrange("p (a b) -> p a b", a=4)
                    up = s[f"v_inv{half}"]
                    pw = lambda n: dve.wait_ge(*s[f"p_inv{half}"].at(b, p0 + n))
                    vw = lambda n: dve.wait_ge(*up.at(b, v0 + n))
                    if st == 1:
                        dve.wait_ge(*s[f"g_inv{half}"].at(b, 4 * c + 1))
                        v.tensor_tensor(four(t["X"]), four(t["M"]), W["ident"][:].unsqueeze(1).broadcast_to((P, 4, P)),
                                        ALU.add).then_inc(*up.up)
                        dve.wait_ge(*s[f"a_inv{half}"].at(b, INV_A * c + 1))
                        v.tensor_tensor(four(t["MT"]), four(t["NT"]), W["blk"][:, 0, :].unsqueeze(1).broadcast_to((P, 4, P)),
                                        ALU.mult).then_inc(*up.up)
                    elif st == 2:
                        pw(3)
                        v.tensor_copy(t["MT"], bank[bb][:, :]).then_inc(*up.up)
                    elif st == 3:
                        pw(4); vw(1)
                        v.tensor_tensor(t["X"], t["X"], bank[ba_][:, :], ALU.add).then_inc(*up.up)
                        pw(6)
                        v.tensor_copy(t["MT"], bank[bb][:, :]).then_inc(*up.up)
                    elif st == 4:
                        pw(7); vw(4)
                        v.tensor_tensor(t["X"], t["X"], bank[ba_][:, :], ALU.add).then_inc(*up.up)
                    elif st == 5:
                        pw(9); vw(6)
                        v.tensor_tensor(t["X"], t["X"], bank[ba_][:, :], ALU.add).then_inc(*up.up)
                    elif st in (8, 11):
                        pw(12 if st == 8 else 15); vw(7 if st == 8 else 8)
                        v.tensor_tensor(t["X"], t["X"], bank[bc][:, :], ALU.add).then_inc(*up.up)
                    elif st == 14:
                        pw(18)
                        dve.wait_ge(*s[f"a_inv{half}"].at(b, INV_A * c + 9))
                        v.tensor_tensor(t["TT"], t["TT"], bank[bc][:, :], ALU.add).then_inc(*up.up)

                def sw(c):
                    if c:
                        for i in range(2):
                            dve.wait_ge(*s["p_w"].at(b, 2 * (c - 1) + i + 1))
                            if i == 0:
                                dve.wait_ge(*s["a_vb"].at(b, 8 * c + 8))
                                dve.wait_ge(*s["a_so"].at(b, 8 * c))
                            for j in range(4):
                                h = 4 * i + j
                                v.scalar_tensor_tensor(out=R[:, h, :], in0=bank[(0, 1)[i]][:, j * P:(j + 1) * P],
                                                       scalar=s1[:, h:h + 1], in1=vb[:, h, :], op0=ALU.mult, op1=ALU.add
                                                       ).then_inc(*s["v_R"].up)

                def sdl(c):
                    if c < NT - 1:
                        for i in range(2):
                            dve.wait_ge(*s["a_dl"].at(b, 2 * c + i + 1))
                            if c:
                                dve.wait_ge(*s["p_s"].at(b, 2 * c))
                            for j in range(4):
                                h = 4 * i + j
                                v.tensor_scalar(DLS[:, h, :], dl[:, h, :], eG[:, 1, c * HV + h:c * HV + h + 1], None,
                                                ALU.mult).then_inc(*s["v_dls"].up)

                def so2(c):
                    for i in range(2):
                        dve.wait_ge(*s["p_o2"].at(b, 2 * c + i + 1))
                        dve.wait_ge(*s["p_dl"].at(b, 2 * c + 2))
                        dst = oo[:, 4 * i:4 * i + 4, :].rearrange("p a b -> p (a b)")
                        if c:
                            dve.wait_ge(*s["a_o1"].at(b, 8 * (c - 1) + 4 * i + 4))
                            v.tensor_tensor(dst, o1s[:, 4 * i:4 * i + 4, :].rearrange("p a b -> p (a b)"),
                                            bank[(0, 1)[i]][:, :], ALU.add).then_inc(*s["v_o"].up)
                        else:
                            v.tensor_copy(dst, bank[(0, 1)[i]][:, :]).then_inc(*s["v_o"].up)

                def ss(c):
                    if c < NT - 1:
                        for i in range(2):
                            dve.wait_ge(*s["p_s"].at(b, 2 * c + i + 1))
                            for j in range(4):
                                h = 4 * i + j
                                ps = bank[(2, 3)[i]][:, j * P:(j + 1) * P]
                                if c:
                                    v.scalar_tensor_tensor(out=State[:, h, :], in0=State[:, h, :],
                                                           scalar=eG[:, 2, c * HV + h:c * HV + h + 1], in1=ps,
                                                           op0=ALU.mult, op1=ALU.add).then_inc(*s["v_S"].up)
                                else:
                                    v.tensor_copy(State[:, h, :], ps).then_inc(*s["v_S"].up)

                def sn1(c):
                    dve.wait_ge(*s["a_so"].at(b, 8 * c + 8))
                    link(v.tensor_tensor(v8(so8), v8(so8), pairs(rq2), ALU.mult))
                    v.tensor_scalar(so8, so8, 1.0 / (P * P), EPS1, ALU.mult, ALU.add).then_inc(*s["v_sr"].up)

                def sn2(c):
                    dve.wait_ge(*s["g_rc"].at(b, c + 1))
                    link(v.tensor_tensor(v8(rc8), v8(rc8), pairs(rqs), ALU.mult))
                    dve.wait_ge(*s["a_sz"].at(b, 2 * c + 2))
                    for h in range(HV):
                        v.scalar_tensor_tensor(out=core[:, h, :], in0=oo[:, h, :], scalar=rc8[:, h:h + 1], in1=sz[:, h, :],
                                               op0=ALU.mult, op1=ALU.mult).then_inc(*s["v_core"].up)

                def swo(c):
                    dve.wait_ge(*s["p_wout"].at(b, c + 1))
                    v.tensor_tensor(zz[:, c, :], xn1[:, c, :], bank[7][:, 0:P], ALU.add).then_inc(*s["v_h"].up)

                def ffn(f):
                    e = f // FC - 1
                    if f % FC or f == 0:
                        return
                    dve.wait_ge(*s["p_fo"].at(b, f))
                    for t in range(NT):
                        ps = bank[6][:, t * P:(t + 1) * P]
                        if e == 0:
                            v.tensor_scalar(facc[:, t, :], ps, wf[:, t, 0:1], None, ALU.mult).then_inc(*s["v_fo"].up)
                        else:
                            if t == 0:
                                dve.wait_ge(*s["v_fo"].at(b, 4 * e))
                            v.scalar_tensor_tensor(out=facc[:, t, :], in0=ps, scalar=wf[:, t, e:e + 1],
                                                   in1=facc[:, t, :], op0=ALU.mult, op1=ALU.add).then_inc(*s["v_fo"].up)

                def hidden():
                    dve.wait_ge(*s["v_h"].at(b, NT))
                    dve.wait_ge(*s["v_fo"].at(b, 4 * EF))
                    link(v.tensor_tensor(x1[:, :, :], x1[:, :, :], zz, ALU.add))
                    link(v.tensor_tensor(facc, facc, x1[:, :, :], ALU.add))
                    dve.wait_ge(*s["p_ct"].at(b, 2 * NT))
                    ms(zz, "v_ms2")
                    dve.wait_ge(*s["g_rz2"].at(b, 1))
                    for t in range(NT):
                        v.tensor_scalar(hbuf[:, t, :], zz[:, t, :], rz[:, t:t + 1], None, ALU.mult).then_inc(*s["v_h2"].up)
                    dve.wait_ge(*s["p_hT"].at(b, 1))
                    v.tensor_scalar(hT, bank[0][:, :], W["ln2"][:, 0:1], None, ALU.mult).then_inc(*s["v_hT"].up)
                    dve.wait_ge(*s["p_r1"].at(b, 1))
                    softmax_shift(bank[1][:, 0:NT * E1].rearrange("p (t n) -> p t n", t=NT), None, "v_lm1")
                    dve.wait_ge(*s["a_fe1"].at(b, 1))
                    softmax_end()
                    link(v.tensor_tensor(lf, pad8[:, :, 0:EF], mrf[:, :, 0:EF], ALU.mult))
                    link(v.tensor_reduce(red4, lf, AX, ALU.add))
                    link(v.reciprocal(rec4, red4))
                    v.tensor_tensor(lf, lf, rec4.unsqueeze(2).broadcast_to((P, NT, E1)), ALU.mult
                                    ).then_inc(*s["v_w1r"].up)
                    dve.wait_ge(*s["p_w1T"].at(b, 1))
                    rest, mid = CV[0:E1, 2, :], CV[0:E1, 1, 0:S // 2].bitcast(BF16)
                    link(v.tensor_copy(wt1, bank[0][0:E1, :]))
                    split_rows(wt1, rest, mid, W96b, E1).then_inc(*s["v_w96b"].up)

                def moe1(p):
                    dve.wait_ge(*s["a_sg1"].at(b, p + 1))
                    dve.wait_ge(*s["p_up1"].at(b, p + 1))
                    if p >= 2:
                        dve.wait_ge(*s["p_down1"].at(b, p - 1))
                    if p >= 2:
                        dve.wait_ge(*s["v_hid1"].at(b, 2 * (p - 1)))
                    v.tensor_tensor(HDT1[:, p % 2, :], SG1[:, p % 2, :], bank[3 + 2 * (p % 2)][:, :], ALU.mult
                                    ).then_inc(*s["v_hid1"].up)
                    dve.wait_ge(*s["v_hid1"].at(b, 2 * p + 1))
                    dve.wait_ge(*s["p_wb1"].at(b, p + 1))
                    v.tensor_tensor(HID1[:, p % 2, :], HDT1[:, p % 2, :], bank[4 + 2 * (p % 2)][:, :], ALU.mult
                                    ).then_inc(*s["v_hid1"].up)

                def moe1_last():
                    dve.wait_ge(*s["p_down1"].at(b, PR1))
                    v.tensor_tensor(facc, facc, bank[7][:, :].rearrange("p (t d) -> p t d", t=NT), ALU.add
                                    ).then_inc(*s["out_ready"].up)

                steps = {"qkv": qkv, "ck": ck, "cd": cd, "cv": cv, "inv": inv, "sw": sw, "sdl": sdl, "so2": so2, "ss": ss,
                         "sn1": sn1, "sn2": sn2, "swo": swo, "ffn": ffn, "ffn_last": lambda: ffn(EF * FC),
                         "hidden": hidden, "moe1": moe1,
                         "moe1_last": moe1_last}
                for step in L1:
                    steps.get(step[0], nothing)(*step[1:])

        for name, g in signals.items():
            sizes[name] = g.n


INV_P, INV_V, INV_A = 18, 10, 10


def constants():
    c = {}
    d = np.arange(P) % HD
    half = HD // 2
    inv = (1.0 / 10000.0 ** (np.arange(half, dtype=np.float32) / half)).astype(np.float32)
    ang = np.arange(S, dtype=np.float32)[None, :] * inv[d % half][:, None]
    sign = np.where(d < half, -1.0, 1.0).astype(np.float32)[:, None]
    cos, sin = np.cos(ang).astype(np.float32), (np.sin(ang) * sign).astype(np.float32)
    c["cos"], c["sin"] = cos, sin
    i, j = np.arange(P)[:, None], np.arange(P)[None, :]
    c["ident"] = np.eye(P)
    c["identb"] = np.eye(P)
    mq = np.zeros((P, S))
    mq[:, S - P:] = np.where(j > i, NEG, 0.0)
    c["maskq"] = mq
    c["maskt"] = np.where(i > j, NEG, 0.0)
    g, o = np.arange(G0)[:, None], np.arange(G0)[None, :]
    rank = np.stack([(o < g), (o > g)]).astype(np.float32)
    c["grank"] = np.broadcast_to(rank[None, :, None], (P, 2, NT, G0, G0))

    def sel(experts, pairs):
        a = np.zeros((96, pairs, P))
        for e in range(experts):
            for part in range(3):
                a[32 * part + e, e // 2, (e % 2) * 64:(e % 2) * 64 + 64] = 1.0
        return a
    c["sel0"], c["sel1"] = sel(E0, PR0), sel(E1, PR1)
    c["upto"], c["after"], c["ones"] = (i <= j), (i > j), np.ones((P, P))
    c["below"] = np.where(j < i, 0.0, NEG)
    c["notabove"] = np.where(i <= j, 0.0, NEG)
    blk = [(i // 16 == j // 16)]
    for n in (16, 32, 64):
        blk.append((i // (2 * n) == j // (2 * n)) & (i // n != j // n))
    c["blk"] = np.stack(blk, 1)
    k, m = np.arange(P)[:, None], np.arange(32)[None, :]
    c["pick"] = np.stack([k == 32 * (m // HD) + m % HD, k == 32 * (m // HD) + HD], 1)
    return c


def lay_out(a):
    perm = np.arange(D).reshape(NH, 2, HD // 2)[:, ::-1].reshape(D)
    rows = lambda v, n=P: np.broadcast_to(v[None, :], (n, v.shape[0]))
    t = {}
    t["Wq"], t["Wqr"] = a["L0_attn_W_q"], a["L0_attn_W_q"][:, perm]
    t["Wdkv"], t["Wuk"], t["Wukr"] = a["L0_attn_W_dkv"], a["L0_attn_W_uk"], a["L0_attn_W_uk"][:, perm]
    t["Wuv"], t["Wo"] = a["L0_attn_W_uv"], a["L0_attn_W_o"]
    t["gam"], t["bet"] = a["L0_attn_ln_gamma"][:, None], a["L0_attn_ln_beta"][:, None]
    t["rw0"], t["rb0"] = a["L0_ffn_router_weight"].T, rows(a["L0_ffn_router_bias"])
    t["gate0"] = a["L0_ffn_gate_w"].reshape(PR0, P, D).transpose(2, 0, 1)
    t["up0"] = a["L0_ffn_up_w"].reshape(PR0, P, D).transpose(2, 0, 1)
    t["down0"] = a["L0_ffn_down_w"].transpose(0, 2, 1).reshape(PR0, P, D).transpose(1, 0, 2)
    t["sg"], t["su"], t["sd"] = a["L0_ffn_shared_gate_w"].T, a["L0_ffn_shared_up_w"].T, a["L0_ffn_shared_down_w"].T
    t["ln1"], t["ln2"] = a["L1_attn_w_ln1"][:, None], a["L1_attn_w_ln2"][:, None]
    t["Wqkvz"], t["Wba"] = a["L1_attn_W_qkvz"], a["L1_attn_W_ba"]
    t["convw"] = a["L1_attn_conv_w"].reshape(NQKV, P, 4).transpose(1, 0, 2)
    t["dtb"], t["alog"], t["gnw"] = rows(a["L1_attn_dt_bias"]), rows(a["L1_attn_A_log"]), a["L1_attn_gate_norm_w"][:, None]
    t["Wout"] = a["L1_attn_W_out"].reshape(HV, P, D).transpose(1, 0, 2)
    t["r1"] = a["L1_attn_W_router"]
    t["ge1"] = a["L1_attn_W_gate_e"].transpose(1, 0, 2).reshape(D, PR1, P)
    t["ue1"] = a["L1_attn_W_up_e"].transpose(1, 0, 2).reshape(D, PR1, P)
    t["de1"] = a["L1_attn_W_down_e"].reshape(PR1, P, D).transpose(1, 0, 2)
    t["rf"] = a["L1_ffn_w_router"]
    t["b1"] = a["L1_ffn_b1"].reshape(EF * FC, P).T
    t["b2"] = a["L1_ffn_b2"]
    return t


def program(nc):
    x = nc.dram_tensor("in_x", (B, S, D), F32, kind="ExternalInput").ap()
    w = {n: nc.dram_tensor("in_" + n, tuple(shape), dt, kind="ExternalInput").ap() for n, (shape, dt) in WEIGHTS.items()}
    out = nc.dram_tensor("out", (B, S, D), F32, kind="ExternalOutput").ap()
    scratch = (nc.dram_tensor("scrq", (3, P, S), BF16, kind="Internal").ap(),
               nc.dram_tensor("scrk", (3, P, S), BF16, kind="Internal").ap(),
               nc.dram_tensor("scrm", (3, NH * NT, P), BF16, kind="Internal").ap())
    w_last = nc.dram_tensor("in_w_last", (EF, P, FC * P + FC * D), F32, kind="ExternalInput").ap()
    return x, w_last, out, w, scratch


def kernel(**inputs):
    import concourse.bacc as bacc
    from concourse.bass_utils import run_bass_kernel_spmd

    per, sizes = {}, {}
    nc = bacc.Bacc("TRN2", target_bir_lowering=False, num_devices=1)
    build(nc, *program(nc), {}, per)
    nc = bacc.Bacc("TRN2", target_bir_lowering=False, num_devices=1)
    build(nc, *program(nc), per, sizes)
    assert per == sizes

    a = {n: np.asarray(v) for n, v in inputs.items()}
    arrays = {"in_x": np.ascontiguousarray(a["L0_attn_x"])}
    w1 = a["L1_ffn_w1"]
    w2 = a["L1_ffn_w2"].reshape(EF, FC, P, D).transpose(0, 2, 1, 3).reshape(EF, P, FC * D)
    arrays["in_w_last"] = np.ascontiguousarray(np.concatenate([w1, w2], axis=2))
    laid = lay_out(a)
    for n, (shape, dt) in WEIGHTS.items():
        if n in laid:
            arrays["in_" + n] = np.ascontiguousarray(laid[n]).reshape(shape)
    for n, v in constants().items():
        arrays["in_" + n] = np.ascontiguousarray(v, dtype=mybir.dt.np(WEIGHTS[n][1]))
    r = run_bass_kernel_spmd(nc, [arrays], core_ids=[0])
    return r.results[0]["out"]
```
